# Optimizing a Trainium2 kernel written in Bass

```python
import numpy as np
import jax
import jax.numpy as jnp

def _softmax(x, axis=-1):
    return jax.nn.softmax(x, axis=axis)

def _gelu(x):
    return jax.nn.gelu(x, approximate=True)

def _silu(x):
    return jax.nn.silu(x)

def _sigmoid(x):
    return jax.nn.sigmoid(x)

def _layernorm(x, axis=-1, eps=1e-05):
    m = jnp.mean(x, axis=axis, keepdims=True)
    v = jnp.var(x, axis=axis, keepdims=True)
    return (x - m) / jnp.sqrt(v + eps)

def _scatter_add(tgt, idx, src, axis=0):
    return tgt.at[idx].add(src)

def _segment_sum(src, seg, n):
    return jax.ops.segment_sum(src, seg, n)
kernel_name = 'mk_adaln_d1_jaxref_r4_593f93'

def setup_inputs(seed: int=0):
    np.random.seed(seed)
    _w = jnp.asarray

    def _L0_attn_setup():
        import jax, jax.numpy as jnp
        import numpy as np
        HID = 512
        HEADS = 16
        HD = HID // HEADS
        EPS = 1e-06

        def _heads(x, b, s):
            return x.reshape(b, s, HEADS, HD).transpose(0, 2, 1, 3)
        key = jax.random.key(seed)
        ks = jax.random.split(key, 9)
        s = 1.0 / np.sqrt(HID)
        return {'hidden_states': jax.random.normal(ks[0], (4, 1024, HID), jnp.float32), 'q_w': jax.random.normal(ks[1], (HID, HID), jnp.float32) * s, 'q_b': jnp.zeros((HID,), jnp.float32), 'k_w': jax.random.normal(ks[2], (HID, HID), jnp.float32) * s, 'k_b': jnp.zeros((HID,), jnp.float32), 'v_w': jax.random.normal(ks[3], (HID, HID), jnp.float32) * s, 'v_b': jnp.zeros((HID,), jnp.float32), 'o_w': jax.random.normal(ks[4], (HID, HID), jnp.float32) * s, 'o_b': jnp.zeros((HID,), jnp.float32)}
    _L0_attn_in = _L0_attn_setup()

    def _L0_ffn_setup():
        import jax, jax.numpy as jnp
        import numpy as np
        B, S, D, H = (4, 512, 512, 2048)

        def fwht(x):
            orig_shape = x.shape
            n = orig_shape[-1]
            x = x.reshape(-1, n)
            h = 1
            while h < n:
                xb = x.reshape(-1, n // (2 * h), 2, h)
                a = xb[:, :, 0, :]
                b = xb[:, :, 1, :]
                x = jnp.stack([a + b, a - b], axis=2).reshape(-1, n)
                h *= 2
            scale = jnp.asarray(1.0 / np.sqrt(n), dtype=x.dtype)
            return (x * scale).reshape(orig_shape)
        key = jax.random.key(seed)
        kx, k1, k2, k3 = jax.random.split(key, 4)
        x = jax.random.normal(kx, (B, S, D), dtype=jnp.float32)
        W1 = jax.random.normal(k1, (H, D), dtype=jnp.float32) * (1.0 / np.sqrt(D))
        W2 = jax.random.normal(k2, (D, H), dtype=jnp.float32) * (1.0 / np.sqrt(H))
        W3 = jax.random.normal(k3, (H, D), dtype=jnp.float32) * (1.0 / np.sqrt(D))
        return {'x': x, 'W1': W1, 'W2': W2, 'W3': W3}
    _L0_ffn_in = _L0_ffn_setup()
    _L0_c = _w((lambda *s: np.random.randn(*s).astype(np.float32) * 0.05)(4, 512))
    _L0_wmod = _w((lambda *s: np.random.randn(*s).astype(np.float32) * 0.05)(512, 6 * 512) * 512 ** (-0.5))
    _d = {'L0_attn_hidden_states': _L0_attn_in['hidden_states'], 'L0_attn_q_w': _L0_attn_in['q_w'], 'L0_attn_q_b': _L0_attn_in['q_b'], 'L0_attn_k_w': _L0_attn_in['k_w'], 'L0_attn_k_b': _L0_attn_in['k_b'], 'L0_attn_v_w': _L0_attn_in['v_w'], 'L0_attn_v_b': _L0_attn_in['v_b'], 'L0_attn_o_w': _L0_attn_in['o_w'], 'L0_attn_o_b': _L0_attn_in['o_b'], 'L0_ffn_W1': _L0_ffn_in['W1'], 'L0_ffn_W2': _L0_ffn_in['W2'], 'L0_ffn_W3': _L0_ffn_in['W3'], 'L0_c': _L0_c, 'L0_wmod': _L0_wmod}
    _x0 = _d['L0_attn_hidden_states']
    _d['L0_attn_hidden_states'] = jax.random.normal(jax.random.fold_in(jax.random.key(seed), 1), (4, 512, 512), dtype=_x0.dtype)
    del _x0
    return _d

def reference(L0_attn_hidden_states, L0_attn_q_w, L0_attn_q_b, L0_attn_k_w, L0_attn_k_b, L0_attn_v_w, L0_attn_v_b, L0_attn_o_w, L0_attn_o_b, L0_ffn_W1, L0_ffn_W2, L0_ffn_W3, L0_c, L0_wmod):

    def _L0_attn_ref(hidden_states, q_w, q_b, k_w, k_b, v_w, v_b, o_w, o_b):
        import jax, jax.numpy as jnp
        import numpy as np
        HID = 512
        HEADS = 16
        HD = HID // HEADS
        EPS = 1e-06

        def _heads(x, b, s):
            return x.reshape(b, s, HEADS, HD).transpose(0, 2, 1, 3)
        b, s, _ = hidden_states.shape
        q = _heads(hidden_states @ q_w.T + q_b, b, s)
        k = _heads(hidden_states @ k_w.T + k_b, b, s)
        v = _heads(hidden_states @ v_w.T + v_b, b, s)
        qp = jax.nn.elu(q) + 1.0
        kp = jax.nn.elu(k) + 1.0
        kv = jnp.einsum('bhsd,bhse->bhde', kp, v)
        z = jnp.einsum('bhsd,bhd->bhs', qp, kp.sum(axis=2))[..., None]
        attn = jnp.einsum('bhsd,bhde->bhse', qp, kv) / (z + EPS)
        out = attn.transpose(0, 2, 1, 3).reshape(b, s, HID)
        return out @ o_w.T + o_b

    def _L0_ffn_ref(x, W1, W2, W3):
        import jax, jax.numpy as jnp
        import numpy as np
        B, S, D, H = (4, 512, 512, 2048)

        def fwht(x):
            orig_shape = x.shape
            n = orig_shape[-1]
            x = x.reshape(-1, n)
            h = 1
            while h < n:
                xb = x.reshape(-1, n // (2 * h), 2, h)
                a = xb[:, :, 0, :]
                b = xb[:, :, 1, :]
                x = jnp.stack([a + b, a - b], axis=2).reshape(-1, n)
                h *= 2
            scale = jnp.asarray(1.0 / np.sqrt(n), dtype=x.dtype)
            return (x * scale).reshape(orig_shape)
        up_gate = jnp.einsum('bsd,hd->bsh', x, W1)
        up_lin = jnp.einsum('bsd,hd->bsh', x, W3)
        hidden = jax.nn.silu(up_gate) * up_lin
        hidden = fwht(hidden)
        out = jnp.einsum('bsh,dh->bsd', hidden, W2)
        return out
    x = L0_attn_hidden_states
    mod = (_silu(L0_c) @ L0_wmod).reshape(L0_c.shape[0], 6, 1, -1)
    sa, ca, ga, sb, cb, gb = (mod[:, 0], mod[:, 1], mod[:, 2], mod[:, 3], mod[:, 4], mod[:, 5])
    ga = (2 * (ga >= 0) - 1) * jnp.maximum(jnp.abs(ga), 0.25)
    gb = (2 * (gb >= 0) - 1) * jnp.maximum(jnp.abs(gb), 0.25)
    h = _layernorm(x, axis=-1) * (1 + ca) + sa
    x = x + ga * _L0_attn_ref(h, L0_attn_q_w, L0_attn_q_b, L0_attn_k_w, L0_attn_k_b, L0_attn_v_w, L0_attn_v_b, L0_attn_o_w, L0_attn_o_b)
    h = _layernorm(x, axis=-1) * (1 + cb) + sb
    x = x + gb * _L0_ffn_ref(h, L0_ffn_W1, L0_ffn_W2, L0_ffn_W3)
    return x

_drawn_inputs = setup_inputs


def setup_inputs(seed=0):
    import zlib

    import numpy as np

    out = dict(_drawn_inputs(seed))
    spreads = {'L0_attn_q_b': (0.0, 0.8),
     'L0_attn_k_b': (0.0, 0.8),
     'L0_attn_v_b': (0.0, 0.326),
     'L0_attn_o_b': (0.0, 0.308)}
    factors = {'L0_attn_q_w': 8.0, 'L0_attn_k_w': 8.0, 'L0_attn_v_w': 5.037}
    for name, (base, spread) in spreads.items():
        noise = np.random.default_rng([zlib.crc32(name.encode()), seed]).standard_normal(out[name].shape)
        drawn = base * np.exp(spread * noise) if base else spread * noise
        out[name] = jnp.asarray(drawn.astype(out[name].dtype))
    for name, factor in factors.items():
        out[name] = (out[name] * factor).astype(out[name].dtype)
    return out
```

```python
from contextlib import ExitStack

import concourse.bass as bass
from concourse import mybir

F32 = mybir.dt.float32
F32R = mybir.dt.float32r
ACT = mybir.ActivationFunctionType
ALU = mybir.AluOpType

P = 128
Q32 = 32
NB, S, D, HID = 4, 512, 512, 2048
KT = D // P
TT = S // P
EPS_LN = 1e-5
EPS_Z = 1e-6
NQ = P // Q32
HW = P + 2
NBLK = HID // P
DC = 64
NCH = D // DC
GH = 256
NG = HID // GH
GB = GH // P
G_MIN = 0.25


def build(nc, x, q_w, q_b, k_w, k_b, v_w, v_b, o_w, o_b, W1, W2, W3, c, wmod, out):
    x1_dram = nc.dram_tensor("x1_scratch", [NB, S, D], F32, kind="Internal").ap()
    g_dram = nc.dram_tensor("g_scratch", [NB, 2, D], F32, kind="Internal").ap()
    w2t_dram = nc.dram_tensor("w2_hadamard_scratch", [NBLK, P, D], F32, kind="Internal").ap()

    ctx = ExitStack()
    with ctx:
        sem = lambda n: ctx.enter_context(nc.semaphore(n))

        top = [2048]

        def region(nbytes):
            at = top[0]
            top[0] = at + (nbytes + 31) // 32 * 32
            return at

        def put(name, shape, dt, at):
            return nc.alloc_sbuf_tensor_at(name, shape, dt, offset=at)

        def new(name, shape, dt=F32):
            n = 4
            for s in shape[1:]:
                n *= s
            return put(name, shape, dt, region(n))

        TILE = D * 4
        r_w = [region(2 * KT * TILE) for _ in range(4)]
        KW, VW, QW, OW = range(4)
        w_hi = [put(f"w_hi{i}", [P, KT, D], F32R, r_w[i]) for i in range(4)]
        w_lo = [put(f"w_lo{i}", [P, KT, D], F32R, r_w[i] + KT * TILE) for i in range(4)]
        h2_hi = [put(f"h2_hi{i}", [P, KT, S], F32R, r_w[i]) for i in range(NB)]
        h2_lo = [put(f"h2_lo{i}", [P, KT, S], F32R, r_w[i] + KT * TILE) for i in range(NB)]
        r_h = region(2 * KT * TILE)
        h_hi = put("h_hi", [P, KT, S], F32R, r_h)
        h_lo = put("h_lo", [P, KT, S], F32R, r_h + KT * TILE)
        xa = new("xa", [P, TT, D])
        xt = new("xt", [P, TT, D])
        r_kv = region(2 * TT * TILE + 2 * TT * KT * HW * 4)
        kp_hi = put("kp_hi", [P, TT, D], F32R, r_kv)
        kp_lo = put("kp_lo", [P, TT, D], F32R, r_kv + TT * TILE)
        r_v = r_kv + 2 * TT * TILE
        v_hi = put("v_hi", [P, TT, KT, HW], F32R, r_v)
        v_lo = put("v_lo", [P, TT, KT, HW], F32R, r_v + TT * KT * HW * 4)
        wm = [put(f"wm{i}", [P, KT, D], F32, r_kv + i * KT * TILE) for i in range(4)]
        x1res = put("x1res", [P, NB * TT, D], F32, r_kv)
        r_q = region(2 * KT * TILE)
        qp_hi = put("qp_hi", [P, KT, S], F32R, r_q)
        qp_lo = put("qp_lo", [P, KT, S], F32R, r_q + KT * TILE)
        raw1 = put("raw1", [P, KT, D], F32, r_q)
        r_a = region(2 * KT * TILE)
        at_hi = put("at_hi", [P, KT, S], F32R, r_a)
        at_lo = put("at_lo", [P, KT, S], F32R, r_a + KT * TILE)
        raw0 = put("raw0", [P, KT, D], F32, r_a)
        wtr = put("wtr", [P, KT, D], F32, r_a + KT * TILE)
        r_s = region(3 * 2 * KT * P * 4)
        st32 = put("st32", [P, 2 * KT, P], F32, r_s)
        st_hi = put("st_hi", [P, 2 * KT, P], F32R, r_s + 2 * KT * P * 4)
        st_lo = put("st_lo", [P, 2 * KT, P], F32R, r_s + 4 * KT * P * 4)
        gb_bc = put("gb_bc", [P, NB, D], F32, r_s)
        r_lin = region(2 * TILE)
        lin = put("lin", [P, 2, D], F32, r_lin)
        r_neg = region(2 * TILE)
        neg = put("neg", [P, 2, D], F32, r_neg)
        val = new("val", [P, 3, D])
        ot = new("ot", [P, 2, D])
        ga_bc = new("ga_bc", [P, 2, D])
        r_bias = region(3 * TILE)
        kb_bc = put("kb_bc", [P, D], F32, r_bias)
        vb_bc = put("vb_bc", [P, D], F32, r_bias + TILE)
        ob_bc = put("ob_bc", [P, D], F32, r_bias + 2 * TILE)
        gaob = new("gaob", [P, D])
        r_c = region(4 * NBLK * DC * 4)
        CB = NBLK * DC * 4
        c_raw = put("c_raw", [P, NBLK, DC], F32, r_c)
        c_tr = put("c_tr", [P, NBLK, DC], F32, r_c + CB)
        c_hi = put("c_hi", [P, NBLK, DC], F32R, r_c + 2 * CB)
        c_lo = put("c_lo", [P, NBLK, DC], F32R, r_c + 3 * CB)
        c_pp = put("c_pp", [P, NBLK, DC], F32, r_c + 3 * CB)
        ident = new("ident", [P, P])
        mask = new("mask", [P, P])
        had_r = new("had_r", [P, P], F32R)
        cs = put("cs", [NB, D], F32, r_neg)
        qb_row = put("qb_row", [KT, P], F32, r_lin)
        gr = put("gr", [NB, 2, D], F32, r_lin)
        gs = put("gs", [NB, 2, D], F32, r_neg)
        hada = put("hada", [P, P], F32, r_c + 2 * CB)
        hadb = put("hadb", [P, P], F32, r_c + 3 * CB)
        cT = new("cT", [P, KT * NB])
        modc = new("modc", [P, 4, KT, NB])
        qb_col = new("qb_col", [P, KT])
        mhalf = new("mhalf", [P, TT])
        stats = new("stats", [P, TT, 6])
        mv = new("mv", [P, TT, 2])
        ve = new("ve", [P, TT])
        rstd = new("rstd", [P, TT])

        FW = KT * GH * 4
        r_slot = [r_q, r_h]
        f1_hi = [put(f"f1_hi{i}", [P, KT, GH], F32R, r_slot[i]) for i in range(2)]
        f1_lo = [put(f"f1_lo{i}", [P, KT, GH], F32R, r_slot[i] + FW) for i in range(2)]
        f3_hi = [put(f"f3_hi{i}", [P, KT, GH], F32R, r_slot[i] + 2 * FW) for i in range(2)]
        f3_lo = [put(f"f3_lo{i}", [P, KT, GH], F32R, r_slot[i] + 3 * FW) for i in range(2)]
        f2_hi = put("f2_hi", [P, GB, D], F32R, r_a)
        f2_lo = put("f2_lo", [P, GB, D], F32R, r_a + GB * TILE)
        hd_hi = put("hd_hi", [P, GB, S], F32R, r_a + 2 * GB * TILE)
        hd_lo = put("hd_lo", [P, GB, S], F32R, r_a + 3 * GB * TILE)
        fraw = [put(f"fraw{i}", [P, KT, GH], F32, r_c + i * CB) for i in range(2)]
        f2raw = put("f2raw", [P, GB, D], F32, r_c + 2 * CB)
        ftr = put("ftr", [P, KT, GH], F32, r_lin)
        gate32 = put("gate32", [P, S], F32, r_neg)
        hid32 = put("hid32", [P, S], F32, r_neg + TILE)
        assert top[0] <= nc.sbuf_usable_end, (top[0], nc.sbuf_usable_end)

        bank = [ctx.enter_context(nc.psum_tensor(f"bank{i}", [P, 512], F32)) for i in range(8)]
        pj = bank[0:2]
        tr = bank[2:4]
        kvb = bank[4:6]
        zb, ab = bank[6], bank[7]
        gate_ps, up_ps = pj
        out_ps = bank[4:8]

        ld_c, ld_qb, ld_kb, ld_vb, ld_ob = (sem(f"ld_{n}") for n in ("c", "qb", "kb", "vb", "ob"))
        ld_xa = sem("ld_xa")
        ld_wm = [sem(f"ld_wm{i}") for i in range(4)]
        ld_raw = [sem(f"ld_raw{i}") for i in range(2)]
        ld_chunk = sem("ld_chunk")
        ld_xt = [sem(f"ld_xt{i}") for i in range(TT)]
        ld_ga = [sem(f"ld_ga{i}") for i in range(2)]
        st_g, st_chunk, st_x1 = sem("st_g"), sem("st_chunk"), sem("st_x1")
        const_ready = sem("const_ready")
        had_step, v_ones = sem("had_step"), sem("v_ones")
        mask_ready = sem("mask_ready")
        cT_ps_ready, cT_ready = sem("cT_ps_ready"), sem("cT_ready")
        mod_ps, mod_ready, g_step, wm_used = sem("mod_ps"), sem("mod_ready"), sem("g_step"), sem("wm_used")
        w_tr, w_hi_done, w_ready = sem("w_tr"), sem("w_hi_done"), sem("w_ready")
        stat_step, rstd_ready, xhat_ready = sem("stat_step"), sem("rstd_ready"), sem("xhat_ready")
        pool_step = sem("pool_step")
        tr_full, val_act, chunk_evac = sem("tr_full"), sem("val_act"), sem("chunk_evac")
        pj_full, lin_ready, neg_ready, exp_ready = sem("pj_full"), sem("lin_ready"), sem("neg_ready"), sem("exp_ready")
        val_dve, split_hi, split_lo = sem("val_dve"), sem("split_hi"), sem("split_lo")
        kv_full, st_ready, st_hi_done, st_split = sem("kv_full"), sem("st_ready"), sem("st_hi_done"), sem("st_split")
        att_full, ze_ready, inv_ready = sem("att_full"), sem("ze_ready"), sem("inv_ready")
        ot_ready, gaob_ready, xob_ready, x1_ready = sem("ot_ready"), sem("gaob_ready"), sem("xob_ready"), sem("x1_ready")
        chunk_tr, chunk_hi, chunk_lo, chunk_step = sem("chunk_tr"), sem("chunk_hi"), sem("chunk_lo"), sem("chunk_step")
        ld_gb, ld_x1 = sem("ld_gb"), [sem(f"ld_x1_{b}") for b in range(NB)]
        ld_f = [sem("ld_f1"), sem("ld_f3")]
        ld_f2 = sem("ld_f2")
        f_tr, f_hi, f_lo = sem("f_tr"), sem("f_hi"), sem("f_lo")
        f2_hi_done, f2_ready = sem("f2_hi_done"), sem("f2_ready")
        gate_full, up_full, gate_used, up_used = sem("gate_full"), sem("up_full"), sem("gate_used"), sem("up_used")
        hid_hi, hid_lo = sem("hid_hi"), sem("hid_lo")
        out_full, contrib, added = sem("out_full"), sem("contrib"), sem("added")
        st_out = sem("st_out")

        pj_at, tr_at, split_at, exp_at, dve_at, act_at, ot_at = {}, {}, {}, {}, {}, {}, {}

        def use(where, key):
            where[key] = len(where)

        def use_split(key, by):
            use(split_at, key)
            use(by, key)

        for kt in range(KT):
            use(tr_at, ("h", 0, kt))
            use_split(("h", 0, kt), act_at)
        for b in range(NB + 1):
            for kind in ("k", "v", "q"):
                for t in range(TT):
                    if b < NB:
                        use(pj_at, (kind, b, t))
                        use_split((kind, b, t), dve_at)
                        if kind != "v":
                            use(exp_at, (kind, b, t))
                    if kind == "v" and b >= 1:
                        use_split(("a", b - 1, t), dve_at)
                if kind != "v" and b < NB:
                    for i in range(2):
                        use(tr_at, ("chunk", 2 * b + (kind == "q"), i))
            if b + 1 < NB:
                for kt in range(KT):
                    use(tr_at, ("h", b + 1, kt))
                    use_split(("h", b + 1, kt), act_at)
            if b >= 1:
                for t in range(TT):
                    use(pj_at, ("o", b - 1, t))
                    use(ot_at, (b - 1, t))
        for b in range(NB):
            for kt in range(KT):
                use(tr_at, ("h2", b, kt))
                use_split(("h2", b, kt), act_at)
        pj_order, tr_order, exp_order = list(pj_at), list(tr_at), list(exp_at)
        raw_of = {KW: raw0, VW: raw1, QW: raw0, OW: raw0}
        raw_wait = {KW: (0, 256), VW: (1, 256), QW: (0, 512), OW: (0, 768)}
        w_dram = {KW: k_w, VW: v_w, QW: q_w, OW: o_w}

        def split_tile(key):
            kind, b, t = key
            if kind == "k":
                return kp_hi[:, t, :], kp_lo[:, t, :]
            if kind == "v":
                return v_hi[:, t, :, 0:P], v_lo[:, t, :, 0:P]
            if kind == "q":
                return qp_hi[:, t, :], qp_lo[:, t, :]
            if kind == "a":
                return at_hi[:, t, :], at_lo[:, t, :]
            if kind == "h":
                return h_hi[:, t, :], h_lo[:, t, :]
            return h2_hi[b][:, t, :], h2_lo[b][:, t, :]

        def val_tile(key):
            v = val[:, split_at[key] % 3, :]
            return v.rearrange("p (g e) -> p g e", g=KT) if key[0] == "v" else v

        def blocks_of(w_ap, q, kt):
            k0 = P * kt + Q32 * q
            return w_ap[:, k0:k0 + Q32].rearrange("(v j) i -> j v i", j=Q32)

        def blocks_at(tile, q, kt):
            return tile[Q32 * q:Q32 * q + Q32, kt, :].rearrange("j (v i) -> j v i", i=Q32)

        block = ctx.enter_context(nc.Block())

        @block.sync
        def _(sp):
            def load_weight(i):
                n, total = raw_wait[i]
                for kt in range(KT):
                    for q in range(NQ):
                        sp.dma_start(blocks_at(raw_of[i], q, kt), blocks_of(w_dram[i], q, kt)).then_inc(ld_raw[n], 16)

            def load_wm(slot, section):
                sp.dma_start(wm[slot][:, :, :],
                             wmod[:, section * D:(section + 1) * D].rearrange("(k p) n -> p k n", p=P)).then_inc(ld_wm[slot], 16)

            def load_xa(b):
                sp.dma_start(xa[:, :, :], x[b, :, :].rearrange("(t p) d -> p t d", p=P)).then_inc(ld_xa, 16)

            def load_chunk(n):
                if n >= 1:
                    sp.wait_ge(chunk_tr, n)
                for q in range(NQ):
                    for v in range(DC // Q32):
                        r0 = n * DC + v * Q32
                        src = W2[r0:r0 + Q32, :].rearrange("j (k a i) -> j k a i", a=NQ, i=Q32)[:, :, q, :]
                        dst = c_raw[Q32 * q:Q32 * q + Q32, :, v * Q32:(v + 1) * Q32]
                        sp.dma_start(dst, src).then_inc(ld_chunk, 16)

            def store_chunk(n):
                sp.wait_ge(chunk_step, 8 * (n + 1))
                sp.dma_start(w2t_dram[:, :, n * DC:(n + 1) * DC].rearrange("b p d -> p b d"), c_tr[:, :, :]).then_inc(st_chunk, 16)

            def load_xt(b, t):
                if b >= 1:
                    sp.wait_ge(st_x1, 16 * (TT * (b - 1) + TT))
                sp.dma_start(xt[:, t, :], x[b, t * P:(t + 1) * P, :]).then_inc(ld_xt[t], 16)

            def load_ga(b):
                if b >= 2:
                    sp.wait_ge(x1_ready, TT * (b - 1))
                sp.dma_start(ga_bc[:, b % 2, :], g_dram[b, 0, :].partition_broadcast(P)).then_inc(ld_ga[b % 2], 16)

            sp.dma_start(cs[:, :], c).then_inc(ld_c, 16)
            sp.dma_start(qb_row[:, :], q_b.rearrange("(g p) -> g p", p=P)).then_inc(ld_qb, 16)
            load_xa(0)
            load_wm(0, 0)
            load_wm(1, 1)
            load_weight(KW)
            sp.dma_start(kb_bc[:, :], k_b.partition_broadcast(P)).then_inc(ld_kb, 16)
            sp.dma_start(vb_bc[:, :], v_b.partition_broadcast(P)).then_inc(ld_vb, 16)
            sp.dma_start(ob_bc[:, :], o_b.partition_broadcast(P)).then_inc(ld_ob, 16)
            load_wm(2, 2)
            load_wm(3, 5)
            sp.wait_ge(wm_used, 2)
            load_wm(0, 3)
            load_wm(1, 4)
            load_weight(VW)
            sp.wait_ge(w_tr, 1)
            load_weight(QW)
            load_chunk(0)
            sp.wait_ge(g_step, 7)
            sp.dma_start(g_dram, gr[:, :, :]).then_inc(st_g, 16)
            sp.wait_ge(st_g, 16)
            load_ga(0)
            load_ga(1)
            for b in range(NB + 1):
                if b + 1 < NB:
                    sp.wait_ge(tr_full, tr_at[("h", b, KT - 1)] + 1)
                    load_xa(b + 1)
                if b < NB:
                    load_chunk(2 * b + 1)
                if b >= 1:
                    for t in range(TT):
                        load_xt(b - 1, t)
                if b >= 3:
                    load_ga(b - 1)
                if b < NB:
                    store_chunk(2 * b)
                if b == 0:
                    sp.wait_ge(w_tr, 3)
                    load_weight(OW)
                if b + 1 < NB:
                    load_chunk(2 * b + 2)
                for t in range(TT):
                    if b >= 1:
                        sp.wait_ge(x1_ready, TT * (b - 1) + t + 1)
                        sp.dma_start(x1_dram[b - 1, t * P:(t + 1) * P, :], xt[:, t, :]).then_inc(st_x1, 16)
                if b < NB:
                    store_chunk(2 * b + 1)
            sp.wait_ge(att_full, NB * KT)
            sp.wait_ge(st_x1, 16 * NB * TT)
            sp.wait_ge(st_chunk, 16 * NCH)
            for b in range(NB):
                sp.dma_start(x1res[:, TT * b:TT * b + TT, :], x1_dram[b, :, :].rearrange("(t p) d -> p t d", p=P)).then_inc(ld_x1[b], 16)

            def load_f(m, w_ap):
                for kt in range(KT):
                    for q in range(NQ):
                        k0 = P * kt + Q32 * q
                        sp.dma_start(blocks_at(fraw[m], q, kt), w_ap[:, k0:k0 + Q32].rearrange("(v j) i -> j v i", j=Q32)).then_inc(ld_f[m], 16)

            def load_f2(g):
                sp.dma_start(f2raw[:, :, :], w2t_dram[bass.ds(g * GB, GB), :, :].rearrange("b p d -> p b d")).then_inc(ld_f2, 16)

            load_f(0, W1[0:GH, :])
            load_f(1, W3[0:GH, :])
            load_f2(0)
            sp.dma_start(gb_bc[:, :, :], g_dram[:, 1, :].partition_broadcast(P)).then_inc(ld_gb, 16)
            with sp.Fori(1, NG) as g:
                sp.wait_ge(f_tr, 2 * g - 1)
                load_f(0, W1[bass.ds(g * GH, GH), :])
                sp.wait_ge(f_tr, 2 * g)
                load_f(1, W3[bass.ds(g * GH, GH), :])
                sp.wait_ge(f2_ready, g)
                load_f2(g)
            for b in range(NB):
                for t in range(TT):
                    n = (NG - 1) * NB * TT + TT * b + t
                    sp.wait_ge(added, n + 1 + 2)
                    sp.dma_start(out[b, t * P:(t + 1) * P, :], x1res[:, TT * b + t, :]).then_inc(st_out, 16)
            sp.wait_ge(st_out, 16 * NB * TT)

        @block.tensor
        def _(pe):
            def three(o, l_hi, l_lo, r_hi, r_lo, first, last):
                nc.tensor.matmul(o, l_hi, r_hi, start=first, stop=False)
                nc.tensor.matmul(o, l_hi, r_lo, start=False, stop=False)
                return nc.tensor.matmul(o, l_lo, r_hi, start=False, stop=last)

            def wait_pj(key):
                n = pj_at[key]
                if n < 2:
                    pe.wait_ge(mod_ready, 2 * n + 2)
                    return
                old = pj_order[n - 2]
                if old[0] == "v":
                    pe.wait_ge(val_dve, dve_at[old] + 1)
                elif old[0] == "o":
                    pe.wait_ge(ot_ready, ot_at[old[1:]] + 1)
                else:
                    pe.wait_ge(lin_ready, exp_at[old] + 1)

            def wait_tr(key):
                n = tr_at[key]
                if n < 2:
                    return
                old = tr_order[n - 2]
                if old[0] == "chunk":
                    pe.wait_ge(chunk_evac, 2 * old[1] + old[2] + 1)
                else:
                    pe.wait_ge(val_act, act_at[old] + 1)

            def transposes(kind, b, src):
                pe.wait_ge(xhat_ready, TT * (b + (NB if kind == "h2" else 0)) + TT)
                for kt in range(KT):
                    key = (kind, b, kt)
                    wait_tr(key)
                    for t in range(TT):
                        mm = nc.tensor.transpose(tr[tr_at[key] % 2][:, t * P:(t + 1) * P], src[:, t, kt * P:(kt + 1) * P], ident[:, :])
                    mm.then_inc(tr_full, 1)

            def project_tile(kind, b, t):
                key = (kind, b, t)
                wait_pj(key)
                o = pj[pj_at[key] % 2][:, :]
                w = {"k": KW, "v": VW, "q": QW, "o": OW}[kind]
                a_hi, a_lo = (at_hi, at_lo) if kind == "o" else (h_hi, h_lo)
                for kt in range(KT):
                    ts = slice(t * P, (t + 1) * P)
                    if kind == "q":
                        mm = three(o, w_hi[w][:, kt, ts], w_lo[w][:, kt, ts], a_hi[:, kt, :], a_lo[:, kt, :], kt == 0, kt == KT - 1)
                    else:
                        mm = three(o, a_hi[:, kt, ts], a_lo[:, kt, ts], w_hi[w][:, kt, :], w_lo[w][:, kt, :], kt == 0, kt == KT - 1)
                mm.then_inc(pj_full, 1)

            def attend(b, g):
                if g == 0:
                    pe.wait_ge(st_split, b + 1)
                    pe.wait_ge(split_lo, split_at[("q", b, KT - 1)] + 1)
                n = KT * b + g
                if n >= 1:
                    pe.wait_ge(ze_ready, n)
                    pe.wait_ge(val_dve, dve_at[("a", (n - 1) // KT, (n - 1) % KT)] + 1)
                three(zb[:, :], st_hi[:, KT + g, :], st_lo[:, KT + g, :], qp_hi[:, g, :], qp_lo[:, g, :], True, True)
                three(ab[:, :], st_hi[:, g, :], st_lo[:, g, :], qp_hi[:, g, :], qp_lo[:, g, :], True, True).then_inc(att_full, 1)

            def key_values(b):
                pe.wait_ge(split_lo, split_at[("v", b, TT - 1)] + 1)
                if b >= 1:
                    pe.wait_ge(st_ready, 2 * KT * b)
                else:
                    pe.wait_ge(g_step, 4)
                    pe.wait_ge(v_ones, 2)
                for g in range(KT):
                    o = kvb[g // 2][:, (g % 2) * HW:(g % 2 + 1) * HW]
                    gs_ = slice(g * P, (g + 1) * P)
                    for t in range(TT):
                        mm = three(o, kp_hi[:, t, gs_], kp_lo[:, t, gs_], v_hi[:, t, g, :], v_lo[:, t, g, :], t == 0, t == TT - 1)
                    if g % 2:
                        mm.then_inc(kv_full, 1)

            def hadamard(n):
                pe.wait_ge(chunk_lo, n + 1)
                for i in range(2):
                    key = ("chunk", n, i)
                    wait_tr(key)
                    o = tr[tr_at[key] % 2][:, :]
                    bs = slice(i * NBLK // 2, (i + 1) * NBLK // 2)
                    nc.tensor.matmul(o, had_r[:, :], c_hi[:, bs, :], start=True, stop=False)
                    nc.tensor.matmul(o, had_r[:, :], c_lo[:, bs, :], start=False, stop=True).then_inc(tr_full, 1)

            pe.wait_ge(const_ready, 2)
            pe.wait_ge(ld_c, 16)
            for kt in range(KT):
                nc.tensor.transpose(bank[4][:, kt * NB:(kt + 1) * NB], cs[:, kt * P:(kt + 1) * P], ident[0:NB, 0:NB])
            pe.wait_ge(ld_qb, 16)
            nc.tensor.transpose(bank[4][:, KT * NB:KT * NB + KT], qb_row[:, :], ident[0:KT, 0:KT]).then_inc(cT_ps_ready, 1)
            pe.wait_ge(cT_ready, 2)

            def mod_columns(slot, total, o, s):
                pe.wait_ge(ld_wm[slot], total)
                for m in range(KT):
                    for k in range(KT):
                        mm = nc.tensor.matmul(o[:, (s * KT + m) * NB:(s * KT + m + 1) * NB], wm[slot][:, k, m * P:(m + 1) * P],
                                              cT[:, k * NB:(k + 1) * NB], start=(k == 0), stop=(k == KT - 1))
                mm.then_inc(wm_used, 1)

            def mod_rows(slot, o):
                pe.wait_ge(ld_wm[slot], 16)
                for k in range(KT):
                    mm = nc.tensor.matmul(o[0:NB, :], cT[:, k * NB:(k + 1) * NB], wm[slot][:, k, :], start=(k == 0), stop=(k == KT - 1))
                mm.then_inc(wm_used, 1)

            mod_columns(0, 16, pj[0], 0)
            mod_columns(1, 16, pj[0], 1)
            transposes("h", 0, xa)
            mod_rows(2, kvb[0])
            mod_rows(3, kvb[1])
            mod_columns(0, 32, pj[1], 0)
            mod_columns(1, 32, pj[1], 1)

            for b in range(NB + 1):
                if b < NB:
                    pe.wait_ge(w_ready, 1)
                    pe.wait_ge(split_lo, split_at[("h", b, KT - 1)] + 1)
                    for t in range(TT):
                        project_tile("k", b, t)
                    if b == 0:
                        pe.wait_ge(had_step, 14)
                    hadamard(2 * b)
                    pe.wait_ge(w_ready, 2)
                for t in range(TT):
                    if b < NB:
                        project_tile("v", b, t)
                    if b >= 1:
                        attend(b - 1, t)
                if b < NB:
                    pe.wait_ge(w_ready, 3)
                    for t in range(TT):
                        project_tile("q", b, t)
                    hadamard(2 * b + 1)
                if b + 1 < NB:
                    transposes("h", b + 1, xa)
                if b >= 1:
                    pe.wait_ge(w_ready, 4)
                    pe.wait_ge(split_lo, split_at[("a", b - 1, KT - 1)] + 1)
                    for t in range(TT):
                        project_tile("o", b - 1, t)
                if b < NB:
                    key_values(b)

            for b in range(NB):
                transposes("h2", b, xa)
            pe.wait_ge(split_lo, len(split_at))

            def ffn(g, par, b):
                n = (g * NB + b) * GB
                if b == 0:
                    pe.wait_ge(f_lo, 2 * g + 2)
                for i in range(GB):
                    hs = slice(i * P, (i + 1) * P)
                    for o, f_h, f_l, used, full in ((gate_ps, f1_hi, f1_lo, gate_used, gate_full), (up_ps, f3_hi, f3_lo, up_used, up_full)):
                        pe.wait_ge(used, n + i + 1)
                        for kt in range(KT):
                            mm = three(o[:, :], f_h[par][:, kt, hs], f_l[par][:, kt, hs], h2_hi[b][:, kt, :], h2_lo[b][:, kt, :], kt == 0, kt == KT - 1)
                        mm.then_inc(full, 1)
                if b == 0:
                    pe.wait_ge(f2_ready, g + 1)
                for i in range(GB):
                    pe.wait_ge(hid_lo, n + i + 2)
                    for t in range(TT):
                        if i == 0:
                            pe.wait_ge(contrib, (g * NB + b) * TT + t + 1)
                        ts = slice(t * P, (t + 1) * P)
                        mm = three(out_ps[t][:, :], hd_hi[:, i, ts], hd_lo[:, i, ts], f2_hi[:, i, :], f2_lo[:, i, :], i == 0, i == GB - 1)
                        if i == GB - 1:
                            mm.then_inc(out_full, 1)

            with pe.Fori(0, NG, 2) as g:
                for par in range(2):
                    for b in range(NB):
                        ffn(g + par, par, b)

        @block.scalar
        def _(act):
            def to_hi(key):
                if key in dve_at:
                    act.wait_ge(val_dve, dve_at[key] + 1)
                else:
                    act.wait_ge(val_act, act_at[key] + 1)
                nc.scalar.activation(split_tile(key)[0], val_tile(key), ACT.Copy).then_inc(split_hi, 1)

            def modulate(kind, b):
                s = 0 if kind == "h" else 2
                for kt in range(KT):
                    key = (kind, b, kt)
                    act.wait_ge(tr_full, tr_at[key] + 1)
                    if split_at[key] >= 3:
                        act.wait_ge(split_lo, split_at[key] - 2)
                    nc.scalar.activation(val_tile(key), tr[tr_at[key] % 2][:, :], ACT.Identity,
                                         bias=modc[:, s, kt, b:b + 1], scale=modc[:, s + 1, kt, b:b + 1]).then_inc(val_act, 1)
                    to_hi(key)

            def exp_tile(key):
                act.wait_ge(neg_ready, exp_at[key] + 1)
                s = exp_at[key] % 2
                nc.scalar.activation(neg[:, s, :], neg[:, s, :], ACT.Exp).then_inc(exp_ready, 1)

            def normaliser(b, g):
                n = KT * b + g
                act.wait_ge(att_full, n + 1)
                if n >= 2:
                    old = ("a", (n - 2) // KT, (n - 2) % KT)
                    act.wait_ge(val_dve, dve_at[old] + 1)
                nc.scalar.activation(neg[:, n % 2, :], zb[:, :], ACT.Copy, bias=EPS_Z).then_inc(ze_ready, 1)

            def chunk_to_hi(n):
                act.wait_ge(chunk_tr, n + 1)
                nc.scalar.activation(c_hi[:, :, :], c_tr[:, :, :], ACT.Copy).then_inc(chunk_hi, 1)

            def chunk_out(n):
                for i in range(2):
                    key = ("chunk", n, i)
                    act.wait_ge(tr_full, tr_at[key] + 1)
                    nc.scalar.activation(c_tr[:, i * NBLK // 2:(i + 1) * NBLK // 2, :],
                                         tr[tr_at[key] % 2][:, :].rearrange("p (b d) -> p b d", d=DC),
                                         ACT.Copy, scale=float(HID) ** -0.5).then_inc(chunk_evac, 1)

            def weight_to_hi(i):
                act.wait_ge(w_tr, i + 1)
                nc.scalar.activation(w_hi[i][:, :, :], wtr[:, :, :], ACT.Copy).then_inc(w_hi_done, 1)

            def feature_tiles(kind, b):
                n = 2 * b + (kind == "q")
                for t in range(TT):
                    exp_tile((kind, b, t))
                    if t >= 1:
                        to_hi((kind, b, t - 1))
                    if t == 1:
                        chunk_to_hi(n)
                to_hi((kind, b, TT - 1))
                chunk_out(n)

            act.wait_ge(cT_ps_ready, 1)
            nc.scalar.activation(cT[:, :], bank[4][:, 0:KT * NB], ACT.Silu).then_inc(cT_ready, 1)
            nc.scalar.activation(qb_col[:, :], bank[4][:, KT * NB:KT * NB + KT], ACT.Copy).then_inc(cT_ready, 1)
            weight_to_hi(KW)
            act.wait_ge(mod_ready, 2)
            modulate("h", 0)
            for b in range(NB + 1):
                if b < NB:
                    feature_tiles("k", b)
                    if b == 0:
                        weight_to_hi(VW)
                for t in range(TT):
                    if b < NB:
                        to_hi(("v", b, t))
                    if b >= 1:
                        normaliser(b - 1, t)
                        to_hi(("a", b - 1, t))
                if b < NB:
                    if b == 0:
                        weight_to_hi(QW)
                    feature_tiles("q", b)
                    if b == 0:
                        weight_to_hi(OW)
                if b + 1 < NB:
                    modulate("h", b + 1)
                if b < NB:
                    act.wait_ge(st_ready, 2 * KT * (b + 1))
                    nc.scalar.activation(st_hi[:, :, :], st32[:, :, :], ACT.Copy).then_inc(st_hi_done, 1)

            act.wait_ge(mod_ready, 4)
            for b in range(NB):
                modulate("h2", b)

            def weight_hi(count, which, par):
                act.wait_ge(f_tr, count)
                nc.scalar.activation((f1_hi, f3_hi)[which][par][:, :, :], ftr[:, :, :], ACT.Copy).then_inc(f_hi, 1)

            def ffn(g, par, b, more):
                n = (g * NB + b) * GB
                for i in range(GB):
                    act.wait_ge(gate_full, n + i + 1)
                    act.wait_ge(up_used, n + i + 1)
                    nc.scalar.activation(gate32[:, :], gate_ps[:, :], ACT.Silu).then_inc(gate_used, 1)
                    if b == 0 and i == 0:
                        act.wait_ge(ld_f2, 16 * g + 16)
                        nc.scalar.activation(f2_hi[:, :, :], f2raw[:, :, :], ACT.Copy).then_inc(f2_hi_done, 1)
                    act.wait_ge(up_used, n + i + 2)
                    nc.scalar.activation(hd_hi[:, i, :], hid32[:, :], ACT.Copy).then_inc(hid_hi, 1)
                    if i == 0 and more and b < 2:
                        weight_hi(2 * g + 3 + b, b, 1 - par)

            act.sem_inc(gate_used, 1)
            act.wait_ge(att_full, NB * KT)
            weight_hi(1, 0, 0)
            weight_hi(2, 1, 0)
            with act.Fori(0, NG - 2, 2) as g:
                for par in range(2):
                    for b in range(NB):
                        ffn(g + par, par, b, True)
            for par in range(2):
                for b in range(NB):
                    ffn(NG - 2 + par, par, b, par == 0)

        @block.vector
        def _(dve):
            def layer_norm(n, src):
                if n >= 1:
                    dve.wait_ge(stat_step, 9 * n)
                for t in range(TT):
                    nc.vector.bn_stats(stats[:, t, :], src[:, t, :]).then_inc(stat_step, 1)

            def layer_norm_rest(n):
                if n >= 1:
                    dve.wait_ge(xhat_ready, TT * n)
                for t in range(TT):
                    dve.wait_ge(stat_step, 9 * n + t + 1)
                    nc.vector.bn_aggr(mv[:, t, :], stats[:, t, :]).then_inc(stat_step, 1)
                dve.wait_ge(stat_step, 9 * n + 8)
                nc.vector.tensor_scalar(ve[:, :], mv[:, :, 1], EPS_LN, None, ALU.add).then_inc(stat_step, 1)

            def normalise(n, t, dst, src):
                if t == 0:
                    dve.wait_ge(rstd_ready, n + 1)
                nc.vector.tensor_scalar(dst[:, t, :], src[:, t, :], mv[:, t, 0:1], rstd[:, t:t + 1],
                                        ALU.subtract, ALU.mult).then_inc(xhat_ready, 1)

            def prepare_weight(i):
                n, total = raw_wait[i]
                dve.wait_ge(ld_raw[n], total)
                if i >= 1:
                    dve.wait_ge(w_ready, i)
                nc.vector.transpose(wtr[:, :, :], raw_of[i][:, :, :]).then_inc(w_tr, 1)
                dve.wait_ge(w_hi_done, i + 1)
                nc.vector.tensor_tensor(w_lo[i][:, :, :], wtr[:, :, :], w_hi[i][:, :, :].bitcast(F32), ALU.subtract).then_inc(w_ready, 1)

            def chunk_transpose(n):
                dve.wait_ge(ld_chunk, 16 * NQ * (DC // Q32) * (n + 1))
                if n >= 1:
                    dve.wait_ge(st_chunk, 16 * n)
                nc.vector.transpose(c_tr[:, :, :], c_raw[:, :, :]).then_inc(chunk_tr, 1)

            def chunk_to_lo(n):
                dve.wait_ge(chunk_hi, n + 1)
                if n >= 1:
                    dve.wait_ge(chunk_step, 8 * n)
                nc.vector.tensor_tensor(c_lo[:, :, :], c_tr[:, :, :], c_hi[:, :, :].bitcast(F32), ALU.subtract).then_inc(chunk_lo, 1)

            def butterfly(n, s):
                if s == 0:
                    dve.wait_ge(chunk_evac, 2 * n + 2)
                else:
                    dve.wait_ge(chunk_step, 8 * n + 2 * s)
                src, dst = (c_tr, c_pp) if s % 2 == 0 else (c_pp, c_tr)
                a = src[:, :, :].rearrange("p (n u h) d -> p n u (h d)", u=2, h=1 << s)
                o = dst[:, :, :].rearrange("p (n u h) d -> p n u (h d)", u=2, h=1 << s)
                for u, op in ((0, ALU.add), (1, ALU.subtract)):
                    nc.vector.tensor_tensor(o[:, :, u, :], a[:, :, 0, :], a[:, :, 1, :], op).then_inc(chunk_step, 1)

            def wait_val(key):
                if split_at[key] >= 3:
                    dve.wait_ge(split_lo, split_at[key] - 2)

            def feature_front(key):
                kind, b, t = key
                e = exp_at[key]
                s = e % 2
                if e >= 2:
                    dve.wait_ge(val_dve, dve_at[exp_order[e - 2]] + 1)
                dve.wait_ge(pj_full, pj_at[key] + 1)
                ps = pj[pj_at[key] % 2][:, :]
                if kind == "k":
                    nc.vector.tensor_tensor(lin[:, s, :], ps, kb_bc[:, :], ALU.add).then_inc(lin_ready, 1)
                else:
                    nc.vector.tensor_scalar(lin[:, s, :], ps, qb_col[:, t:t + 1], None, ALU.add).then_inc(lin_ready, 1)
                dve.wait_ge(lin_ready, e + 1)
                nc.vector.tensor_scalar(neg[:, s, :], lin[:, s, :], 0.0, None, ALU.min).then_inc(neg_ready, 1)

            def feature_back(key):
                e = exp_at[key]
                dve.wait_ge(exp_ready, e + 1)
                wait_val(key)
                nc.vector.scalar_tensor_tensor(val_tile(key), lin[:, e % 2, :], 0.0, neg[:, e % 2, :],
                                               ALU.max, ALU.add).then_inc(val_dve, 1)

            dve.wait_ge(const_ready, 2)
            src = ident
            for s in range(7):
                dst = had_r if s == 6 else (hada, hadb)[s % 2]
                if s >= 1:
                    dve.wait_ge(had_step, 2 * s)
                a = src[:, :].rearrange("p (n u h) -> p n u h", u=2, h=1 << s)
                o = dst[:, :].rearrange("p (n u h) -> p n u h", u=2, h=1 << s)
                for u, op in ((0, ALU.add), (1, ALU.subtract)):
                    nc.vector.tensor_tensor(o[:, :, u, :], a[:, :, 0, :], a[:, :, 1, :], op).then_inc(had_step, 1)
                src = dst
            dve.wait_ge(ld_xa, 16)
            layer_norm(0, xa)
            layer_norm_rest(0)
            for t in range(TT):
                normalise(0, t, xa, xa)
            n_col = KT * NB
            dve.wait_ge(wm_used, 2)
            nc.vector.tensor_copy(modc[:, 0, :, :], pj[0][:, 0:n_col].rearrange("p (k b) -> p k b", b=NB)).then_inc(mod_ready, 1)
            nc.vector.tensor_scalar(modc[:, 1, :, :], pj[0][:, n_col:2 * n_col].rearrange("p (k b) -> p k b", b=NB),
                                    1.0, None, ALU.add).then_inc(mod_ready, 1)
            prepare_weight(KW)
            dve.wait_ge(wm_used, 4)
            for i in range(2):
                nc.vector.tensor_scalar(gs[:, i, :], kvb[i][0:NB, :], 0.0, 2.0, ALU.is_ge, ALU.mult).then_inc(g_step, 1)
            for i in range(2):
                nc.vector.tensor_copy(gr[:, i, :], kvb[i][0:NB, :]).then_inc(g_step, 1)
            dve.wait_ge(g_step, 2)
            nc.vector.tensor_scalar(gs[:, :, :], gs[:, :, :], -1.0, None, ALU.add).then_inc(g_step, 1)
            dve.wait_ge(g_step, 4)
            nc.vector.scalar_tensor_tensor(gr[:, :, :], gr[:, :, :], -1.0, gr[:, :, :], ALU.mult, ALU.max).then_inc(g_step, 1)
            dve.wait_ge(g_step, 6)
            nc.vector.scalar_tensor_tensor(gr[:, :, :], gr[:, :, :], G_MIN, gs[:, :, :], ALU.max, ALU.mult).then_inc(g_step, 1)
            dve.wait_ge(wm_used, 6)
            nc.vector.tensor_copy(modc[:, 2, :, :], pj[1][:, 0:n_col].rearrange("p (k b) -> p k b", b=NB)).then_inc(mod_ready, 1)
            nc.vector.tensor_scalar(modc[:, 3, :, :], pj[1][:, n_col:2 * n_col].rearrange("p (k b) -> p k b", b=NB),
                                    1.0, None, ALU.add).then_inc(mod_ready, 1)
            dve.wait_ge(st_g, 16)
            dve.wait_ge(ld_kb, 16)
            dve.wait_ge(ld_vb, 16)
            dve.wait_ge(cT_ready, 2)
            dve.wait_ge(mask_ready, 1)
            for b in range(NB + 1):
                if b < NB:
                    if b + 1 < NB:
                        dve.wait_ge(ld_xa, 16 * (b + 2))
                        layer_norm(b + 1, xa)
                    for t in range(TT):
                        feature_front(("k", b, t))
                        if t >= 1:
                            feature_back(("k", b, t - 1))
                        if t == 0:
                            chunk_transpose(2 * b)
                        if t == 2:
                            chunk_to_lo(2 * b)
                    feature_back(("k", b, TT - 1))
                    if b == 0:
                        prepare_weight(VW)
                    if b + 1 < NB:
                        layer_norm_rest(b + 1)
                for t in range(TT):
                    if b < NB:
                        key = ("v", b, t)
                        dve.wait_ge(pj_full, pj_at[key] + 1)
                        wait_val(key)
                        nc.vector.tensor_tensor(val_tile(key), pj[pj_at[key] % 2][:, :].rearrange("p (g e) -> p g e", g=KT),
                                                vb_bc[:, :].rearrange("p (g e) -> p g e", g=KT), ALU.add).then_inc(val_dve, 1)
                        butterfly(2 * b, t)
                    if b >= 1:
                        key = ("a", b - 1, t)
                        n = KT * (b - 1) + t
                        dve.wait_ge(ze_ready, n + 1)
                        nc.vector.reciprocal(neg[:, n % 2, :], neg[:, n % 2, :]).then_inc(inv_ready, 1)
                        wait_val(key)
                        dve.wait_ge(inv_ready, n + 1)
                        nc.vector.tensor_tensor(val_tile(key), ab[:, :], neg[:, n % 2, :], ALU.mult).then_inc(val_dve, 1)
                if b < NB:
                    if b == 0:
                        prepare_weight(QW)
                    for t in range(TT):
                        if b + 1 < NB:
                            normalise(b + 1, t, xa, xa)
                        feature_front(("q", b, t))
                        if t >= 1:
                            feature_back(("q", b, t - 1))
                        if t == 0:
                            chunk_transpose(2 * b + 1)
                        if t == 2:
                            chunk_to_lo(2 * b + 1)
                    feature_back(("q", b, TT - 1))
                    if b == 0:
                        prepare_weight(OW)
                for t in range(TT):
                    if b >= 1:
                        key = ("o", b - 1, t)
                        n = ot_at[(b - 1, t)]
                        if t == 0:
                            dve.wait_ge(ld_ga[(b - 1) % 2], 16 * ((b - 1) // 2 + 1))
                        dve.wait_ge(pj_full, pj_at[key] + 1)
                        if n >= 2:
                            dve.wait_ge(x1_ready, n - 1)
                        nc.vector.tensor_tensor(ot[:, n % 2, :], pj[pj_at[key] % 2][:, :], ga_bc[:, (b - 1) % 2, :],
                                                ALU.mult).then_inc(ot_ready, 1)
                    if b < NB:
                        butterfly(2 * b + 1, t)
                if b < NB:
                    if b >= 1:
                        dve.wait_ge(st_split, b)
                    for g in range(KT):
                        if g % 2 == 0:
                            dve.wait_ge(kv_full, 2 * b + g // 2 + 1)
                        ps = kvb[g // 2][:, (g % 2) * HW:(g % 2 + 1) * HW]
                        nc.vector.tensor_tensor(st32[:, g, :], ps[:, 0:P], mask[:, :], ALU.mult).then_inc(st_ready, 1)
                        nc.vector.tensor_scalar(st32[:, KT + g, :], mask[:, :], ps[:, P:P + 1], None, ALU.mult).then_inc(st_ready, 1)

            for b in range(NB):
                dve.wait_ge(ld_x1[b], 16)
                x1b = x1res[:, TT * b:TT * b + TT, :]
                layer_norm(NB + b, x1b)
                layer_norm_rest(NB + b)
                last = ("h2", b - 1, KT - 1) if b else ("h", NB - 1, KT - 1)
                dve.wait_ge(tr_full, tr_at[last] + 1)
                for t in range(TT):
                    normalise(NB + b, t, xa, x1b)

            def ffn_transpose(count, which):
                dve.wait_ge(f_lo, count)
                nc.vector.transpose(ftr[:, :, :], fraw[which][:, :, :]).then_inc(f_tr, 1)

            def contribution(g, b):
                for t in range(TT):
                    m = (g * NB + b) * TT + t
                    dve.wait_ge(out_full, m + 1)
                    dve.wait_ge(added, m + 1)
                    nc.vector.tensor_tensor(ot[:, t % 2, :], out_ps[t][:, :], gb_bc[:, b, :], ALU.mult).then_inc(contrib, 1)

            def ffn(g, par, b, more):
                n = (g * NB + b) * GB
                for i in range(GB):
                    dve.wait_ge(hid_lo, n + i + 1)
                    dve.wait_ge(gate_used, n + i + 2)
                    dve.wait_ge(up_full, n + i + 1)
                    nc.vector.tensor_tensor(hid32[:, :], up_ps[:, :], gate32[:, :], ALU.mult).then_inc(up_used, 1)
                    dve.wait_ge(hid_hi, n + i + 1)
                    nc.vector.tensor_tensor(hd_lo[:, i, :], hid32[:, :], hd_hi[:, i, :].bitcast(F32), ALU.subtract).then_inc(hid_lo, 1)
                    if i == 0 and b == 0:
                        dve.wait_ge(f2_hi_done, g + 1)
                        nc.vector.tensor_tensor(f2_lo[:, :, :], f2raw[:, :, :], f2_hi[:, :, :].bitcast(F32), ALU.subtract).then_inc(f2_ready, 1)
                    if i == 0 and more and b < 2:
                        dve.wait_ge(ld_f[b], 16 * KT * NQ * (g + 2))
                        ffn_transpose(2 * g + 2 + b, b)
                contribution(g, b)

            dve.sem_inc(up_used, 1)
            dve.sem_inc(contrib, TT)
            dve.sem_inc(hid_lo, 1)
            dve.wait_ge(ld_f[0], 16 * KT * NQ)
            nc.vector.transpose(ftr[:, :, :], fraw[0][:, :, :]).then_inc(f_tr, 1)
            dve.wait_ge(ld_f[1], 16 * KT * NQ)
            ffn_transpose(1, 1)
            dve.wait_ge(ld_gb, 16)
            with dve.Fori(0, NG - 2, 2) as g:
                for par in range(2):
                    for b in range(NB):
                        ffn(g + par, par, b, True)
            for par in range(2):
                for b in range(NB):
                    ffn(NG - 2 + par, par, b, par == 0)

        @block.gpsimd
        def _(pool):
            nc.gpsimd.memset(ident[:, :], 0.0).then_inc(pool_step, 1)
            nc.gpsimd.memset(mask[:, :], 1.0).then_inc(pool_step, 1)
            nc.gpsimd.memset(mhalf[:, :], -0.5).then_inc(const_ready, 1)
            pool.wait_ge(pool_step, 2)
            nc.gpsimd.affine_select(out=ident[:, :], in_=ident[:, :], compare_op=ALU.not_equal, fill=1.0,
                                    base=0, pattern=[[-1, P]], channel_multiplier=1).then_inc(const_ready, 1)
            head = mask[:, :].rearrange("p (a j) -> p a j", j=Q32)
            nc.gpsimd.affine_select(out=head, in_=head, compare_op=ALU.is_ge, fill=0.0,
                                    base=0, pattern=[[-Q32, NQ], [0, Q32]], channel_multiplier=1).then_inc(pool_step, 1)
            pool.wait_ge(pool_step, 3)
            nc.gpsimd.affine_select(out=head, in_=head, compare_op=ALU.is_ge, fill=0.0,
                                    base=Q32 - 1, pattern=[[Q32, NQ], [0, Q32]], channel_multiplier=-1).then_inc(mask_ready, 1)

            def rstd_of(n):
                pool.wait_ge(stat_step, 9 * (n + 1))
                if n == 0:
                    pool.wait_ge(const_ready, 2)
                else:
                    pool.wait_ge(xhat_ready, TT * n)
                nc.gpsimd.tensor_tensor(rstd[:, :], ve[:, :], mhalf[:, :], ALU.pow).then_inc(rstd_ready, 1)

            def to_lo(key):
                pool.wait_ge(split_hi, split_at[key] + 1)
                hi, lo = split_tile(key)
                nc.gpsimd.tensor_tensor(lo, val_tile(key), hi.bitcast(F32), ALU.subtract).then_inc(split_lo, 1)

            rstd_of(0)
            for kt in range(KT):
                to_lo(("h", 0, kt))
            pool.wait_ge(wm_used, 6)
            nc.gpsimd.memset(v_hi[:, :, :, P:HW].bitcast(F32), 1.0).then_inc(v_ones, 1)
            nc.gpsimd.memset(v_lo[:, :, :, P:HW].bitcast(F32), 0.0).then_inc(v_ones, 1)
            pool.wait_ge(ld_ob, 16)
            for b in range(NB + 1):
                if b < NB:
                    for t in range(TT):
                        to_lo(("k", b, t))
                    if b + 1 < NB:
                        rstd_of(b + 1)
                for t in range(TT):
                    if b < NB:
                        to_lo(("v", b, t))
                    if b >= 1:
                        to_lo(("a", b - 1, t))
                if b < NB:
                    for t in range(TT):
                        to_lo(("q", b, t))
                if b + 1 < NB:
                    for kt in range(KT):
                        to_lo(("h", b + 1, kt))
                if b >= 1:
                    pool.wait_ge(ld_ga[(b - 1) % 2], 16 * ((b - 1) // 2 + 1))
                    if b >= 2:
                        pool.wait_ge(xob_ready, TT * (b - 1))
                    nc.gpsimd.tensor_tensor(gaob[:, :], ga_bc[:, (b - 1) % 2, :], ob_bc[:, :], ALU.mult).then_inc(gaob_ready, 1)
                    pool.wait_ge(gaob_ready, b)
                    for t in range(TT):
                        n = ot_at[(b - 1, t)]
                        pool.wait_ge(ld_xt[t], 16 * b)
                        nc.gpsimd.tensor_tensor(xt[:, t, :], xt[:, t, :], gaob[:, :], ALU.add).then_inc(xob_ready, 1)
                        pool.wait_ge(xob_ready, n + 1)
                        pool.wait_ge(ot_ready, n + 1)
                        nc.gpsimd.tensor_tensor(xt[:, t, :], xt[:, t, :], ot[:, n % 2, :], ALU.add).then_inc(x1_ready, 1)
                if b < NB:
                    pool.wait_ge(st_hi_done, b + 1)
                    nc.gpsimd.tensor_tensor(st_lo[:, :, :], st32[:, :, :], st_hi[:, :, :].bitcast(F32), ALU.subtract).then_inc(st_split, 1)

            for b in range(NB):
                rstd_of(NB + b)
                for kt in range(KT):
                    to_lo(("h2", b, kt))

            def weight_lo(count, which, par):
                pool.wait_ge(f_hi, count)
                nc.gpsimd.tensor_tensor((f1_lo, f3_lo)[which][par][:, :, :], ftr[:, :, :],
                                        (f1_hi, f3_hi)[which][par][:, :, :].bitcast(F32), ALU.subtract).then_inc(f_lo, 1)

            def ffn(g, par, b, more):
                if more and b < 2:
                    weight_lo(2 * g + 3 + b, b, 1 - par)
                for t in range(TT):
                    m = (g * NB + b) * TT + t
                    pool.wait_ge(contrib, m + TT + 1)
                    xr = x1res[:, TT * b + t, :]
                    nc.gpsimd.tensor_tensor(xr, xr, ot[:, t % 2, :], ALU.add).then_inc(added, 1)

            pool.sem_inc(added, 2)
            weight_lo(1, 0, 0)
            weight_lo(2, 1, 0)
            with pool.Fori(0, NG - 2, 2) as g:
                for par in range(2):
                    for b in range(NB):
                        ffn(g + par, par, b, True)
            for par in range(2):
                for b in range(NB):
                    ffn(NG - 2 + par, par, b, par == 0)


_INS = ['L0_attn_hidden_states', 'L0_attn_q_w', 'L0_attn_q_b', 'L0_attn_k_w', 'L0_attn_k_b', 'L0_attn_v_w', 'L0_attn_v_b',
        'L0_attn_o_w', 'L0_attn_o_b', 'L0_ffn_W1', 'L0_ffn_W2', 'L0_ffn_W3', 'L0_c', 'L0_wmod']


def kernel(**inputs):
    import numpy as _np
    import concourse.bacc as _bacc
    from concourse import mybir as _mybir
    from concourse.bass_utils import run_bass_kernel_spmd as _run

    nc = _bacc.Bacc("TRN2", target_bir_lowering=False, num_devices=1, dynamic_dma_scratch_size=1024)
    arrays, args = {}, []
    for name in _INS:
        a = _np.ascontiguousarray(inputs[name])
        arrays[f"in_{name}_dram"] = a
        args.append(nc.dram_tensor(f"in_{name}_dram", a.shape, _mybir.dt.from_np(a.dtype), kind="ExternalInput").ap())
    o = nc.dram_tensor("out_dram", arrays["in_L0_attn_hidden_states_dram"].shape, _mybir.dt.float32, kind="ExternalOutput").ap()
    build(nc, *args, o)
    r = _run(nc, [arrays], core_ids=[0])
    return r.results[0]["out_dram"]
```

```python
from contextlib import ExitStack

import concourse.bass as bass
from concourse import mybir

F32 = mybir.dt.float32
F32R = mybir.dt.float32r
ACT = mybir.ActivationFunctionType
ALU = mybir.AluOpType

P = 128
Q32 = 32
NB, S, D, HID = 4, 512, 512, 2048
KT = D // P
TT = S // P
EPS_LN = 1e-5
EPS_Z = 1e-6
NQ = P // Q32
HW = P + 2
NBLK = HID // P
DC = 64
NCH = D // DC
GH = 256
NG = HID // GH
GB = GH // P
G_MIN = 0.25
NH = D // Q32
GHD = NH // KT


def build(nc, x, q_w, q_b, k_w, k_b, v_w, v_b, o_w, o_b, W1, W2, W3, c, wmod, out):
    x1_dram = nc.dram_tensor("x1_scratch", [NB, S, D], F32, kind="Internal").ap()
    g_dram = nc.dram_tensor("g_scratch", [NB, 2, D], F32, kind="Internal").ap()
    w2t_dram = nc.dram_tensor("w2_hadamard_scratch", [NBLK, P, D], F32, kind="Internal").ap()

    ctx = ExitStack()
    with ctx:
        sem = lambda n: ctx.enter_context(nc.semaphore(n))

        top = [2048]

        def region(nbytes):
            at = top[0]
            top[0] = at + (nbytes + 31) // 32 * 32
            return at

        def put(name, shape, dt, at):
            return nc.alloc_sbuf_tensor_at(name, shape, dt, offset=at)

        def new(name, shape, dt=F32):
            n = 4
            for s in shape[1:]:
                n *= s
            return put(name, shape, dt, region(n))

        TILE = D * 4
        r_w = [region(2 * KT * TILE) for _ in range(4)]
        KW, VW, QW, OW = range(4)
        w_hi = [put(f"w_hi{i}", [P, KT, D], F32R, r_w[i]) for i in range(4)]
        w_lo = [put(f"w_lo{i}", [P, KT, D], F32R, r_w[i] + KT * TILE) for i in range(4)]
        r_h2 = [r_w[VW], r_w[QW], r_w[KW], r_w[OW]]
        h2_hi = [put(f"h2_hi{i}", [P, KT, S], F32R, r_h2[i]) for i in range(NB)]
        h2_lo = [put(f"h2_lo{i}", [P, KT, S], F32R, r_h2[i] + KT * TILE) for i in range(NB)]
        r_h = region(2 * KT * TILE)
        h_hi = put("h_hi", [P, KT, S], F32R, r_h)
        h_lo = put("h_lo", [P, KT, S], F32R, r_h + KT * TILE)
        r_xa = region(TT * TILE)
        xa = put("xa", [P, TT, D], F32, r_xa)
        r_xt = region(TT * TILE)
        xt = put("xt", [P, TT, D], F32, r_xt)
        wmx = put("wmx", [P, KT, D], F32, r_xt)
        r_kv = region(2 * TT * TILE + 2 * TT * KT * HW * 4)
        kp_hi = put("kp_hi", [P, TT, D], F32R, r_kv)
        kp_lo = put("kp_lo", [P, TT, D], F32R, r_kv + TT * TILE)
        r_v = r_kv + 2 * TT * TILE
        v_hi = put("v_hi", [P, TT, KT, HW], F32R, r_v)
        v_lo = put("v_lo", [P, TT, KT, HW], F32R, r_v + TT * KT * HW * 4)
        wm = [put(f"wm{i}", [P, KT, D], F32, r_kv + i * KT * TILE) for i in range(2)]
        x1res = [put(f"x1res{b}", [P, TT, D], F32, r_kv + b * TT * TILE) for b in range(NB)]
        atz_hi = put("atz_hi", [P, KT, S], F32R, r_kv + 2 * TT * TILE)
        atz_lo = put("atz_lo", [P, KT, S], F32R, r_kv + 3 * TT * TILE)
        r_q = region(2 * KT * TILE)
        qp_hi = put("qp_hi", [P, KT, S], F32R, r_q)
        qp_lo = put("qp_lo", [P, KT, S], F32R, r_q + KT * TILE)
        raw1 = put("raw1", [P, KT, D], F32, r_q)
        r_a = region(2 * KT * TILE)
        at_hi = put("at_hi", [P, KT, S], F32R, r_a)
        at_lo = put("at_lo", [P, KT, S], F32R, r_a + KT * TILE)
        raw0 = put("raw0", [P, KT, D], F32, r_a)
        wtr = put("wtr", [P, KT, D], F32, r_a + KT * TILE)
        SW = KT * (P + NH)
        r_s = region(max(3 * SW * 4 + P * 4, NB * TILE))
        st32 = put("st32", [P, SW], F32, r_s)
        st_hi = put("st_hi", [P, SW], F32R, r_s + SW * 4)
        st_lo = put("st_lo", [P, SW], F32R, r_s + 2 * SW * 4)
        gb_bc = put("gb_bc", [P, NB, D], F32, r_s)
        r_lin = region(2 * TILE)
        lin = put("lin", [P, 2, D], F32, r_lin)
        r_neg = region(2 * TILE)
        neg = put("neg", [P, 2, D], F32, r_neg)
        val = new("val", [P, 3, D])
        r_ot = region(2 * TILE)
        ot = put("ot", [P, 2, D], F32, r_ot)
        gr = put("gr", [NB, 2, D], F32, r_ot)
        ga_bc = new("ga_bc", [P, 2, D])
        r_bias = region(3 * TILE)
        kb_bc = put("kb_bc", [P, D], F32, r_bias)
        vb_bc = put("vb_bc", [P, D], F32, r_bias + TILE)
        ob_bc = put("ob_bc", [P, D], F32, r_bias + 2 * TILE)
        r_go = region(TILE)
        gaob = put("gaob", [P, D], F32, r_go)
        gs = put("gs", [NB, D], F32, r_go)
        r_c = region(4 * NBLK * DC * 4)
        CB = NBLK * DC * 4
        c_raw = put("c_raw", [P, NBLK, DC], F32, r_c)
        c_tr = put("c_tr", [P, NBLK, DC], F32, r_c + CB)
        c_hi = put("c_hi", [P, NBLK, DC], F32R, r_c + 2 * CB)
        c_lo = put("c_lo", [P, NBLK, DC], F32R, r_c + 3 * CB)
        c_pp = put("c_pp", [P, NBLK, DC], F32, r_c + 3 * CB)
        ident = new("ident", [P, P])
        mask = put("mask", [P, P], F32, r_s + 3 * SW * 4)
        had_r = new("had_r", [P, P], F32R)
        inv_hi = new("inv_hi", [NH, S], F32R)
        r_inv = region(TILE)
        inv32 = put("inv32", [NH, S], F32, r_inv)
        inv_lo = put("inv_lo", [NH, S], F32R, r_inv)
        spread_r = new("spread_r", [NH, KT, P], F32R)
        spread32 = put("spread32", [NH, KT, P], F32, r_c)
        cs = put("cs", [NB, D], F32, r_neg)
        qb_row = put("qb_row", [KT, P], F32, r_lin)
        hada = put("hada", [P, P], F32, r_c + 2 * CB)
        hadb = put("hadb", [P, P], F32, r_c + 3 * CB)
        cT = new("cT", [P, KT * NB])
        modc = new("modc", [P, 4, KT, NB])
        qb_col = new("qb_col", [P, KT])
        qb_neg = new("qb_neg", [P, KT])
        mhalf = new("mhalf", [P, TT])
        stats = new("stats", [P, TT, 6])
        mv = new("mv", [P, TT, 2])
        ve = new("ve", [P, TT])
        rstd = new("rstd", [P, TT])

        FW = KT * GH * 4
        r_slot = [r_h, r_q]
        f1_hi = [put(f"f1_hi{i}", [P, KT, GH], F32R, r_slot[i]) for i in range(2)]
        f1_lo = [put(f"f1_lo{i}", [P, KT, GH], F32R, r_slot[i] + FW) for i in range(2)]
        f3_hi = [put(f"f3_hi{i}", [P, KT, GH], F32R, r_slot[i] + 2 * FW) for i in range(2)]
        f3_lo = [put(f"f3_lo{i}", [P, KT, GH], F32R, r_slot[i] + 3 * FW) for i in range(2)]
        f2_hi = put("f2_hi", [P, GB, D], F32R, r_a)
        f2_lo = put("f2_lo", [P, GB, D], F32R, r_a + GB * TILE)
        hd_hi = put("hd_hi", [P, GB, S], F32R, r_a + 2 * GB * TILE)
        hd_lo = put("hd_lo", [P, GB, S], F32R, r_a + 3 * GB * TILE)
        fraw = [put(f"fraw{i}", [P, KT, GH], F32, r_xa + i * FW) for i in range(2)]
        r_xh2 = [r_w[KW], r_w[KW] + KT * TILE, r_w[OW], r_c]
        xh2 = [put(f"xh2_{b}", [P, TT, D], F32, r_xh2[b]) for b in range(NB)]
        f2raw = put("f2raw", [P, GB, D], F32, r_c + 2 * CB)
        ftr = put("ftr", [P, KT, GH], F32, r_lin)
        gate32 = put("gate32", [P, S], F32, r_neg)
        hid32 = put("hid32", [P, S], F32, r_neg + TILE)
        assert top[0] <= nc.sbuf_usable_end, (top[0], nc.sbuf_usable_end)

        bank = [ctx.enter_context(nc.psum_tensor(f"bank{i}", [P, 512], F32)) for i in range(8)]
        pj = bank[0:2]
        tr = bank[2:4]
        kvb = bank[4:6]
        zb, ab = bank[6], bank[7]
        gate_ps, up_ps = pj
        out_ps = bank[4:8]

        ld_c, ld_qb, ld_kb, ld_vb, ld_ob = (sem(f"ld_{n}") for n in ("c", "qb", "kb", "vb", "ob"))
        ld_xa = sem("ld_xa")
        ld_wm = [sem(f"ld_wm{i}") for i in range(4)]
        ld_wmx = sem("ld_wmx")
        ld_raw = [[sem(f"ld_raw{i}_{k}") for k in range(KT)] for i in range(2)]
        ld_chunk = sem("ld_chunk")
        ld_xt = [sem(f"ld_xt{i}") for i in range(TT)]
        ld_ga = [sem(f"ld_ga{i}") for i in range(2)]
        st_g, st_chunk, st_x1 = sem("st_g"), sem("st_chunk"), [sem(f"st_x1_{t}") for t in range(TT)]
        const_ready = sem("const_ready")
        had_step, v_ones = sem("had_step"), sem("v_ones")
        mask_ready = sem("mask_ready")
        cT_ps_ready, cT_ready = sem("cT_ps_ready"), sem("cT_ready")
        mod_ps, mod_ready, g_step, wm_used = sem("mod_ps"), sem("mod_ready"), sem("g_step"), sem("wm_used")
        wmx_used = sem("wmx_used")
        w_tr, w_hi_done, w_ready = sem("w_tr"), sem("w_hi_done"), sem("w_ready")
        stat_step, rstd_ready, xhat_ready = sem("stat_step"), sem("rstd_ready"), sem("xhat_ready")
        pool_step = sem("pool_step")
        tr_full, val_act, chunk_evac = sem("tr_full"), sem("val_act"), sem("chunk_evac")
        pj_full, k_lin, q_lin, relu_ready, exp_ready = sem("pj_full"), sem("k_lin"), sem("q_lin"), sem("relu_ready"), sem("exp_ready")
        v_hi_done, v_lo_done = sem("v_hi_done"), sem("v_lo_done")
        val_dve, split_hi, split_lo = sem("val_dve"), sem("split_hi"), sem("split_lo")
        kv_full, st_step, st_ready, st_hi_done, st_split = sem("kv_full"), sem("st_step"), sem("st_ready"), sem("st_hi_done"), sem("st_split")
        z_full, ze_ready, inv_ready, inv_hi_done, inv_split = (sem(n) for n in ("z_full", "ze_ready", "inv_ready", "inv_hi_done", "inv_split"))
        spread_step, inv_out = sem("spread_step"), sem("inv_out")
        att_full, spread_ready, ksum_zero = sem("att_full"), sem("spread_ready"), sem("ksum_zero")
        ot_ready, gaob_ready, xob_ready, x1_ready = sem("ot_ready"), sem("gaob_ready"), sem("xob_ready"), sem("x1_ready")
        chunk_tr, chunk_hi, chunk_lo, chunk_step = sem("chunk_tr"), sem("chunk_hi"), sem("chunk_lo"), sem("chunk_step")
        ld_xh2, ld_gb, ld_x1 = sem("ld_xh2"), sem("ld_gb"), [sem(f"ld_x1_{b}") for b in range(NB)]
        ld_f = [sem("ld_f1"), sem("ld_f3")]
        ld_f2 = sem("ld_f2")
        f_tr, f_hi, f_lo = sem("f_tr"), sem("f_hi"), sem("f_lo")
        f2_hi_done, f2_ready = sem("f2_hi_done"), sem("f2_ready")
        gate_full, up_full, gate_used, up_used = sem("gate_full"), sem("up_full"), sem("gate_used"), sem("up_used")
        hid_hi, hid_lo = sem("hid_hi"), sem("hid_lo")
        out_full, contrib, added = sem("out_full"), sem("contrib"), sem("added")
        st_out = sem("st_out")

        pj_at, tr_at, split_at, exp_at, dve_at, act_at, ot_at = {}, {}, {}, {}, {}, {}, {}

        def use(where, key):
            where[key] = len(where)

        def use_split(key, by):
            use(split_at, key)
            use(by, key)

        for kt in range(KT):
            use(tr_at, ("h", 0, kt))
            use_split(("h", 0, kt), act_at)
        for b in range(NB):
            for t in range(TT):
                use(pj_at, ("k", b, t))
                use(exp_at, ("k", b, t))
                if t >= 1:
                    use_split(("k", b, t - 1), dve_at)
                if t == 0 and b >= 1:
                    for i in range(2):
                        use(tr_at, ("chunk", 2 * b - 1, i))
            if b >= 1:
                use_split(("a", b - 1, 0), dve_at)
            use_split(("k", b, TT - 1), dve_at)
            for t in range(TT):
                use(pj_at, ("v", b, t))
                if t >= 1 and b >= 1:
                    use_split(("a", b - 1, t), dve_at)
            for t in range(TT):
                use(pj_at, ("q", b, t))
                use(exp_at, ("q", b, t))
                use_split(("q", b, t), dve_at)
            for i in range(2):
                use(tr_at, ("chunk", 2 * b, i))
            for kt in range(KT):
                key = ("h", b + 1, kt) if b + 1 < NB else ("h2", 0, kt)
                use(tr_at, key)
                use_split(key, act_at)
            if b >= 1:
                for t in range(TT):
                    use(pj_at, ("o", b - 1, t))
                    use(ot_at, (b - 1, t))
        for g in range(KT):
            use_split(("a", NB - 1, g), dve_at)
        for i in range(2):
            use(tr_at, ("chunk", NCH - 1, i))
        for t in range(TT):
            use(pj_at, ("o", NB - 1, t))
            use(ot_at, (NB - 1, t))
        for b in range(1, NB):
            for kt in range(KT):
                use(tr_at, ("h2", b, kt))
                use_split(("h2", b, kt), act_at)
        pj_order, tr_order, exp_order = list(pj_at), list(tr_at), list(exp_at)
        raw_of = {KW: raw0, VW: raw1, QW: raw0, OW: raw0}
        raw_slot = {KW: (0, 1), VW: (1, 1), QW: (0, 2), OW: (0, 3)}
        w_dram = {KW: k_w, VW: v_w, QW: q_w, OW: o_w}

        def at_of(b):
            return (atz_hi, atz_lo) if b == NB - 1 else (at_hi, at_lo)

        def split_tile(key):
            kind, b, t = key
            if kind == "k":
                return kp_hi[:, t, :], kp_lo[:, t, :]
            if kind == "q":
                return qp_hi[:, t, :], qp_lo[:, t, :]
            if kind == "a":
                return at_of(b)[0][:, t, :], at_of(b)[1][:, t, :]
            if kind == "h":
                return h_hi[:, t, :], h_lo[:, t, :]
            return h2_hi[b][:, t, :], h2_lo[b][:, t, :]

        def banks_in_flight(b):
            return 2 if b == NB - 1 else 1

        def att_banks(b, g):
            return (kvb[0], kvb[1]) if g % banks_in_flight(b) else (zb, ab)

        def val_tile(key):
            return val[:, split_at[key] % 3, :]

        def blocks_of(w_ap, q, kt):
            k0 = P * kt + Q32 * q
            return w_ap[:, k0:k0 + Q32].rearrange("(v j) i -> j v i", j=Q32)

        def blocks_at(tile, q, kt):
            return tile[Q32 * q:Q32 * q + Q32, kt, :].rearrange("j (v i) -> j v i", i=Q32)

        def butterfly(eng, n, s, u):
            if s == 0:
                eng.wait_ge(chunk_evac, 2 * n + 2)
            else:
                eng.wait_ge(chunk_step, 8 * n + 2 * s)
            src, dst = (c_tr, c_pp) if s % 2 == 0 else (c_pp, c_tr)
            a = src[:, :, :].rearrange("p (n u h) d -> p n u (h d)", u=2, h=1 << s)
            o = dst[:, :, :].rearrange("p (n u h) d -> p n u (h d)", u=2, h=1 << s)
            eng.tensor_tensor(o[:, :, u, :], a[:, :, 0, :], a[:, :, 1, :], (ALU.add, ALU.subtract)[u]).then_inc(chunk_step, 1)

        block = ctx.enter_context(nc.Block())

        @block.sync
        def _(sp):
            def load_weight(i):
                n, _ = raw_slot[i]
                for kt in range(KT):
                    for q in range(NQ):
                        sp.dma_start(blocks_at(raw_of[i], q, kt), blocks_of(w_dram[i], q, kt)).then_inc(ld_raw[n][kt], 16)

            def wmod_of(section):
                return wmod[:, section * D:(section + 1) * D].rearrange("(k p) n -> p k n", p=P)

            def load_xa(b):
                sp.dma_start(xa[:, :, :], x[b, :, :].rearrange("(t p) d -> p t d", p=P)).then_inc(ld_xa, 16)

            def load_chunk(n):
                if n >= 1:
                    sp.wait_ge(chunk_tr, n)
                for q in range(NQ):
                    for v in range(DC // Q32):
                        r0 = n * DC + v * Q32
                        src = W2[r0:r0 + Q32, :].rearrange("j (k a i) -> j k a i", a=NQ, i=Q32)[:, :, q, :]
                        dst = c_raw[Q32 * q:Q32 * q + Q32, :, v * Q32:(v + 1) * Q32]
                        sp.dma_start(dst, src).then_inc(ld_chunk, 16)

            def store_chunk(n):
                sp.wait_ge(chunk_step, 8 * (n + 1))
                sp.dma_start(w2t_dram[:, :, n * DC:(n + 1) * DC].rearrange("b p d -> p b d"), c_tr[:, :, :]).then_inc(st_chunk, 16)

            def load_xt(b):
                for t in range(TT):
                    if b >= 1:
                        sp.wait_ge(st_x1[t], 16 * b)
                    sp.dma_start(xt[:, t, :], x[b, t * P:(t + 1) * P, :]).then_inc(ld_xt[t], 16)

            def store_x1(b):
                for t in range(TT):
                    sp.wait_ge(x1_ready, TT * b + t + 1)
                    sp.dma_start(x1_dram[b, t * P:(t + 1) * P, :], xt[:, t, :]).then_inc(st_x1[t], 16)

            def x1_of(b):
                return x1_dram[b, :, :].rearrange("(t p) d -> p t d", p=P)

            def load_ga(b):
                if b >= 2:
                    sp.wait_ge(x1_ready, TT * (b - 1))
                sp.dma_start(ga_bc[:, b % 2, :], g_dram[b, 0, :].partition_broadcast(P)).then_inc(ld_ga[b % 2], 16)

            def load_f(m, w_ap):
                for kt in range(KT):
                    for q in range(NQ):
                        sp.dma_start(blocks_at(fraw[m], q, kt), blocks_of(w_ap, q, kt)).then_inc(ld_f[m], 16)

            def load_f_group(g):
                sp.wait_ge(f_tr, 2 * g - 1)
                load_f(0, W1[bass.ds(g * GH, GH), :])
                sp.wait_ge(f_tr, 2 * g)
                load_f(1, W3[bass.ds(g * GH, GH), :])

            def load_f2(g):
                sp.dma_start(f2raw[:, :, :], w2t_dram[bass.ds(g * GB, GB), :, :].rearrange("b p d -> p b d")).then_inc(ld_f2, 16)

            sp.dma_start(cs[:, :], c).then_inc(ld_c, 16)
            sp.dma_start(qb_row[:, :], q_b.rearrange("(g p) -> g p", p=P)).then_inc(ld_qb, 16)
            for i in range(2):
                sp.dma_start(wm[i][:, :, :], wmod_of(i)).then_inc(ld_wm[i], 16)
            load_xa(0)
            load_weight(KW)
            sp.dma_start(kb_bc[:, :], k_b.partition_broadcast(P)).then_inc(ld_kb, 16)
            load_weight(VW)
            sp.dma_start(vb_bc[:, :], v_b.partition_broadcast(P)).then_inc(ld_vb, 16)
            sp.dma_start(ob_bc[:, :], o_b.partition_broadcast(P)).then_inc(ld_ob, 16)
            sp.dma_start(wmx[:, :, :], wmod_of(2)).then_inc(ld_wmx, 16)
            sp.wait_ge(w_tr, KT)
            load_weight(QW)
            sp.wait_ge(tr_full, tr_at[("h", 0, KT - 1)] + 1)
            load_xa(1)
            sp.wait_ge(spread_ready, 1)
            load_chunk(0)
            sp.wait_ge(wmx_used, 1)
            sp.dma_start(wmx[:, :, :], wmod_of(5)).then_inc(ld_wmx, 16)
            load_chunk(1)
            sp.wait_ge(wmx_used, 2)
            sp.dma_start(wmx[:, :, :], wmod_of(3)).then_inc(ld_wmx, 16)
            sp.wait_ge(w_tr, 3 * KT)
            load_weight(OW)
            sp.wait_ge(wmx_used, 3)
            sp.dma_start(wmx[:, :, :], wmod_of(4)).then_inc(ld_wmx, 16)
            sp.wait_ge(g_step, 10)
            sp.dma_start(g_dram, gr[:, :, :]).then_inc(st_g, 16)
            sp.wait_ge(st_g, 16)
            load_ga(0)
            load_ga(1)
            for b in range(NB):
                if b >= 1:
                    store_chunk(2 * b - 1)
                    load_chunk(2 * b + 1)
                if b >= 2:
                    load_ga(b)
                store_chunk(2 * b)
                if b == NB - 1:
                    sp.wait_ge(kv_full, 2 * NB)
                    for i in range(2):
                        sp.dma_start(x1res[i][:, :, :], x1_of(i)).then_inc(ld_x1[i], 16)
                if b + 2 < NB:
                    sp.wait_ge(tr_full, tr_at[("h", b + 1, KT - 1)] + 1)
                    load_xa(b + 2)
                if b + 1 < NB:
                    load_chunk(2 * b + 2)
                if b >= 1:
                    store_x1(b - 1)
                else:
                    sp.wait_ge(wmx_used, 4)
                load_xt(b)
                if b == NB - 2:
                    sp.wait_ge(tr_full, tr_at[("h", NB - 1, KT - 1)] + 1)
                    load_f(0, W1[0:GH, :])
                    load_f(1, W3[0:GH, :])
                    sp.wait_ge(pj_full, pj_at[("k", NB - 1, TT - 1)] + 1)
                    sp.dma_start(xh2[0][:, :, :], x1_of(0)).then_inc(ld_xh2, 16)
            sp.wait_ge(att_full, NB * KT)
            sp.dma_start(gb_bc[:, :, :], g_dram[:, 1, :].partition_broadcast(P)).then_inc(ld_gb, 16)
            store_chunk(NCH - 1)
            sp.wait_ge(st_chunk, 16 * NCH)
            load_f2(0)
            sp.wait_ge(pj_full, len(pj_at))
            sp.dma_start(x1res[2][:, :, :], x1_of(2)).then_inc(ld_x1[2], 16)
            store_x1(NB - 1)
            load_f_group(1)
            for t in range(TT):
                sp.wait_ge(st_x1[t], 16 * NB)
            sp.dma_start(x1res[3][:, :, :], x1_of(3)).then_inc(ld_x1[3], 16)
            sp.wait_ge(f2_ready, 1)
            load_f2(1)
            with sp.Fori(2, NG) as g:
                load_f_group(g)
                sp.wait_ge(f2_ready, g)
                load_f2(g)
            for b in range(NB):
                for t in range(TT):
                    m = (NG - 1) * NB * TT + TT * b + t
                    sp.wait_ge(added, m + 1 + 2)
                    sp.dma_start(out[b, t * P:(t + 1) * P, :], x1res[b][:, t, :]).then_inc(st_out, 16)
            sp.wait_ge(st_out, 16 * NB * TT)

        @block.tensor
        def _(pe):
            def three(o, l_hi, l_lo, r_hi, r_lo, first, last):
                nc.tensor.matmul(o, l_hi, r_hi, start=first, stop=False)
                nc.tensor.matmul(o, l_hi, r_lo, start=False, stop=False)
                return nc.tensor.matmul(o, l_lo, r_hi, start=False, stop=last)

            def wait_pj(key):
                n = pj_at[key]
                if n < 2:
                    pe.wait_ge(mod_ready, 2)
                    return
                kind, b, t = pj_order[n - 2]
                if kind == "v":
                    pe.wait_ge(v_lo_done, TT * b + t + 1)
                elif kind == "o":
                    pe.wait_ge(ot_ready, ot_at[(b, t)] + 1)
                elif kind == "k":
                    pe.wait_ge(k_lin, TT * b + t + 1)
                else:
                    pe.wait_ge(relu_ready, exp_at[(kind, b, t)] + 1)

            def wait_tr(key):
                n = tr_at[key]
                if n < 2:
                    return
                old = tr_order[n - 2]
                if old[0] == "chunk":
                    pe.wait_ge(chunk_evac, 2 * old[1] + old[2] + 1)
                else:
                    pe.wait_ge(val_act, act_at[old] + 1)

            def transposes(kind, b, src, kts=range(KT)):
                n = b + (NB if kind == "h2" else 0)
                pe.wait_ge(xhat_ready, TT * n + TT)
                for kt in kts:
                    key = (kind, b, kt)
                    wait_tr(key)
                    for t in range(TT):
                        mm = nc.tensor.transpose(tr[tr_at[key] % 2][:, t * P:(t + 1) * P], src[:, t, kt * P:(kt + 1) * P], ident[:, :])
                    mm.then_inc(tr_full, 1)

            def project_tile(kind, b, t):
                key = (kind, b, t)
                wait_pj(key)
                o = pj[pj_at[key] % 2][:, :]
                w = {"k": KW, "v": VW, "q": QW, "o": OW}[kind]
                a_hi, a_lo = at_of(b) if kind == "o" else (h_hi, h_lo)
                for kt in range(KT):
                    if kind == "o" and t == 0:
                        pe.wait_ge(split_lo, split_at[("a", b, kt)] + 1)
                    ts = slice(t * P, (t + 1) * P)
                    if kind == "q":
                        mm = three(o, w_hi[w][:, kt, ts], w_lo[w][:, kt, ts], a_hi[:, kt, :], a_lo[:, kt, :], kt == 0, kt == KT - 1)
                    else:
                        mm = three(o, a_hi[:, kt, ts], a_lo[:, kt, ts], w_hi[w][:, kt, :], w_lo[w][:, kt, :], kt == 0, kt == KT - 1)
                mm.then_inc(pj_full, 1)

            def normaliser(b):
                pe.wait_ge(st_split, b + 1)
                pe.wait_ge(split_lo, split_at[("q", b, KT - 1)] + 1)
                if b == 0:
                    pe.wait_ge(mod_ready, 4)
                    pe.wait_ge(g_step, 7)
                else:
                    pe.wait_ge(val_dve, dve_at[("a", b - 1, KT - 1)] + 1)
                for g in range(KT):
                    cols = slice(KT * P + g * NH, KT * P + (g + 1) * NH)
                    mm = three(zb[0:NH, :], st_hi[:, cols], st_lo[:, cols], qp_hi[:, g, :], qp_lo[:, g, :], g == 0, g == KT - 1)
                mm.then_inc(z_full, 1)

            def attend(b, g):
                if g == 0:
                    pe.wait_ge(inv_split, b + 1)
                    pe.wait_ge(spread_ready, 1)
                in_flight = banks_in_flight(b)
                if g >= in_flight:
                    pe.wait_ge(val_dve, dve_at[("a", b, g - in_flight)] + 1)
                zi, o = att_banks(b, g)
                nc.tensor.matmul(zi[:, :], spread_r[:, g, :], inv_hi[:, :], start=True, stop=False)
                nc.tensor.matmul(zi[:, :], spread_r[:, g, :], inv_lo[:, :], start=False, stop=True)
                cols = slice(g * P, (g + 1) * P)
                three(o[:, :], st_hi[:, cols], st_lo[:, cols], qp_hi[:, g, :], qp_lo[:, g, :], True, True).then_inc(att_full, 1)

            def key_values(b):
                pe.wait_ge(split_lo, split_at[("k", b, TT - 1)] + 1)
                pe.wait_ge(v_lo_done, TT * (b + 1))
                if b >= 1:
                    pe.wait_ge(st_step, 2 * KT * b)
                else:
                    pe.wait_ge(v_ones, 2)
                for g in range(KT):
                    o = kvb[g // 2][:, (g % 2) * HW:(g % 2 + 1) * HW]
                    ds_ = slice(g * P, (g + 1) * P)
                    for t in range(TT):
                        mm = three(o, kp_hi[:, t, ds_], kp_lo[:, t, ds_], v_hi[:, t, g, :], v_lo[:, t, g, :], t == 0, t == TT - 1)
                    if g % 2:
                        mm.then_inc(kv_full, 1)

            def hadamard(n):
                pe.wait_ge(chunk_lo, n + 1)
                for i in range(2):
                    key = ("chunk", n, i)
                    wait_tr(key)
                    o = tr[tr_at[key] % 2][:, :]
                    bs = slice(i * NBLK // 2, (i + 1) * NBLK // 2)
                    nc.tensor.matmul(o, had_r[:, :], c_hi[:, bs, :], start=True, stop=False)
                    nc.tensor.matmul(o, had_r[:, :], c_lo[:, bs, :], start=False, stop=True).then_inc(tr_full, 1)

            def mod_columns(w, o, s):
                for m in range(KT):
                    for k in range(KT):
                        mm = nc.tensor.matmul(o[:, (s * KT + m) * NB:(s * KT + m + 1) * NB], w[:, k, m * P:(m + 1) * P],
                                              cT[:, k * NB:(k + 1) * NB], start=(k == 0), stop=(k == KT - 1))
                return mm

            def mod_rows(o):
                for k in range(KT):
                    mm = nc.tensor.matmul(o[0:NB, :], cT[:, k * NB:(k + 1) * NB], wmx[:, k, :], start=(k == 0), stop=(k == KT - 1))
                return mm

            pe.wait_ge(const_ready, 2)
            pe.wait_ge(ld_c, 16)
            for kt in range(KT):
                nc.tensor.transpose(bank[4][:, kt * NB:(kt + 1) * NB], cs[:, kt * P:(kt + 1) * P], ident[0:NB, 0:NB])
            pe.wait_ge(ld_qb, 16)
            nc.tensor.transpose(bank[4][:, KT * NB:KT * NB + KT], qb_row[:, :], ident[0:KT, 0:KT]).then_inc(cT_ps_ready, 1)
            pe.wait_ge(cT_ready, 1)
            for i in range(2):
                pe.wait_ge(ld_wm[i], 16)
                mod_columns(wm[i], pj[0], i).then_inc(wm_used, 1)
            transposes("h", 0, xa)

            for b in range(NB):
                pe.wait_ge(split_lo, split_at[("h", b, KT - 1)] + 1)
                for t in range(TT):
                    if b == 0 and t == 0:
                        pe.wait_ge(w_ready, KT * (KW + 1))
                    project_tile("k", b, t)
                    if t == 0 and b >= 1:
                        normaliser(b - 1)
                        hadamard(2 * b - 1)
                if b >= 1:
                    attend(b - 1, 0)
                if b == 0:
                    pe.wait_ge(ld_wmx, 16)
                    mod_rows(zb).then_inc(wmx_used, 1)
                    pe.wait_ge(w_ready, KT * (VW + 1))
                for t in range(TT):
                    project_tile("v", b, t)
                    if t < TT - 1 and b >= 1:
                        attend(b - 1, t + 1)
                    if b == 0 and t == 1:
                        pe.wait_ge(ld_wmx, 32)
                        mod_rows(ab).then_inc(wmx_used, 1)
                if b == 0:
                    pe.wait_ge(had_step, 14)
                    pe.wait_ge(w_ready, KT * (QW + 1))
                for t in range(2):
                    project_tile("q", b, t)
                hadamard(2 * b)
                if b == 0:
                    pe.wait_ge(ld_wmx, 48)
                    pe.wait_ge(g_step, 2)
                    mod_columns(wmx, zb, 0).then_inc(wmx_used, 1)
                key_values(b)
                for t in range(2, TT):
                    project_tile("q", b, t)
                if b + 1 < NB:
                    transposes("h", b + 1, xa)
                else:
                    transposes("h2", 0, xh2[0])
                if b == 0:
                    pe.wait_ge(ld_wmx, 64)
                    pe.wait_ge(g_step, 7)
                    mod_columns(wmx, ab, 0).then_inc(wmx_used, 1)
                if b >= 1:
                    pe.wait_ge(w_ready, KT * (OW + 1))
                if b == NB - 1:
                    normaliser(b)
                for t in range(TT):
                    if b == NB - 1 and t == TT - 1:
                        attend(b, 0)
                    if b >= 1:
                        project_tile("o", b - 1, t)
            for g in range(1, KT):
                attend(NB - 1, g)
            hadamard(NCH - 1)
            for t in range(TT):
                project_tile("o", NB - 1, t)

            pe.wait_ge(ot_ready, NB * TT)

            def ffn(g, par, b):
                n = (g * NB + b) * GB
                first = isinstance(g, int) and g == 0
                if first:
                    pe.wait_ge(split_lo, split_at[("h2", b, KT - 1)] + 1)
                if b == 0:
                    pe.wait_ge(f_lo, 2 * g + 2)
                for i in range(GB):
                    hs = slice(i * P, (i + 1) * P)
                    for o, f_h, f_l, used, full in ((gate_ps, f1_hi, f1_lo, gate_used, gate_full), (up_ps, f3_hi, f3_lo, up_used, up_full)):
                        pe.wait_ge(used, n + i + 1)
                        for kt in range(KT):
                            mm = three(o[:, :], f_h[par][:, kt, hs], f_l[par][:, kt, hs], h2_hi[b][:, kt, :], h2_lo[b][:, kt, :], kt == 0, kt == KT - 1)
                        mm.then_inc(full, 1)
                    if first and b + 1 < NB:
                        transposes("h2", b + 1, xh2[b + 1], range(i * KT // GB, (i + 1) * KT // GB))
                if b == 0:
                    pe.wait_ge(f2_ready, g + 1)
                for i in range(GB):
                    pe.wait_ge(hid_lo, n + i + 2)
                    for t in range(TT):
                        if i == 0:
                            pe.wait_ge(contrib, (g * NB + b) * TT + t + 1)
                        ts = slice(t * P, (t + 1) * P)
                        mm = three(out_ps[t][:, :], hd_hi[:, i, ts], hd_lo[:, i, ts], f2_hi[:, i, :], f2_lo[:, i, :], i == 0, i == GB - 1)
                        if i == GB - 1:
                            mm.then_inc(out_full, 1)

            for b in range(NB):
                ffn(0, 0, b)
            with pe.Fori(1, NG - 1, 2) as g:
                for par in (1, 0):
                    for b in range(NB):
                        ffn(g + (1 - par), par, b)
            for b in range(NB):
                ffn(NG - 1, 1, b)

        @block.scalar
        def _(act):
            def to_hi(key):
                if key in dve_at:
                    act.wait_ge(val_dve, dve_at[key] + 1)
                else:
                    act.wait_ge(val_act, act_at[key] + 1)
                nc.scalar.activation(split_tile(key)[0], val_tile(key), ACT.Copy).then_inc(split_hi, 1)

            def modulate(kind, b, kts=range(KT)):
                s = 0 if kind == "h" else 2
                for kt in kts:
                    key = (kind, b, kt)
                    act.wait_ge(tr_full, tr_at[key] + 1)
                    if split_at[key] >= 3:
                        act.wait_ge(split_lo, split_at[key] - 2)
                    nc.scalar.activation(val_tile(key), tr[tr_at[key] % 2][:, :], ACT.Identity,
                                         bias=modc[:, s, kt, b:b + 1], scale=modc[:, s + 1, kt, b:b + 1]).then_inc(val_act, 1)
                    to_hi(key)

            def feature_exp(key):
                kind, b, t = key
                e = exp_at[key]
                s = e % 2
                if kind == "k":
                    act.wait_ge(k_lin, TT * b + t + 1)
                    nc.scalar.activation(neg[:, s, :], lin[:, s, :], ACT.Relu, scale=-1.0).then_inc(relu_ready, 1)
                else:
                    ps = pj[pj_at[key] % 2][:, :]
                    act.wait_ge(val_dve, dve_at[exp_order[e - 2]] + 1)
                    act.wait_ge(pj_full, pj_at[key] + 1)
                    nc.scalar.activation(lin[:, s, :], ps, ACT.Identity, bias=qb_col[:, t:t + 1]).then_inc(q_lin, 1)
                    nc.scalar.activation(neg[:, s, :], ps, ACT.Relu, bias=qb_neg[:, t:t + 1], scale=-1.0).then_inc(relu_ready, 1)
                act.wait_ge(relu_ready, e + 1)
                nc.scalar.activation(neg[:, s, :], neg[:, s, :], ACT.Exp, scale=-1.0).then_inc(exp_ready, 1)

            def value_hi(b, t):
                key = ("v", b, t)
                act.wait_ge(pj_full, pj_at[key] + 1)
                nc.scalar.activation(v_hi[:, t, :, 0:P], pj[pj_at[key] % 2][:, :].rearrange("p (g e) -> p g e", g=KT),
                                     ACT.Copy).then_inc(v_hi_done, 1)

            def normaliser_epsilon(b):
                act.wait_ge(z_full, b + 1)
                nc.scalar.activation(zb[0:NH, :], zb[0:NH, :], ACT.Copy, bias=EPS_Z).then_inc(ze_ready, 1)

            def inverse_out(b, g):
                key = ("a", b, g)
                act.wait_ge(att_full, KT * b + g + 1)
                act.wait_ge(split_lo, split_at[key] - 2)
                nc.scalar.activation(val_tile(key), att_banks(b, g)[0][:, :], ACT.Copy).then_inc(inv_out, 1)

            def inverse_hi(b):
                act.wait_ge(inv_ready, b + 1)
                if b >= 1:
                    act.wait_ge(att_full, KT * b)
                nc.scalar.activation(inv_hi[:, :], inv32[:, :], ACT.Copy).then_inc(inv_hi_done, 1)

            def chunk_to_hi(n):
                act.wait_ge(chunk_tr, n + 1)
                nc.scalar.activation(c_hi[:, :, :], c_tr[:, :, :], ACT.Copy).then_inc(chunk_hi, 1)

            def chunk_out(n):
                for i in range(2):
                    key = ("chunk", n, i)
                    act.wait_ge(tr_full, tr_at[key] + 1)
                    nc.scalar.activation(c_tr[:, i * NBLK // 2:(i + 1) * NBLK // 2, :],
                                         tr[tr_at[key] % 2][:, :].rearrange("p (b d) -> p b d", d=DC),
                                         ACT.Copy, scale=float(HID) ** -0.5).then_inc(chunk_evac, 1)

            def weight_to_hi(i, kt):
                act.wait_ge(w_tr, KT * i + kt + 1)
                nc.scalar.activation(w_hi[i][:, kt, :], wtr[:, kt, :], ACT.Copy).then_inc(w_hi_done, 1)

            def ffn_weight_hi(count, which, par):
                act.wait_ge(f_tr, count)
                nc.scalar.activation((f1_hi, f3_hi)[which][par][:, :, :], ftr[:, :, :], ACT.Copy).then_inc(f_hi, 1)

            act.wait_ge(cT_ps_ready, 1)
            qb_ps = bank[4][:, KT * NB:KT * NB + KT]
            nc.scalar.activation(qb_col[:, :], qb_ps, ACT.Copy)
            nc.scalar.activation(qb_neg[:, :], qb_ps, ACT.Copy, scale=-1.0)
            nc.scalar.activation(cT[:, :], bank[4][:, 0:KT * NB], ACT.Silu).then_inc(cT_ready, 1)
            act.wait_ge(cT_ready, 1)
            for kt in range(2):
                weight_to_hi(KW, kt)
            act.wait_ge(mod_ready, 2)
            modulate("h", 0)
            for kt in range(2, KT):
                weight_to_hi(KW, kt)
            for b in range(NB):
                for t in range(TT):
                    if t == 1 and b >= 1:
                        inverse_hi(b - 1)
                    feature_exp(("k", b, t))
                    if b == 0:
                        weight_to_hi(VW, t)
                    if t == 0 and b >= 1:
                        normaliser_epsilon(b - 1)
                        chunk_out(2 * b - 1)
                    if t >= 1:
                        to_hi(("k", b, t - 1))
                if b >= 1:
                    inverse_out(b - 1, 0)
                for t in range(TT):
                    if b >= 1:
                        to_hi(("a", b - 1, t))
                    if t == 0:
                        to_hi(("k", b, TT - 1))
                    value_hi(b, t)
                    if b >= 1 and t < TT - 1:
                        inverse_out(b - 1, t + 1)
                    if b == 0:
                        weight_to_hi(QW, t)
                    if t == 3:
                        chunk_to_hi(2 * b)
                for t in range(TT):
                    if t == 2:
                        chunk_out(2 * b)
                    feature_exp(("q", b, t))
                    if b == 0:
                        weight_to_hi(OW, t)
                    if t >= 1:
                        to_hi(("q", b, t - 1))
                    if t == 2:
                        act.wait_ge(st_ready, KT * (b + 1))
                        nc.scalar.activation(st_hi[:, :], st32[:, :], ACT.Copy).then_inc(st_hi_done, 1)
                to_hi(("q", b, TT - 1))
                if b + 1 < NB:
                    modulate("h", b + 1)
                    chunk_to_hi(2 * b + 1)
            act.wait_ge(mod_ready, 4)
            modulate("h2", 0)
            normaliser_epsilon(NB - 1)
            inverse_hi(NB - 1)
            ffn_weight_hi(1, 0, 0)
            chunk_to_hi(NCH - 1)
            inverse_out(NB - 1, 0)
            for g in range(KT):
                if g + 1 < KT:
                    inverse_out(NB - 1, g + 1)
                to_hi(("a", NB - 1, g))
            chunk_out(NCH - 1)
            ffn_weight_hi(2, 1, 0)

            def ffn(g, par, b, more):
                first = isinstance(g, int) and g == 0
                wb = 1 if first else 0
                n = (g * NB + b) * GB
                for i in range(GB):
                    act.wait_ge(gate_full, n + i + 1)
                    act.wait_ge(up_used, n + i + 1)
                    nc.scalar.activation(gate32[:, :], gate_ps[:, :], ACT.Silu).then_inc(gate_used, 1)
                    if b == 0 and i == (1 if first else 0):
                        act.wait_ge(ld_f2, 16 * g + 16)
                        nc.scalar.activation(f2_hi[:, :, :], f2raw[:, :, :], ACT.Copy).then_inc(f2_hi_done, 1)
                    act.wait_ge(up_used, n + i + 2)
                    nc.scalar.activation(hd_hi[:, i, :], hid32[:, :], ACT.Copy).then_inc(hid_hi, 1)
                    if i == 0 and more and wb <= b < wb + 2:
                        ffn_weight_hi(2 * g + 3 + b - wb, b - wb, 1 - par)
                    if first and b + 1 < NB:
                        modulate("h2", b + 1, range(i * KT // GB, (i + 1) * KT // GB))

            act.sem_inc(gate_used, 1)
            for b in range(NB):
                ffn(0, 0, b, True)
            with act.Fori(1, NG - 1, 2) as g:
                for par in (1, 0):
                    for b in range(NB):
                        ffn(g + (1 - par), par, b, True)
            for b in range(NB):
                ffn(NG - 1, 1, b, False)

        @block.vector
        def _(dve):
            def statistics(n, src):
                if n < NB:
                    dve.wait_ge(ld_xa, 16 * (n + 1))
                elif n == NB:
                    dve.wait_ge(ld_xh2, 16)
                else:
                    dve.wait_ge(ld_x1[n - NB], 16)
                if n >= 1:
                    dve.wait_ge(stat_step, 9 * n)
                for t in range(TT):
                    nc.vector.bn_stats(stats[:, t, :], src[:, t, :]).then_inc(stat_step, 1)

            def mean_variance(n):
                if n >= 1:
                    dve.wait_ge(xhat_ready, TT * n)
                for t in range(TT):
                    dve.wait_ge(stat_step, 9 * n + t + 1)
                    nc.vector.bn_aggr(mv[:, t, :], stats[:, t, :]).then_inc(stat_step, 1)
                dve.wait_ge(stat_step, 9 * n + 8)
                nc.vector.tensor_scalar(ve[:, :], mv[:, :, 1], EPS_LN, None, ALU.add).then_inc(stat_step, 1)

            def normalise(n, t, dst, src):
                dve.wait_ge(rstd_ready, n + 1)
                nc.vector.tensor_scalar(dst[:, t, :], src[:, t, :], mv[:, t, 0:1], rstd[:, t:t + 1],
                                        ALU.subtract, ALU.mult).then_inc(xhat_ready, 1)

            def weight_transpose(i, kt):
                n, loads = raw_slot[i]
                dve.wait_ge(ld_raw[n][kt], 16 * NQ * loads)
                if i >= 1:
                    dve.wait_ge(w_ready, KT * (i - 1) + kt + 1)
                nc.vector.transpose(wtr[:, kt, :], raw_of[i][:, kt, :]).then_inc(w_tr, 1)

            def weight_to_lo(i, kt):
                dve.wait_ge(w_hi_done, KT * i + kt + 1)
                nc.vector.tensor_tensor(w_lo[i][:, kt, :], wtr[:, kt, :], w_hi[i][:, kt, :].bitcast(F32), ALU.subtract).then_inc(w_ready, 1)

            def chunk_transpose(n):
                dve.wait_ge(ld_chunk, 16 * NQ * (DC // Q32) * (n + 1))
                if n >= 1:
                    dve.wait_ge(st_chunk, 16 * n)
                nc.vector.transpose(c_tr[:, :, :], c_raw[:, :, :]).then_inc(chunk_tr, 1)

            def chunk_to_lo(n):
                dve.wait_ge(chunk_hi, n + 1)
                if n >= 1:
                    dve.wait_ge(chunk_step, 8 * n)
                nc.vector.tensor_tensor(c_lo[:, :, :], c_tr[:, :, :], c_hi[:, :, :].bitcast(F32), ALU.subtract).then_inc(chunk_lo, 1)

            def k_bias(b, t):
                key = ("k", b, t)
                e = exp_at[key]
                if e >= 2:
                    dve.wait_ge(val_dve, dve_at[exp_order[e - 2]] + 1)
                dve.wait_ge(pj_full, pj_at[key] + 1)
                nc.vector.tensor_tensor(lin[:, e % 2, :], pj[pj_at[key] % 2][:, :], kb_bc[:, :], ALU.add).then_inc(k_lin, 1)

            def wait_val(key):
                if split_at[key] >= 3:
                    dve.wait_ge(split_lo, split_at[key] - 2)

            def feature(key):
                e = exp_at[key]
                dve.wait_ge(exp_ready, e + 1)
                wait_val(key)
                nc.vector.scalar_tensor_tensor(val_tile(key), lin[:, e % 2, :], 0.0, neg[:, e % 2, :],
                                               ALU.max, ALU.add).then_inc(val_dve, 1)

            def value_lo(b, t):
                key = ("v", b, t)
                dve.wait_ge(v_hi_done, TT * b + t + 1)
                nc.vector.tensor_tensor(v_lo[:, t, :, 0:P], pj[pj_at[key] % 2][:, :].rearrange("p (g e) -> p g e", g=KT),
                                        v_hi[:, t, :, 0:P].bitcast(F32), ALU.subtract).then_inc(v_lo_done, 1)

            def inverse(b):
                dve.wait_ge(ze_ready, b + 1)
                if b >= 1:
                    dve.wait_ge(att_full, KT * b)
                nc.vector.reciprocal(inv32[:, :], zb[0:NH, :]).then_inc(inv_ready, 1)

            def inverse_lo(b):
                dve.wait_ge(inv_hi_done, b + 1)
                nc.vector.tensor_tensor(inv_lo[:, :], inv32[:, :], inv_hi[:, :].bitcast(F32), ALU.subtract).then_inc(inv_split, 1)

            def attention(b, g):
                key = ("a", b, g)
                dve.wait_ge(inv_out, KT * b + g + 1)
                nc.vector.tensor_tensor(val_tile(key), att_banks(b, g)[1][:, :], val_tile(key), ALU.mult).then_inc(val_dve, 1)

            def key_value_state(b):
                if b >= 1:
                    dve.wait_ge(st_split, b)
                    dve.wait_ge(st_ready, KT * b)
                else:
                    dve.wait_ge(ksum_zero, 1)
                for g in range(KT):
                    if g % 2 == 0:
                        dve.wait_ge(kv_full, 2 * b + g // 2 + 1)
                    ps = kvb[g // 2][:, (g % 2) * HW:(g % 2 + 1) * HW]
                    state = st32[:, g * P:(g + 1) * P]
                    nc.vector.scalar_tensor_tensor(state, vb_bc[:, g * P:(g + 1) * P], ps[:, P:P + 1], ps[:, 0:P],
                                                   ALU.mult, ALU.add).then_inc(st_step, 1)
                    k0 = KT * P + g * NH + g * GHD
                    nc.vector.tensor_scalar(st32[:, k0:k0 + GHD], mask[:, 0:P:Q32], ps[:, P:P + 1], None, ALU.mult).then_inc(st_step, 1)
                for g in range(KT):
                    dve.wait_ge(st_step, 2 * KT * b + 2 * g + 1)
                    state = st32[:, g * P:(g + 1) * P]
                    nc.vector.tensor_tensor(state, state, mask[:, :], ALU.mult).then_inc(st_ready, 1)

            def residual(b, t):
                key = ("o", b, t)
                n = ot_at[(b, t)]
                if t == 0:
                    dve.wait_ge(ld_ga[b % 2], 16 * (b // 2 + 1))
                dve.wait_ge(pj_full, pj_at[key] + 1)
                if n >= 2:
                    dve.wait_ge(x1_ready, n - 1)
                nc.vector.tensor_tensor(ot[:, n % 2, :], pj[pj_at[key] % 2][:, :], ga_bc[:, b % 2, :], ALU.mult).then_inc(ot_ready, 1)

            def gate(i, ps, done):
                if i:
                    dve.wait_ge(g_step, 5)
                nc.vector.tensor_scalar(gs[:, :], ps, 0.0, 2.0, ALU.is_ge, ALU.mult).then_inc(g_step, 1)
                nc.vector.tensor_copy(gr[:, i, :], ps).then_inc(g_step, 1)
                dve.wait_ge(g_step, done + 1)
                nc.vector.tensor_scalar(gs[:, :], gs[:, :], -1.0, None, ALU.add).then_inc(g_step, 1)
                dve.wait_ge(g_step, done + 2)
                nc.vector.scalar_tensor_tensor(gr[:, i, :], gr[:, i, :], -1.0, gr[:, i, :], ALU.mult, ALU.max).then_inc(g_step, 1)
                dve.wait_ge(g_step, done + 4)
                nc.vector.scalar_tensor_tensor(gr[:, i, :], gr[:, i, :], G_MIN, gs[:, :], ALU.max, ALU.mult).then_inc(g_step, 1)

            def modulation(s, ps, plus):
                ps = ps[:, 0:KT * NB].rearrange("p (k b) -> p k b", b=NB)
                if plus:
                    nc.vector.tensor_scalar(modc[:, s, :, :], ps, plus, None, ALU.add).then_inc(mod_ready, 1)
                else:
                    nc.vector.tensor_copy(modc[:, s, :, :], ps).then_inc(mod_ready, 1)

            def ffn_transpose(count, which):
                if not (isinstance(count, int) and count == 0):
                    dve.wait_ge(f_lo, count)
                nc.vector.transpose(ftr[:, :, :], fraw[which][:, :, :]).then_inc(f_tr, 1)

            dve.wait_ge(const_ready, 2)
            src = ident
            for s in range(7):
                dst = had_r if s == 6 else (hada, hadb)[s % 2]
                if s >= 1:
                    dve.wait_ge(had_step, 2 * s)
                a = src[:, :].rearrange("p (n u h) -> p n u h", u=2, h=1 << s)
                o = dst[:, :].rearrange("p (n u h) -> p n u h", u=2, h=1 << s)
                for u, op in ((0, ALU.add), (1, ALU.subtract)):
                    nc.vector.tensor_tensor(o[:, :, u, :], a[:, :, 0, :], a[:, :, 1, :], op).then_inc(had_step, 1)
                src = dst
            statistics(0, xa)
            mean_variance(0)
            for t in range(TT):
                normalise(0, t, xa, xa)
            for kt in range(KT):
                if kt == 2:
                    dve.wait_ge(wm_used, 2)
                    modulation(0, pj[0][:, :], 0.0)
                    modulation(1, pj[0][:, KT * NB:2 * KT * NB], 1.0)
                weight_transpose(KW, kt)
                if kt >= 1:
                    weight_to_lo(KW, kt - 1)
            weight_to_lo(KW, KT - 1)
            dve.wait_ge(ld_kb, 16)
            dve.wait_ge(ld_vb, 16)
            dve.wait_ge(mask_ready, 1)
            for b in range(NB):
                for t in range(TT):
                    k_bias(b, t)
                    if t >= 1:
                        feature(("k", b, t - 1))
                    if b == 0:
                        weight_transpose(VW, t)
                        if t >= 1:
                            weight_to_lo(VW, t - 1)
                    elif t == 0:
                        inverse(b - 1)
                    else:
                        if t == 1:
                            inverse_lo(b - 1)
                        butterfly(dve, 2 * b - 1, t - 1, 0)
                if b == 0:
                    weight_to_lo(VW, TT - 1)
                    dve.wait_ge(wmx_used, 1)
                    gate(0, zb[0:NB, :], 0)
                else:
                    attention(b - 1, 0)
                feature(("k", b, TT - 1))
                for t in range(TT):
                    value_lo(b, t)
                    if b == 0:
                        weight_transpose(QW, t)
                    else:
                        if t == 0:
                            butterfly(dve, 2 * b - 1, 3, 0)
                        if t < TT - 1:
                            attention(b - 1, t + 1)
                    if t == 2:
                        chunk_transpose(2 * b)
                        if b == 0:
                            dve.wait_ge(wmx_used, 2)
                            gate(1, ab[0:NB, :], 5)
                n = b + 1
                ln_src = xa if n < NB else xh2[0]
                for t in range(TT):
                    if t >= 1:
                        feature(("q", b, t - 1))
                    if t == 0:
                        chunk_to_lo(2 * b)
                        statistics(n, ln_src)
                    if t == 1:
                        mean_variance(n)
                    if t == 2:
                        if b == 0:
                            dve.wait_ge(wmx_used, 3)
                            modulation(2, zb[:, :], 0.0)
                        key_value_state(b)
                        for u in range(TT):
                            normalise(n, u, ln_src, ln_src)
                    if t >= 2:
                        butterfly(dve, 2 * b, t - 2, 0)
                        butterfly(dve, 2 * b, t - 2, 1)
                    if b == 0:
                        weight_transpose(OW, t)
                feature(("q", b, TT - 1))
                for s in (2, 3):
                    butterfly(dve, 2 * b, s, 0)
                    butterfly(dve, 2 * b, s, 1)
                if b == 0:
                    dve.wait_ge(wmx_used, 4)
                    modulation(3, ab[:, :], 1.0)
                    dve.wait_ge(st_g, 16)
                if b == NB - 1:
                    inverse(b)
                for t in range(TT):
                    if b >= 1:
                        residual(b - 1, t)
                    if t == 0 and b == NB - 1:
                        inverse_lo(b)
                        dve.wait_ge(ld_f[0], 16 * KT * NQ)
                        dve.wait_ge(val_dve, dve_at[("q", b, TT - 1)] + 1)
                        ffn_transpose(0, 0)
                    if t == 1:
                        chunk_transpose(2 * b + 1)
                    if t == 2:
                        chunk_to_lo(2 * b + 1)
                    if t >= 2 and b == NB - 1:
                        attention(b, t - 2)
            for g in range(2, KT):
                attention(NB - 1, g)
            dve.wait_ge(ld_f[1], 16 * KT * NQ)
            ffn_transpose(1, 1)
            for t in range(TT):
                residual(NB - 1, t)
                butterfly(dve, NCH - 1, t, 0)

            dve.sem_inc(up_used, 1)
            dve.sem_inc(contrib, TT)
            dve.sem_inc(hid_lo, 1)

            def second_norm(b):
                statistics(NB + b, x1res[b])
                mean_variance(NB + b)
                if b == NB - 1:
                    dve.wait_ge(st_chunk, 16 * NCH)
                for t in range(TT):
                    normalise(NB + b, t, xh2[b], x1res[b])

            second_norm(1)

            def contribution(g, b):
                for t in range(TT):
                    m = (g * NB + b) * TT + t
                    dve.wait_ge(out_full, m + 1)
                    dve.wait_ge(added, m + 1)
                    nc.vector.tensor_tensor(ot[:, t % 2, :], out_ps[t][:, :], gb_bc[:, b, :], ALU.mult).then_inc(contrib, 1)

            def ffn(g, par, b, more):
                n = (g * NB + b) * GB
                first = isinstance(g, int) and g == 0
                wb = 1 if first else 0
                for i in range(GB):
                    dve.wait_ge(hid_lo, n + i + 1)
                    dve.wait_ge(gate_used, n + i + 2)
                    dve.wait_ge(up_full, n + i + 1)
                    nc.vector.tensor_tensor(hid32[:, :], up_ps[:, :], gate32[:, :], ALU.mult).then_inc(up_used, 1)
                    dve.wait_ge(hid_hi, n + i + 1)
                    nc.vector.tensor_tensor(hd_lo[:, i, :], hid32[:, :], hd_hi[:, i, :].bitcast(F32), ALU.subtract).then_inc(hid_lo, 1)
                    if b == 0 and i == (1 if first else 0):
                        dve.wait_ge(f2_hi_done, g + 1)
                        nc.vector.tensor_tensor(f2_lo[:, :, :], f2raw[:, :, :], f2_hi[:, :, :].bitcast(F32), ALU.subtract).then_inc(f2_ready, 1)
                    if i == 0 and more and wb <= b < wb + 2:
                        dve.wait_ge(ld_f[b - wb], 16 * KT * NQ * (g + 2))
                        ffn_transpose(2 * g + 2 + b - wb, b - wb)
                    if i == 1 and first and b + 2 < NB:
                        second_norm(b + 2)
                contribution(g, b)

            dve.wait_ge(ld_gb, 16)
            for b in range(NB):
                ffn(0, 0, b, True)
            with dve.Fori(1, NG - 1, 2) as g:
                for par in (1, 0):
                    for b in range(NB):
                        ffn(g + (1 - par), par, b, True)
            for b in range(NB):
                ffn(NG - 1, 1, b, False)

        @block.gpsimd
        def _(pool):
            nc.gpsimd.memset(ident[:, :], 0.0).then_inc(pool_step, 1)
            nc.gpsimd.memset(mask[:, :], 1.0).then_inc(pool_step, 1)
            nc.gpsimd.memset(mhalf[:, :], -0.5).then_inc(const_ready, 1)
            pool.wait_ge(pool_step, 2)
            nc.gpsimd.affine_select(out=ident[:, :], in_=ident[:, :], compare_op=ALU.not_equal, fill=1.0,
                                    base=0, pattern=[[-1, P]], channel_multiplier=1).then_inc(const_ready, 1)
            heads = mask[:, :].rearrange("p (a j) -> p a j", j=Q32)
            nc.gpsimd.affine_select(out=heads, in_=heads, compare_op=ALU.is_ge, fill=0.0,
                                    base=0, pattern=[[-Q32, NQ], [0, Q32]], channel_multiplier=1).then_inc(pool_step, 1)
            pool.wait_ge(pool_step, 3)
            nc.gpsimd.affine_select(out=heads, in_=heads, compare_op=ALU.is_ge, fill=0.0,
                                    base=Q32 - 1, pattern=[[Q32, NQ], [0, Q32]], channel_multiplier=-1).then_inc(mask_ready, 1)

            nc.gpsimd.memset(spread32[:, :, :], 1.0).then_inc(spread_step, 1)
            for n, (base, sign) in enumerate(((0, 1), (Q32 - 1, -1))):
                pool.wait_ge(spread_step, n + 1)
                nc.gpsimd.affine_select(out=spread32[:, :, :], in_=spread32[:, :, :], compare_op=ALU.is_ge, fill=0.0,
                                        base=base, pattern=[[sign * P, KT], [sign, P]], channel_multiplier=-sign * Q32).then_inc(spread_step, 1)
            pool.wait_ge(spread_step, 3)
            nc.gpsimd.tensor_copy(spread_r[:, :, :], spread32[:, :, :]).then_inc(spread_ready, 1)
            nc.gpsimd.memset(st32[:, KT * P:], 0.0).then_inc(ksum_zero, 1)

            def ffn_weight_lo(count, which, par):
                pool.wait_ge(f_hi, count)
                nc.gpsimd.tensor_tensor((f1_lo, f3_lo)[which][par][:, :, :], ftr[:, :, :],
                                        (f1_hi, f3_hi)[which][par][:, :, :].bitcast(F32), ALU.subtract).then_inc(f_lo, 1)

            def rstd_of(n):
                pool.wait_ge(stat_step, 9 * (n + 1))
                if n == 0:
                    pool.wait_ge(const_ready, 2)
                else:
                    pool.wait_ge(xhat_ready, TT * n)
                nc.gpsimd.tensor_tensor(rstd[:, :], ve[:, :], mhalf[:, :], ALU.pow).then_inc(rstd_ready, 1)

            def to_lo(key):
                pool.wait_ge(split_hi, split_at[key] + 1)
                hi, lo = split_tile(key)
                nc.gpsimd.tensor_tensor(lo, val_tile(key), hi.bitcast(F32), ALU.subtract).then_inc(split_lo, 1)

            def weight_to_lo(i, kt):
                pool.wait_ge(w_hi_done, KT * i + kt + 1)
                nc.gpsimd.tensor_tensor(w_lo[i][:, kt, :], wtr[:, kt, :], w_hi[i][:, kt, :].bitcast(F32), ALU.subtract).then_inc(w_ready, 1)

            def output_bias(b):
                pool.wait_ge(ld_ga[b % 2], 16 * (b // 2 + 1))
                if b >= 1:
                    pool.wait_ge(xob_ready, TT * b)
                nc.gpsimd.tensor_tensor(gaob[:, :], ga_bc[:, b % 2, :], ob_bc[:, :], ALU.mult).then_inc(gaob_ready, 1)
                pool.wait_ge(gaob_ready, b + 1)

            def add_residual(b, t):
                n = ot_at[(b, t)]
                pool.wait_ge(ld_xt[t], 16 * (b + 1))
                nc.gpsimd.tensor_tensor(xt[:, t, :], xt[:, t, :], gaob[:, :], ALU.add).then_inc(xob_ready, 1)
                pool.wait_ge(xob_ready, n + 1)
                pool.wait_ge(ot_ready, n + 1)
                nc.gpsimd.tensor_tensor(xt[:, t, :], xt[:, t, :], ot[:, n % 2, :], ALU.add).then_inc(x1_ready, 1)

            rstd_of(0)
            for kt in range(KT):
                to_lo(("h", 0, kt))
            pool.wait_ge(wm_used, 2)
            nc.gpsimd.memset(v_hi[:, :, :, P:HW].bitcast(F32), 1.0).then_inc(v_ones, 1)
            nc.gpsimd.memset(v_lo[:, :, :, P:HW].bitcast(F32), 0.0).then_inc(v_ones, 1)
            pool.wait_ge(ld_ob, 16)
            for b in range(NB):
                for t in range(TT):
                    if t >= 1:
                        if b >= 1:
                            butterfly(pool, 2 * b - 1, t - 1, 1)
                        to_lo(("k", b, t - 1))
                for t in range(TT):
                    if b >= 1:
                        to_lo(("a", b - 1, t))
                    if t == 0:
                        to_lo(("k", b, TT - 1))
                        if b >= 1:
                            butterfly(pool, 2 * b - 1, 3, 1)
                    if b == 0:
                        weight_to_lo(QW, t)
                for t in range(TT):
                    if t == 1:
                        rstd_of(b + 1)
                    if t >= 1:
                        to_lo(("q", b, t - 1))
                    if t == 2:
                        pool.wait_ge(st_hi_done, b + 1)
                        nc.gpsimd.tensor_tensor(st_lo[:, :], st32[:, :], st_hi[:, :].bitcast(F32), ALU.subtract).then_inc(st_split, 1)
                    if b == 0:
                        weight_to_lo(OW, t)
                to_lo(("q", b, TT - 1))
                for kt in range(KT):
                    to_lo(("h", b + 1, kt) if b + 1 < NB else ("h2", 0, kt))
                if b >= 1:
                    output_bias(b - 1)
                for t in range(TT):
                    if b >= 1:
                        add_residual(b - 1, t)
                    if b == NB - 1 and t == 0:
                        ffn_weight_lo(1, 0, 0)
            for g in range(KT):
                to_lo(("a", NB - 1, g))
            ffn_weight_lo(2, 1, 0)
            output_bias(NB - 1)
            for t in range(TT):
                add_residual(NB - 1, t)
                butterfly(pool, NCH - 1, t, 1)
            rstd_of(NB + 1)

            def ffn(g, par, b, more):
                first = isinstance(g, int) and g == 0
                wb = 1 if first else 0
                if first:
                    pool.wait_ge(ld_x1[b], 16)
                if more and wb <= b < wb + 2:
                    ffn_weight_lo(2 * g + 3 + b - wb, b - wb, 1 - par)
                if isinstance(g, int) and g == 0 and b + 1 < NB:
                    for kt in range(KT):
                        to_lo(("h2", b + 1, kt))
                    if b + 2 < NB:
                        rstd_of(NB + b + 2)
                for t in range(TT):
                    m = (g * NB + b) * TT + t
                    pool.wait_ge(contrib, m + TT + 1)
                    xr = x1res[b][:, t, :]
                    nc.gpsimd.tensor_tensor(xr, xr, ot[:, t % 2, :], ALU.add).then_inc(added, 1)

            pool.sem_inc(added, 2)
            for b in range(NB):
                ffn(0, 0, b, True)
            with pool.Fori(1, NG - 1, 2) as g:
                for par in (1, 0):
                    for b in range(NB):
                        ffn(g + (1 - par), par, b, True)
            for b in range(NB):
                ffn(NG - 1, 1, b, False)


_INS = ['L0_attn_hidden_states', 'L0_attn_q_w', 'L0_attn_q_b', 'L0_attn_k_w', 'L0_attn_k_b', 'L0_attn_v_w', 'L0_attn_v_b',
        'L0_attn_o_w', 'L0_attn_o_b', 'L0_ffn_W1', 'L0_ffn_W2', 'L0_ffn_W3', 'L0_c', 'L0_wmod']


def kernel(**inputs):
    import numpy as _np
    import concourse.bacc as _bacc
    from concourse import mybir as _mybir
    from concourse.bass_utils import run_bass_kernel_spmd as _run

    nc = _bacc.Bacc("TRN2", target_bir_lowering=False, num_devices=1, dynamic_dma_scratch_size=1024)
    arrays, args = {}, []
    for name in _INS:
        a = _np.ascontiguousarray(inputs[name])
        arrays[f"in_{name}_dram"] = a
        args.append(nc.dram_tensor(f"in_{name}_dram", a.shape, _mybir.dt.from_np(a.dtype), kind="ExternalInput").ap())
    o = nc.dram_tensor("out_dram", arrays["in_L0_attn_hidden_states_dram"].shape, _mybir.dt.float32, kind="ExternalOutput").ap()
    build(nc, *args, o)
    r = _run(nc, [arrays], core_ids=[0])
    return r.results[0]["out_dram"]
```

```python
from contextlib import ExitStack

import concourse.bass as bass
from concourse import mybir

F32 = mybir.dt.float32
F32R = mybir.dt.float32r
ACT = mybir.ActivationFunctionType
ALU = mybir.AluOpType

P = 128
Q32 = 32
NB, S, D, HID = 4, 512, 512, 2048
KT = D // P
TT = S // P
EPS_LN = 1e-5
EPS_Z = 1e-6
NQ = P // Q32
HW = P + 2
VG = HW + P
NBLK = HID // P
DC = 64
NCH = D // DC
GH = 256
NG = HID // GH
GB = GH // P
G_MIN = 0.25
NH = D // Q32
GHD = NH // KT


def build(nc, x, q_w, q_b, k_w, k_b, v_w, v_b, o_w, o_b, W1, W2, W3, c, wmod, out):
    x1_dram = nc.dram_tensor("x1_scratch", [NB, S, D], F32, kind="Internal").ap()
    g_dram = nc.dram_tensor("g_scratch", [NB, 2, D], F32, kind="Internal").ap()
    w2t_dram = nc.dram_tensor("w2_hadamard_scratch", [NBLK, P, D], F32, kind="Internal").ap()

    ctx = ExitStack()
    with ctx:
        sem = lambda n: ctx.enter_context(nc.semaphore(n))

        top = [2048]

        def region(nbytes):
            at = top[0]
            top[0] = at + (nbytes + 31) // 32 * 32
            return at

        def put(name, shape, dt, at):
            return nc.alloc_sbuf_tensor_at(name, shape, dt, offset=at)

        def new(name, shape, dt=F32):
            n = 4
            for s in shape[1:]:
                n *= s
            return put(name, shape, dt, region(n))

        TILE = D * 4
        r_w = [region(2 * KT * TILE) for _ in range(4)]
        KW, VW, QW, OW = range(4)
        w_hi = [put(f"w_hi{i}", [P, KT, D], F32R, r_w[i]) for i in range(4)]
        w_lo = [put(f"w_lo{i}", [P, KT, D], F32R, r_w[i] + KT * TILE) for i in range(4)]
        r_h2 = [r_w[VW], r_w[QW], r_w[KW], r_w[OW]]
        h2_hi = [put(f"h2_hi{i}", [P, KT, S], F32R, r_h2[i]) for i in range(NB)]
        h2_lo = [put(f"h2_lo{i}", [P, KT, S], F32R, r_h2[i] + KT * TILE) for i in range(NB)]
        r_h = region(2 * KT * TILE)
        h_hi = put("h_hi", [P, KT, S], F32R, r_h)
        h_lo = put("h_lo", [P, KT, S], F32R, r_h + KT * TILE)
        r_xa = region(TT * TILE)
        xa = put("xa", [P, TT, D], F32, r_xa)
        r_xt = region(TT * TILE)
        xt = put("xt", [P, TT, D], F32, r_xt)
        wmx = put("wmx", [P, KT, D], F32, r_xt)
        r_kv = region(2 * TT * TILE + TT * KT * VG * 4)
        kp_hi = put("kp_hi", [P, TT, D], F32R, r_kv)
        kp_lo = put("kp_lo", [P, TT, D], F32R, r_kv + TT * TILE)
        r_v = r_kv + 2 * TT * TILE
        v = put("v", [P, TT, KT, VG], F32R, r_v)
        wm = [put(f"wm{i}", [P, KT, D], F32, r_kv + i * KT * TILE) for i in range(2)]
        x1res = [put(f"x1res{b}", [P, TT, D], F32, r_kv + b * TT * TILE) for b in range(NB)]
        atz_hi = put("atz_hi", [P, KT, S], F32R, r_kv + 2 * TT * TILE)
        atz_lo = put("atz_lo", [P, KT, S], F32R, r_kv + 3 * TT * TILE)
        r_q = region(2 * KT * TILE)
        qp_hi = put("qp_hi", [P, KT, S], F32R, r_q)
        qp_lo = put("qp_lo", [P, KT, S], F32R, r_q + KT * TILE)
        raw1 = put("raw1", [P, KT, D], F32, r_q)
        r_a = region(2 * KT * TILE)
        at_hi = put("at_hi", [P, KT, S], F32R, r_a)
        at_lo = put("at_lo", [P, KT, S], F32R, r_a + KT * TILE)
        raw0 = put("raw0", [P, KT, D], F32, r_a)
        wtr = put("wtr", [P, KT, D], F32, r_a + KT * TILE)
        SW = KT * (P + NH)
        r_s = region(max(3 * SW * 4 + P * 4, NB * TILE))
        st32 = put("st32", [P, SW], F32, r_s)
        st_hi = put("st_hi", [P, SW], F32R, r_s + SW * 4)
        st_lo = put("st_lo", [P, SW], F32R, r_s + 2 * SW * 4)
        gb_bc = put("gb_bc", [P, NB, D], F32, r_s)
        r_lin = region(2 * TILE)
        lin = put("lin", [P, 2, D], F32, r_lin)
        r_neg = region(2 * TILE)
        neg = put("neg", [P, 2, D], F32, r_neg)
        val = new("val", [P, 3, D])
        r_ot = region(2 * TILE)
        ot = put("ot", [P, 2, D], F32, r_ot)
        gr = put("gr", [NB, 2, D], F32, r_ot)
        ga_bc = new("ga_bc", [P, 2, D])
        r_bias = region(3 * TILE)
        kb_bc = put("kb_bc", [P, D], F32, r_bias)
        vb_bc = put("vb_bc", [P, D], F32, r_bias + TILE)
        ob_bc = put("ob_bc", [P, D], F32, r_bias + 2 * TILE)
        r_go = region(TILE)
        gaob = put("gaob", [P, D], F32, r_go)
        gs = put("gs", [NB, D], F32, r_go)
        r_c = region(4 * NBLK * DC * 4)
        CB = NBLK * DC * 4
        c_raw = put("c_raw", [P, NBLK, DC], F32, r_c)
        c_tr = put("c_tr", [P, NBLK, DC], F32, r_c + CB)
        c_hi = put("c_hi", [P, NBLK, DC], F32R, r_c + 2 * CB)
        c_lo = put("c_lo", [P, NBLK, DC], F32R, r_c + 3 * CB)
        c_pp = put("c_pp", [P, NBLK, DC], F32, r_c + 3 * CB)
        ident = new("ident", [P, P])
        mask = put("mask", [P, P], F32, r_s + 3 * SW * 4)
        had_r = new("had_r", [P, P], F32R)
        inv_hi = new("inv_hi", [NH, S], F32R)
        r_inv = region(TILE)
        inv32 = put("inv32", [NH, S], F32, r_inv)
        inv_lo = put("inv_lo", [NH, S], F32R, r_inv)
        spread_r = new("spread_r", [NH, KT, P], F32R)
        spread32 = put("spread32", [NH, KT, P], F32, r_c)
        cs = put("cs", [NB, D], F32, r_neg)
        qb_row = put("qb_row", [KT, P], F32, r_lin)
        hada = put("hada", [P, P], F32, r_c + 2 * CB)
        hadb = put("hadb", [P, P], F32, r_c + 3 * CB)
        cT = new("cT", [P, KT * NB])
        modc = new("modc", [P, 4, KT, NB])
        qb_col = new("qb_col", [P, KT])
        qb_neg = new("qb_neg", [P, KT])
        mhalf = new("mhalf", [P, TT])
        stats = new("stats", [P, TT, 6])
        mv = new("mv", [P, TT, 2])
        ve = new("ve", [P, TT])
        rstd = new("rstd", [P, TT])

        FW = KT * GH * 4
        r_slot = [r_h, r_q]
        f1_hi = [put(f"f1_hi{i}", [P, KT, GH], F32R, r_slot[i]) for i in range(2)]
        f1_lo = [put(f"f1_lo{i}", [P, KT, GH], F32R, r_slot[i] + FW) for i in range(2)]
        f3_hi = [put(f"f3_hi{i}", [P, KT, GH], F32R, r_slot[i] + 2 * FW) for i in range(2)]
        f3_lo = [put(f"f3_lo{i}", [P, KT, GH], F32R, r_slot[i] + 3 * FW) for i in range(2)]
        f2_hi = put("f2_hi", [P, GB, D], F32R, r_a)
        f2_lo = put("f2_lo", [P, GB, D], F32R, r_a + GB * TILE)
        hd_hi = put("hd_hi", [P, GB, S], F32R, r_a + 2 * GB * TILE)
        hd_lo = put("hd_lo", [P, GB, S], F32R, r_a + 3 * GB * TILE)
        fraw = [put(f"fraw{i}", [P, KT, GH], F32, r_xa + i * FW) for i in range(2)]
        r_xh2 = [r_w[KW], r_w[KW] + KT * TILE, r_w[OW], r_c]
        xh2 = [put(f"xh2_{b}", [P, TT, D], F32, r_xh2[b]) for b in range(NB)]
        f2raw = put("f2raw", [P, GB, D], F32, r_c + 2 * CB)
        ftr = put("ftr", [P, KT, GH], F32, r_lin)
        gate32 = put("gate32", [P, S], F32, r_neg)
        hid32 = put("hid32", [P, S], F32, r_neg + TILE)
        assert top[0] <= nc.sbuf_usable_end, (top[0], nc.sbuf_usable_end)

        bank = [ctx.enter_context(nc.psum_tensor(f"bank{i}", [P, 512], F32)) for i in range(8)]
        pj = bank[0:2]
        tr = bank[2:4]
        zb, ab = bank[6], bank[7]
        kv_bank = bank[4:8]
        gate_ps, up_ps = pj
        out_ps = bank[4:8]

        ld_c, ld_qb, ld_kb, ld_vb, ld_ob = (sem(f"ld_{n}") for n in ("c", "qb", "kb", "vb", "ob"))
        ld_x0 = [sem(f"ld_x0_{t}") for t in range(TT)]
        ld_xa = sem("ld_xa")
        ld_wm = [[sem(f"ld_wm{i}_{k}") for k in range(KT)] for i in range(2)]
        ld_wmx = sem("ld_wmx")
        ld_raw = [[sem(f"ld_raw{i}_{k}") for k in range(KT)] for i in range(2)]
        ld_chunk = sem("ld_chunk")
        ld_xt = [sem(f"ld_xt{i}") for i in range(TT)]
        ld_ga = [sem(f"ld_ga{i}") for i in range(2)]
        st_g, st_chunk, st_x1 = sem("st_g"), sem("st_chunk"), [sem(f"st_x1_{t}") for t in range(TT)]
        const_ready = sem("const_ready")
        had_step, v_ones = sem("had_step"), sem("v_ones")
        mask_ready = sem("mask_ready")
        cT_ps_ready, cT_ready = sem("cT_ps_ready"), sem("cT_ready")
        mod_ps, mod_ready, g_step, wm_used = sem("mod_ps"), sem("mod_ready"), sem("g_step"), sem("wm_used")
        wmx_used, mod_row = sem("wmx_used"), sem("mod_row")
        w_tr, w_hi_done, w_ready = sem("w_tr"), sem("w_hi_done"), sem("w_ready")
        stat_step, rstd_ready, xhat_ready = sem("stat_step"), sem("rstd_ready"), sem("xhat_ready")
        pool_step = sem("pool_step")
        tr_full, val_act, chunk_evac = sem("tr_full"), sem("val_act"), sem("chunk_evac")
        pj_full, k_lin, q_lin, relu_ready, exp_ready = sem("pj_full"), sem("k_lin"), sem("q_lin"), sem("relu_ready"), sem("exp_ready")
        v_hi_done, v_lo_done = sem("v_hi_done"), sem("v_lo_done")
        val_dve, split_hi, split_lo = sem("val_dve"), sem("split_hi"), sem("split_lo")
        kv_full, st_step, st_ready, st_hi_done, st_split = sem("kv_full"), sem("st_step"), sem("st_ready"), sem("st_hi_done"), sem("st_split")
        z_full, ze_ready, inv_ready, inv_hi_done, inv_split = (sem(n) for n in ("z_full", "ze_ready", "inv_ready", "inv_hi_done", "inv_split"))
        spread_step, inv_out = sem("spread_step"), sem("inv_out")
        att_full, spread_ready, ksum_zero = sem("att_full"), sem("spread_ready"), sem("ksum_zero")
        ot_ready, gaob_ready, xob_ready, x1_ready = sem("ot_ready"), sem("gaob_ready"), sem("xob_ready"), sem("x1_ready")
        chunk_tr, chunk_hi, chunk_lo, chunk_step = sem("chunk_tr"), sem("chunk_hi"), sem("chunk_lo"), sem("chunk_step")
        ld_xh2, ld_gb, ld_x1 = sem("ld_xh2"), sem("ld_gb"), [sem(f"ld_x1_{b}") for b in range(NB)]
        ld_f = [sem("ld_f1"), sem("ld_f3")]
        ld_f2 = sem("ld_f2")
        f_tr, f_hi, f_lo = sem("f_tr"), sem("f_hi"), sem("f_lo")
        f2_hi_done, f2_ready = sem("f2_hi_done"), sem("f2_ready")
        gate_full, up_full, gate_used, up_used = sem("gate_full"), sem("up_full"), sem("gate_used"), sem("up_used")
        hid_hi, hid_lo = sem("hid_hi"), sem("hid_lo")
        out_full, contrib, added = sem("out_full"), sem("contrib"), sem("added")
        st_out = sem("st_out")

        pj_at, tr_at, split_at, exp_at, dve_at, act_at, ot_at = {}, {}, {}, {}, {}, {}, {}

        def use(where, key):
            where[key] = len(where)

        def use_split(key, by):
            use(split_at, key)
            use(by, key)

        def transposed_after(b, t):
            return range(2 * t, min(2 * t + 2, KT if b + 1 < NB else 2))

        for kt in range(KT):
            use(tr_at, ("h", 0, kt))
            use_split(("h", 0, kt), act_at)
        for b in range(NB):
            for t in range(TT):
                use(pj_at, ("k", b, t))
                use(exp_at, ("k", b, t))
                if t >= 1:
                    use_split(("k", b, t - 1), dve_at)
                if t == 0 and b >= 1:
                    for i in range(2):
                        use(tr_at, ("chunk", 2 * b - 1, i))
            if b >= 1:
                use_split(("a", b - 1, 0), dve_at)
            use_split(("k", b, TT - 1), dve_at)
            for t in range(TT):
                use(pj_at, ("v", b, t))
                if t >= 1 and b >= 1:
                    use_split(("a", b - 1, t), dve_at)
            for t in range(TT):
                use(pj_at, ("q", b, t))
                use(exp_at, ("q", b, t))
                use_split(("q", b, t), dve_at)
            for i in range(2):
                use(tr_at, ("chunk", 2 * b, i))
            for t in range(TT):
                if b >= 1:
                    use(pj_at, ("o", b - 1, t))
                    use(ot_at, (b - 1, t))
                for kt in transposed_after(b, t):
                    key = ("h", b + 1, kt) if b + 1 < NB else ("h2", 0, kt)
                    use(tr_at, key)
                    use_split(key, act_at)
        for g in range(KT):
            use_split(("a", NB - 1, g), dve_at)
        for i in range(2):
            use(tr_at, ("chunk", NCH - 1, i))
        for kt in range(2, KT):
            use(tr_at, ("h2", 0, kt))
            use_split(("h2", 0, kt), act_at)
        for t in range(TT):
            use(pj_at, ("o", NB - 1, t))
            use(ot_at, (NB - 1, t))
        for b in range(1, NB):
            for kt in range(KT):
                use(tr_at, ("h2", b, kt))
                use_split(("h2", b, kt), act_at)
        pj_order, tr_order, exp_order = list(pj_at), list(tr_at), list(exp_at)
        raw_of = {KW: raw0, VW: raw1, QW: raw0, OW: raw0}
        raw_slot = {KW: (0, 1), VW: (1, 1), QW: (0, 2), OW: (0, 3)}
        w_dram = {KW: k_w, VW: v_w, QW: q_w, OW: o_w}

        def at_of(b):
            return (atz_hi, atz_lo) if b == NB - 1 else (at_hi, at_lo)

        def split_tile(key):
            kind, b, t = key
            if kind == "k":
                return kp_hi[:, t, :], kp_lo[:, t, :]
            if kind == "q":
                return qp_hi[:, t, :], qp_lo[:, t, :]
            if kind == "a":
                return at_of(b)[0][:, t, :], at_of(b)[1][:, t, :]
            if kind == "h":
                return h_hi[:, t, :], h_lo[:, t, :]
            return h2_hi[b][:, t, :], h2_lo[b][:, t, :]

        def att_banks(g):
            return (kv_bank[0], kv_bank[1]) if g % 2 else (zb, ab)

        def val_tile(key):
            return val[:, split_at[key] % 3, :]

        def blocks_of(w_ap, q, kt):
            k0 = P * kt + Q32 * q
            return w_ap[:, k0:k0 + Q32].rearrange("(v j) i -> j v i", j=Q32)

        def blocks_at(tile, q, kt):
            return tile[Q32 * q:Q32 * q + Q32, kt, :].rearrange("j (v i) -> j v i", i=Q32)

        def butterfly(eng, n, s, u):
            if s == 0:
                eng.wait_ge(chunk_evac, 2 * n + 2)
            else:
                eng.wait_ge(chunk_step, 8 * n + 2 * s)
            src, dst = (c_tr, c_pp) if s % 2 == 0 else (c_pp, c_tr)
            a = src[:, :, :].rearrange("p (n u h) d -> p n u (h d)", u=2, h=1 << s)
            o = dst[:, :, :].rearrange("p (n u h) d -> p n u (h d)", u=2, h=1 << s)
            eng.tensor_tensor(o[:, :, u, :], a[:, :, 0, :], a[:, :, 1, :], (ALU.add, ALU.subtract)[u]).then_inc(chunk_step, 1)

        def add_residual(eng, b, t):
            n = ot_at[(b, t)]
            eng.wait_ge(xob_ready, n + 1)
            eng.wait_ge(ot_ready, n + 1)
            if n >= 1:
                eng.wait_ge(x1_ready, n)
            eng.tensor_tensor(xt[:, t, :], xt[:, t, :], ot[:, n % 2, :], ALU.add).then_inc(x1_ready, 1)

        def add_contribution(eng, m, b, t):
            eng.wait_ge(contrib, m + TT + 1)
            eng.wait_ge(added, m + 2)
            xr = x1res[b][:, t, :]
            eng.tensor_tensor(xr, xr, ot[:, t % 2, :], ALU.add).then_inc(added, 1)

        block = ctx.enter_context(nc.Block())

        @block.sync
        def _(sp):
            def load_weight(i):
                n, _ = raw_slot[i]
                for kt in range(KT):
                    for q in range(NQ):
                        sp.dma_start(blocks_at(raw_of[i], q, kt), blocks_of(w_dram[i], q, kt)).then_inc(ld_raw[n][kt], 16)

            def wmod_of(section):
                return wmod[:, section * D:(section + 1) * D].rearrange("(k p) n -> p k n", p=P)

            def load_xa(b):
                sp.dma_start(xa[:, :, :], x[b, :, :].rearrange("(t p) d -> p t d", p=P)).then_inc(ld_xa, 16)

            def load_chunk(n):
                if n >= 1:
                    sp.wait_ge(chunk_tr, n)
                for q in range(NQ):
                    for v in range(DC // Q32):
                        r0 = n * DC + v * Q32
                        src = W2[r0:r0 + Q32, :].rearrange("j (k a i) -> j k a i", a=NQ, i=Q32)[:, :, q, :]
                        dst = c_raw[Q32 * q:Q32 * q + Q32, :, v * Q32:(v + 1) * Q32]
                        sp.dma_start(dst, src).then_inc(ld_chunk, 16)

            def store_chunk(n):
                sp.wait_ge(chunk_step, 8 * (n + 1))
                sp.dma_start(w2t_dram[:, :, n * DC:(n + 1) * DC].rearrange("b p d -> p b d"), c_tr[:, :, :]).then_inc(st_chunk, 16)

            def load_xt(b, t):
                if b >= 1:
                    sp.wait_ge(st_x1[t], 16 * b)
                sp.dma_start(xt[:, t, :], x[b, t * P:(t + 1) * P, :]).then_inc(ld_xt[t], 16)

            def store_x1(b, t):
                sp.wait_ge(x1_ready, TT * b + t + 1)
                sp.dma_start(x1_dram[b, t * P:(t + 1) * P, :], xt[:, t, :]).then_inc(st_x1[t], 16)

            def x1_of(b):
                return x1_dram[b, :, :].rearrange("(t p) d -> p t d", p=P)

            def load_ga(b):
                if b >= 2:
                    sp.wait_ge(x1_ready, TT * (b - 1))
                sp.dma_start(ga_bc[:, b % 2, :], g_dram[b, 0, :].partition_broadcast(P)).then_inc(ld_ga[b % 2], 16)

            def load_f(m, w_ap):
                for kt in range(KT):
                    for q in range(NQ):
                        sp.dma_start(blocks_at(fraw[m], q, kt), blocks_of(w_ap, q, kt)).then_inc(ld_f[m], 16)

            def load_f_group(g):
                sp.wait_ge(f_tr, 2 * g - 1)
                load_f(0, W1[bass.ds(g * GH, GH), :])
                sp.wait_ge(f_tr, 2 * g)
                load_f(1, W3[bass.ds(g * GH, GH), :])

            def load_f2(g):
                sp.dma_start(f2raw[:, :, :], w2t_dram[bass.ds(g * GB, GB), :, :].rearrange("b p d -> p b d")).then_inc(ld_f2, 16)

            sp.dma_start(cs[:, :], c).then_inc(ld_c, 16)
            sp.dma_start(qb_row[:, :], q_b.rearrange("(g p) -> g p", p=P)).then_inc(ld_qb, 16)
            for i in range(2):
                for k in range(KT):
                    sp.dma_start(wm[i][:, k, :], wmod[k * P:(k + 1) * P, i * D:(i + 1) * D]).then_inc(ld_wm[i][k], 16)
                if i == 0:
                    for t in range(TT):
                        sp.dma_start(xa[:, t, :], x[0, t * P:(t + 1) * P, :]).then_inc(ld_x0[t], 16)
            load_weight(KW)
            sp.dma_start(kb_bc[:, :], k_b.partition_broadcast(P)).then_inc(ld_kb, 16)
            load_weight(VW)
            sp.dma_start(vb_bc[:, :], v_b.partition_broadcast(P)).then_inc(ld_vb, 16)
            sp.dma_start(ob_bc[:, :], o_b.partition_broadcast(P)).then_inc(ld_ob, 16)
            sp.dma_start(wmx[:, :, :], wmod_of(2)).then_inc(ld_wmx, 16)
            sp.wait_ge(w_tr, KT)
            load_weight(QW)
            sp.wait_ge(tr_full, tr_at[("h", 0, KT - 1)] + 1)
            load_xa(1)
            sp.wait_ge(spread_ready, 1)
            load_chunk(0)
            sp.wait_ge(wmx_used, 1)
            sp.dma_start(wmx[:, :, :], wmod_of(5)).then_inc(ld_wmx, 16)
            load_chunk(1)
            sp.wait_ge(wmx_used, 2)
            sp.dma_start(wmx[:, :, :], wmod_of(3)).then_inc(ld_wmx, 16)
            sp.wait_ge(w_tr, 3 * KT)
            load_weight(OW)
            sp.wait_ge(wmx_used, 3)
            sp.dma_start(wmx[:, :, :], wmod_of(4)).then_inc(ld_wmx, 16)
            sp.wait_ge(g_step, 10)
            sp.dma_start(g_dram, gr[:, :, :]).then_inc(st_g, 16)
            store_chunk(0)
            sp.wait_ge(st_g, 16)
            load_ga(0)
            load_ga(1)
            for b in range(NB):
                if b == NB - 1:
                    load_f(0, W1[0:GH, :])
                if b >= 1:
                    store_chunk(2 * b - 1)
                if b == NB - 1:
                    sp.wait_ge(pj_full, pj_at[("k", NB - 1, TT - 1)] + 1)
                    sp.dma_start(xh2[0][:, :, :], x1_of(0)).then_inc(ld_xh2, 16)
                if b >= 1:
                    load_chunk(2 * b + 1)
                if b >= 2:
                    load_ga(b)
                if b == NB - 1:
                    load_f(1, W3[0:GH, :])
                    sp.wait_ge(kv_full, KT * NB)
                    for i in range(2):
                        sp.dma_start(x1res[i][:, :, :], x1_of(i)).then_inc(ld_x1[i], 16)
                if b >= 1:
                    store_chunk(2 * b)
                if b + 1 < NB:
                    sp.wait_ge(tr_full, tr_at[("h", b + 1, KT - 1)] + 1)
                if b + 2 < NB:
                    load_xa(b + 2)
                if b + 1 < NB:
                    load_chunk(2 * b + 2)
                if b == 0:
                    sp.wait_ge(wmx_used, 4)
                for t in range(TT):
                    if b >= 1:
                        store_x1(b - 1, t)
                    if t >= 1:
                        load_xt(b, t - 1)
                load_xt(b, TT - 1)
            sp.wait_ge(att_full, NB * KT)
            sp.dma_start(gb_bc[:, :, :], g_dram[:, 1, :].partition_broadcast(P)).then_inc(ld_gb, 16)
            store_chunk(NCH - 1)
            sp.wait_ge(st_chunk, 16 * NCH)
            load_f2(0)
            sp.wait_ge(pj_full, len(pj_at))
            sp.dma_start(x1res[2][:, :, :], x1_of(2)).then_inc(ld_x1[2], 16)
            for t in range(TT):
                store_x1(NB - 1, t)
            load_f_group(1)
            for t in range(TT):
                sp.wait_ge(st_x1[t], 16 * NB)
            sp.dma_start(x1res[3][:, :, :], x1_of(3)).then_inc(ld_x1[3], 16)
            sp.wait_ge(f2_ready, 1)
            load_f2(1)
            with sp.Fori(2, NG) as g:
                load_f_group(g)
                sp.wait_ge(f2_ready, g)
                load_f2(g)
            for b in range(NB):
                for t in range(TT):
                    m = (NG - 1) * NB * TT + TT * b + t
                    sp.wait_ge(added, m + 1 + 2)
                    sp.dma_start(out[b, t * P:(t + 1) * P, :], x1res[b][:, t, :]).then_inc(st_out, 16)
            sp.wait_ge(st_out, 16 * NB * TT)

        @block.tensor
        def _(pe):
            def three(o, l_hi, l_lo, r_hi, r_lo, first, last):
                nc.tensor.matmul(o, l_hi, r_hi, start=first, stop=False)
                nc.tensor.matmul(o, l_hi, r_lo, start=False, stop=False)
                return nc.tensor.matmul(o, l_lo, r_hi, start=False, stop=last)

            def wait_pj(key):
                n = pj_at[key]
                if n < 2:
                    pe.wait_ge(mod_ready, 2)
                    return
                kind, b, t = pj_order[n - 2]
                if kind == "v":
                    pe.wait_ge(v_lo_done, TT * b + t + 1)
                elif kind == "o":
                    pe.wait_ge(ot_ready, ot_at[(b, t)] + 1)
                elif kind == "k":
                    pe.wait_ge(k_lin, TT * b + t + 1)
                else:
                    pe.wait_ge(relu_ready, exp_at[(kind, b, t)] + 1)

            def wait_tr(key):
                n = tr_at[key]
                if n < 2:
                    return
                old = tr_order[n - 2]
                if old[0] == "chunk":
                    pe.wait_ge(chunk_evac, 2 * old[1] + old[2] + 1)
                else:
                    pe.wait_ge(val_act, act_at[old] + 1)

            def transposes(kind, b, src, kts=range(KT)):
                n = b + (NB if kind == "h2" else 0)
                pe.wait_ge(xhat_ready, TT * n + TT)
                for kt in kts:
                    key = (kind, b, kt)
                    wait_tr(key)
                    for t in range(TT):
                        mm = nc.tensor.transpose(tr[tr_at[key] % 2][:, t * P:(t + 1) * P], src[:, t, kt * P:(kt + 1) * P], ident[:, :])
                    mm.then_inc(tr_full, 1)

            def project_tile(kind, b, t):
                key = (kind, b, t)
                wait_pj(key)
                o = pj[pj_at[key] % 2][:, :]
                w = {"k": KW, "v": VW, "q": QW, "o": OW}[kind]
                a_hi, a_lo = at_of(b) if kind == "o" else (h_hi, h_lo)
                for kt in range(KT):
                    if t == 0 and b == 0:
                        pe.wait_ge(w_ready, KT * w + kt + 1)
                    if t == 0 and kind in ("k", "o"):
                        pe.wait_ge(split_lo, split_at[("h" if kind == "k" else "a", b, kt)] + 1)
                    ts = slice(t * P, (t + 1) * P)
                    if kind == "q":
                        mm = three(o, w_hi[w][:, kt, ts], w_lo[w][:, kt, ts], a_hi[:, kt, :], a_lo[:, kt, :], kt == 0, kt == KT - 1)
                    else:
                        mm = three(o, a_hi[:, kt, ts], a_lo[:, kt, ts], w_hi[w][:, kt, :], w_lo[w][:, kt, :], kt == 0, kt == KT - 1)
                mm.then_inc(pj_full, 1)

            def normaliser(b):
                pe.wait_ge(st_split, b + 1)
                if b == 0:
                    pe.wait_ge(mod_ready, 3)
                for g in range(KT):
                    pe.wait_ge(split_lo, split_at[("q", b, g)] + 1)
                    cols = slice(KT * P + g * NH, KT * P + (g + 1) * NH)
                    mm = three(zb[0:NH, :], st_hi[:, cols], st_lo[:, cols], qp_hi[:, g, :], qp_lo[:, g, :], g == 0, g == KT - 1)
                mm.then_inc(z_full, 1)

            def attend(b, g):
                if g == 0:
                    pe.wait_ge(inv_split, b + 1)
                    pe.wait_ge(spread_ready, 1)
                    pe.wait_ge(mod_ready, 4)
                if g >= 2:
                    pe.wait_ge(val_dve, dve_at[("a", b, g - 2)] + 1)
                zi, o = att_banks(g)
                nc.tensor.matmul(zi[:, :], spread_r[:, g, :], inv_hi[:, :], start=True, stop=False)
                nc.tensor.matmul(zi[:, :], spread_r[:, g, :], inv_lo[:, :], start=False, stop=True)
                cols = slice(g * P, (g + 1) * P)
                three(o[:, :], st_hi[:, cols], st_lo[:, cols], qp_hi[:, g, :], qp_lo[:, g, :], True, True).then_inc(att_full, 1)

            def key_values(b):
                pe.wait_ge(split_lo, split_at[("k", b, TT - 1)] + 1)
                pe.wait_ge(v_lo_done, TT * (b + 1))
                if b >= 1:
                    pe.wait_ge(st_step, 3 * KT * b)
                    pe.wait_ge(val_dve, dve_at[("a", b - 1, KT - 1)] + 1)
                else:
                    pe.wait_ge(v_ones, 1)
                    pe.wait_ge(g_step, 7)
                for g in range(KT):
                    o = kv_bank[g]
                    ds_ = slice(g * P, (g + 1) * P)
                    for t in range(TT):
                        first, last = t == 0, t == TT - 1
                        if last:
                            nc.tensor.matmul(o[:, 0:HW], kp_lo[:, t, ds_], v[:, t, g, 0:HW], start=False, stop=False)
                        mm = nc.tensor.matmul(o[:, 0:VG], kp_hi[:, t, ds_], v[:, t, g, :], start=first, stop=last)
                        if not last:
                            nc.tensor.matmul(o[:, 0:HW], kp_lo[:, t, ds_], v[:, t, g, 0:HW], start=False, stop=False)
                    mm.then_inc(kv_full, 1)

            def hadamard(n):
                pe.wait_ge(chunk_lo, n + 1)
                for i in range(2):
                    key = ("chunk", n, i)
                    wait_tr(key)
                    o = tr[tr_at[key] % 2][:, :]
                    bs = slice(i * NBLK // 2, (i + 1) * NBLK // 2)
                    nc.tensor.matmul(o, had_r[:, :], c_hi[:, bs, :], start=True, stop=False)
                    nc.tensor.matmul(o, had_r[:, :], c_lo[:, bs, :], start=False, stop=True).then_inc(tr_full, 1)

            def mod_columns(w, o, s):
                for m in range(KT):
                    for k in range(KT):
                        mm = nc.tensor.matmul(o[:, (s * KT + m) * NB:(s * KT + m + 1) * NB], w[:, k, m * P:(m + 1) * P],
                                              cT[:, k * NB:(k + 1) * NB], start=(k == 0), stop=(k == KT - 1))
                return mm

            def mod_rows(w, o, loads=None):
                for k in range(KT):
                    if loads:
                        pe.wait_ge(loads[k], 16)
                    mm = nc.tensor.matmul(o[0:NB, :], cT[:, k * NB:(k + 1) * NB], w[:, k, :], start=(k == 0), stop=(k == KT - 1))
                return mm

            pe.wait_ge(const_ready, 2)
            pe.wait_ge(ld_c, 16)
            for kt in range(KT):
                nc.tensor.transpose(bank[4][:, kt * NB:(kt + 1) * NB], cs[:, kt * P:(kt + 1) * P], ident[0:NB, 0:NB])
            pe.wait_ge(ld_qb, 16)
            nc.tensor.transpose(bank[4][:, KT * NB:KT * NB + KT], qb_row[:, :], ident[0:KT, 0:KT]).then_inc(cT_ps_ready, 1)
            pe.wait_ge(cT_ready, 1)
            for i in range(2):
                mod_rows(wm[i], pj[i], ld_wm[i]).then_inc(wm_used, 1)
            for i in range(2):
                pe.wait_ge(mod_row, i + 1)
                for m in range(KT):
                    n = (i * KT + m) * NB
                    mm = nc.tensor.transpose(bank[5][:, n:n + NB], gr[:, i, m * P:(m + 1) * P], ident[0:NB, 0:NB])
            mm.then_inc(wm_used, 1)
            transposes("h", 0, xa)

            for b in range(NB):
                if b >= 1:
                    normaliser(b - 1)
                for t in range(TT):
                    project_tile("k", b, t)
                    if t == 0 and b == 1:
                        pe.wait_ge(ld_wmx, 64)
                        mod_columns(wmx, ab, 0).then_inc(wmx_used, 1)
                    if t == 0 and b >= 1:
                        hadamard(2 * b - 1)
                if b >= 1:
                    attend(b - 1, 0)
                if b == 0:
                    pe.wait_ge(ld_wmx, 16)
                    mod_rows(wmx, zb).then_inc(wmx_used, 1)
                for t in range(TT):
                    project_tile("v", b, t)
                    if t < TT - 1 and b >= 1:
                        attend(b - 1, t + 1)
                    if b == 0 and t == 1:
                        pe.wait_ge(ld_wmx, 32)
                        mod_rows(wmx, ab).then_inc(wmx_used, 1)
                if b == 0:
                    pe.wait_ge(had_step, 14)
                for t in range(2):
                    project_tile("q", b, t)
                hadamard(2 * b)
                key_values(b)
                for t in range(2, TT):
                    project_tile("q", b, t)
                for t in range(TT):
                    if b >= 1:
                        project_tile("o", b - 1, t)
                    if transposed_after(b, t):
                        if b + 1 < NB:
                            transposes("h", b + 1, xa, transposed_after(b, t))
                        else:
                            transposes("h2", 0, xh2[0], transposed_after(b, t))
                            normaliser(b)
                    if b == 0 and t == 0:
                        pe.wait_ge(ld_wmx, 48)
                        pe.wait_ge(st_step, 3 * KT)
                        mod_columns(wmx, zb, 0).then_inc(wmx_used, 1)
            for g in range(KT):
                attend(NB - 1, g)
            hadamard(NCH - 1)
            for t in range(TT):
                project_tile("o", NB - 1, t)
                if t == 0:
                    transposes("h2", 0, xh2[0], range(2, KT))

            pe.wait_ge(ot_ready, NB * TT - 1)

            def ffn(g, par, b):
                n = (g * NB + b) * GB
                first = isinstance(g, int) and g == 0
                if first:
                    pe.wait_ge(split_lo, split_at[("h2", b, KT - 1)] + 1)
                for i in range(GB):
                    hs = slice(i * P, (i + 1) * P)
                    for o, f_h, f_l, used, full in ((gate_ps, f1_hi, f1_lo, gate_used, gate_full), (up_ps, f3_hi, f3_lo, up_used, up_full)):
                        pe.wait_ge(used, n + i + 1)
                        if b == 0 and i == 0:
                            pe.wait_ge(f_lo, 2 * g + (2 if full is up_full else 1))
                        if first and b == 0 and i == 0 and full is up_full:
                            pe.wait_ge(ot_ready, NB * TT)
                        for kt in range(KT):
                            mm = three(o[:, :], f_h[par][:, kt, hs], f_l[par][:, kt, hs], h2_hi[b][:, kt, :], h2_lo[b][:, kt, :], kt == 0, kt == KT - 1)
                        mm.then_inc(full, 1)
                    if first and b + 1 < NB:
                        transposes("h2", b + 1, xh2[b + 1], range(i * KT // GB, (i + 1) * KT // GB))
                if b == 0:
                    pe.wait_ge(f2_ready, g + 1)
                for i in range(GB):
                    pe.wait_ge(hid_lo, n + i + 2)
                    for t in range(TT):
                        if i == 0:
                            pe.wait_ge(contrib, (g * NB + b) * TT + t + 1)
                        ts = slice(t * P, (t + 1) * P)
                        mm = three(out_ps[t][:, :], hd_hi[:, i, ts], hd_lo[:, i, ts], f2_hi[:, i, :], f2_lo[:, i, :], i == 0, i == GB - 1)
                        if i == GB - 1:
                            mm.then_inc(out_full, 1)

            for b in range(NB):
                ffn(0, 0, b)
            with pe.Fori(1, NG - 1, 2) as g:
                for par in (1, 0):
                    for b in range(NB):
                        ffn(g + (1 - par), par, b)
            for b in range(NB):
                ffn(NG - 1, 1, b)

        @block.scalar
        def _(act):
            def to_hi(key):
                if key in dve_at:
                    act.wait_ge(val_dve, dve_at[key] + 1)
                else:
                    act.wait_ge(val_act, act_at[key] + 1)
                nc.scalar.activation(split_tile(key)[0], val_tile(key), ACT.Copy).then_inc(split_hi, 1)

            def modulate(kind, b, kts=range(KT)):
                s = 0 if kind == "h" else 2
                for kt in kts:
                    key = (kind, b, kt)
                    act.wait_ge(tr_full, tr_at[key] + 1)
                    if split_at[key] >= 3:
                        act.wait_ge(split_lo, split_at[key] - 2)
                    nc.scalar.activation(val_tile(key), tr[tr_at[key] % 2][:, :], ACT.Identity,
                                         bias=modc[:, s, kt, b:b + 1], scale=modc[:, s + 1, kt, b:b + 1]).then_inc(val_act, 1)
                    to_hi(key)

            def feature_exp(key):
                kind, b, t = key
                e = exp_at[key]
                s = e % 2
                if kind == "k":
                    act.wait_ge(k_lin, TT * b + t + 1)
                    nc.scalar.activation(neg[:, s, :], lin[:, s, :], ACT.Relu, scale=-1.0).then_inc(relu_ready, 1)
                else:
                    ps = pj[pj_at[key] % 2][:, :]
                    act.wait_ge(val_dve, dve_at[exp_order[e - 2]] + 1)
                    act.wait_ge(pj_full, pj_at[key] + 1)
                    nc.scalar.activation(lin[:, s, :], ps, ACT.Identity, bias=qb_col[:, t:t + 1]).then_inc(q_lin, 1)
                    nc.scalar.activation(neg[:, s, :], ps, ACT.Relu, bias=qb_neg[:, t:t + 1], scale=-1.0).then_inc(relu_ready, 1)
                act.wait_ge(relu_ready, e + 1)
                nc.scalar.activation(neg[:, s, :], neg[:, s, :], ACT.Exp, scale=-1.0).then_inc(exp_ready, 1)

            def value_hi(b, t):
                key = ("v", b, t)
                act.wait_ge(pj_full, pj_at[key] + 1)
                nc.scalar.activation(v[:, t, :, 0:P], pj[pj_at[key] % 2][:, :].rearrange("p (g e) -> p g e", g=KT),
                                     ACT.Copy).then_inc(v_hi_done, 1)

            def normaliser_epsilon(b):
                act.wait_ge(z_full, b + 1)
                nc.scalar.activation(zb[0:NH, :], zb[0:NH, :], ACT.Copy, bias=EPS_Z).then_inc(ze_ready, 1)

            def inverse_out(b, g):
                key = ("a", b, g)
                act.wait_ge(att_full, KT * b + g + 1)
                act.wait_ge(split_lo, split_at[key] - 2)
                nc.scalar.activation(val_tile(key), att_banks(g)[0][:, :], ACT.Copy).then_inc(inv_out, 1)

            def inverse_hi(b):
                act.wait_ge(inv_ready, b + 1)
                if b >= 1:
                    act.wait_ge(att_full, KT * b)
                nc.scalar.activation(inv_hi[:, :], inv32[:, :], ACT.Copy).then_inc(inv_hi_done, 1)

            def chunk_to_hi(n):
                act.wait_ge(chunk_tr, n + 1)
                nc.scalar.activation(c_hi[:, :, :], c_tr[:, :, :], ACT.Copy).then_inc(chunk_hi, 1)

            def chunk_out(n):
                for i in range(2):
                    key = ("chunk", n, i)
                    act.wait_ge(tr_full, tr_at[key] + 1)
                    nc.scalar.activation(c_tr[:, i * NBLK // 2:(i + 1) * NBLK // 2, :],
                                         tr[tr_at[key] % 2][:, :].rearrange("p (b d) -> p b d", d=DC),
                                         ACT.Copy, scale=float(HID) ** -0.5).then_inc(chunk_evac, 1)

            def weight_to_hi(i, kt):
                act.wait_ge(w_tr, KT * i + kt + 1)
                nc.scalar.activation(w_hi[i][:, kt, :], wtr[:, kt, :], ACT.Copy).then_inc(w_hi_done, 1)

            def ffn_weight_hi(count, which, par):
                act.wait_ge(f_tr, count)
                nc.scalar.activation((f1_hi, f3_hi)[which][par][:, :, :], ftr[:, :, :], ACT.Copy).then_inc(f_hi, 1)

            act.wait_ge(cT_ps_ready, 1)
            qb_ps = bank[4][:, KT * NB:KT * NB + KT]
            nc.scalar.activation(qb_col[:, :], qb_ps, ACT.Copy)
            nc.scalar.activation(qb_neg[:, :], qb_ps, ACT.Copy, scale=-1.0)
            nc.scalar.activation(cT[:, :], bank[4][:, 0:KT * NB], ACT.Silu).then_inc(cT_ready, 1)
            act.wait_ge(cT_ready, 1)
            for i in range(2):
                act.wait_ge(wm_used, i + 1)
                nc.scalar.activation(gr[:, i, :], pj[i][0:NB, :], ACT.Copy).then_inc(mod_row, 1)
            weight_to_hi(KW, 0)
            act.wait_ge(mod_ready, 2)
            for kt in range(KT):
                modulate("h", 0, range(kt, kt + 1))
                if kt + 1 < KT:
                    weight_to_hi(KW, kt + 1)
            for b in range(NB):
                if b >= 1:
                    normaliser_epsilon(b - 1)
                for t in range(TT):
                    if t == 1 and b >= 1:
                        inverse_hi(b - 1)
                    feature_exp(("k", b, t))
                    if b == 0:
                        weight_to_hi(VW, t)
                    if t == 0 and b >= 1:
                        chunk_out(2 * b - 1)
                    if t >= 1:
                        to_hi(("k", b, t - 1))
                if b >= 1:
                    inverse_out(b - 1, 0)
                for t in range(TT):
                    if b >= 1:
                        to_hi(("a", b - 1, t))
                    if t == 0:
                        to_hi(("k", b, TT - 1))
                    value_hi(b, t)
                    if b >= 1 and t < TT - 1:
                        inverse_out(b - 1, t + 1)
                    if b == 0:
                        for kt in range(2 * t, min(2 * t + 2, KT)):
                            weight_to_hi(QW, kt)
                    if t == 3:
                        chunk_to_hi(2 * b)
                for t in range(TT):
                    if t == 2:
                        chunk_out(2 * b)
                    feature_exp(("q", b, t))
                    if t >= 1:
                        to_hi(("q", b, t - 1))
                    if t == 2:
                        act.wait_ge(st_ready, KT * (b + 1))
                        nc.scalar.activation(st_hi[:, :], st32[:, :], ACT.Copy).then_inc(st_hi_done, 1)
                to_hi(("q", b, TT - 1))
                if b + 1 < NB:
                    modulate("h", b + 1)
                    if b == 0:
                        for kt in range(KT):
                            weight_to_hi(OW, kt)
                    chunk_to_hi(2 * b + 1)
            act.wait_ge(mod_ready, 4)
            modulate("h2", 0, range(2))
            normaliser_epsilon(NB - 1)
            ffn_weight_hi(1, 0, 0)
            inverse_hi(NB - 1)
            inverse_out(NB - 1, 0)
            for g in range(KT):
                if g + 1 < KT:
                    inverse_out(NB - 1, g + 1)
                if g == 1:
                    chunk_to_hi(NCH - 1)
                to_hi(("a", NB - 1, g))
            chunk_out(NCH - 1)
            ffn_weight_hi(2, 1, 0)
            modulate("h2", 0, range(2, KT))

            def weight2_to_hi(g):
                act.wait_ge(ld_f2, 16 * g + 16)
                nc.scalar.activation(f2_hi[:, :, :], f2raw[:, :, :], ACT.Copy).then_inc(f2_hi_done, 1)

            def ffn(g, par, b, more):
                first = isinstance(g, int) and g == 0
                wb = 1 if first else 0
                n = (g * NB + b) * GB
                for i in range(GB):
                    act.wait_ge(gate_full, n + i + 1)
                    act.wait_ge(up_used, n + i + 1)
                    nc.scalar.activation(gate32[:, :], gate_ps[:, :], ACT.Silu).then_inc(gate_used, 1)
                    if b == 0 and i == 0 and not first:
                        weight2_to_hi(g)
                    act.wait_ge(up_used, n + i + 2)
                    nc.scalar.activation(hd_hi[:, i, :], hid32[:, :], ACT.Copy).then_inc(hid_hi, 1)
                    if i == GB - 1 and more and wb <= b < wb + 2:
                        ffn_weight_hi(2 * g + 3 + b - wb, b - wb, 1 - par)
                    if first and b + 1 < NB:
                        modulate("h2", b + 1, range(i * KT // GB, (i + 1) * KT // GB))
                    if b == 0 and i == 0 and first:
                        weight2_to_hi(g)

            act.sem_inc(gate_used, 1)
            for b in range(NB):
                ffn(0, 0, b, True)
            with act.Fori(1, NG - 1, 2) as g:
                for par in (1, 0):
                    for b in range(NB):
                        ffn(g + (1 - par), par, b, True)
            for b in range(NB):
                ffn(NG - 1, 1, b, False)

        @block.vector
        def _(dve):
            def statistics(n, src):
                if 0 < n < NB:
                    dve.wait_ge(ld_xa, 16 * n)
                elif n == NB:
                    dve.wait_ge(ld_xh2, 16)
                elif n > NB:
                    dve.wait_ge(ld_x1[n - NB], 16)
                if n >= 1:
                    dve.wait_ge(stat_step, 9 * n)
                for t in range(TT):
                    if n == 0:
                        dve.wait_ge(ld_x0[t], 16)
                    nc.vector.bn_stats(stats[:, t, :], src[:, t, :]).then_inc(stat_step, 1)

            def mean_variance(n):
                if n >= 1:
                    dve.wait_ge(xhat_ready, TT * n)
                for t in range(TT):
                    dve.wait_ge(stat_step, 9 * n + t + 1)
                    nc.vector.bn_aggr(mv[:, t, :], stats[:, t, :]).then_inc(stat_step, 1)
                dve.wait_ge(stat_step, 9 * n + 8)
                nc.vector.tensor_scalar(ve[:, :], mv[:, :, 1], EPS_LN, None, ALU.add).then_inc(stat_step, 1)

            def normalise(n, t, dst, src):
                dve.wait_ge(rstd_ready, n + 1)
                nc.vector.tensor_scalar(dst[:, t, :], src[:, t, :], mv[:, t, 0:1], rstd[:, t:t + 1],
                                        ALU.subtract, ALU.mult).then_inc(xhat_ready, 1)

            def second_statistics(b):
                statistics(NB + b, x1res[b])
                mean_variance(NB + b)

            def second_normalise(b):
                if b == NB - 1:
                    dve.wait_ge(st_chunk, 16 * NCH)
                for t in range(TT):
                    normalise(NB + b, t, xh2[b], x1res[b])

            def weight_transpose(i, kt):
                n, loads = raw_slot[i]
                dve.wait_ge(ld_raw[n][kt], 16 * NQ * loads)
                if i >= 1:
                    dve.wait_ge(w_ready, KT * (i - 1) + kt + 1)
                nc.vector.transpose(wtr[:, kt, :], raw_of[i][:, kt, :]).then_inc(w_tr, 1)

            def weight_to_lo(i, kt):
                dve.wait_ge(w_hi_done, KT * i + kt + 1)
                nc.vector.tensor_tensor(w_lo[i][:, kt, :], wtr[:, kt, :], w_hi[i][:, kt, :].bitcast(F32), ALU.subtract).then_inc(w_ready, 1)

            def chunk_transpose(n):
                dve.wait_ge(ld_chunk, 16 * NQ * (DC // Q32) * (n + 1))
                if n >= 1:
                    dve.wait_ge(st_chunk, 16 * n)
                nc.vector.transpose(c_tr[:, :, :], c_raw[:, :, :]).then_inc(chunk_tr, 1)

            def chunk_to_lo(n):
                dve.wait_ge(chunk_hi, n + 1)
                if n >= 1:
                    dve.wait_ge(chunk_step, 8 * n)
                nc.vector.tensor_tensor(c_lo[:, :, :], c_tr[:, :, :], c_hi[:, :, :].bitcast(F32), ALU.subtract).then_inc(chunk_lo, 1)

            def k_bias(b, t):
                key = ("k", b, t)
                e = exp_at[key]
                if e >= 2:
                    dve.wait_ge(val_dve, dve_at[exp_order[e - 2]] + 1)
                dve.wait_ge(pj_full, pj_at[key] + 1)
                nc.vector.tensor_tensor(lin[:, e % 2, :], pj[pj_at[key] % 2][:, :], kb_bc[:, :], ALU.add).then_inc(k_lin, 1)

            def wait_val(key):
                if split_at[key] >= 3:
                    dve.wait_ge(split_lo, split_at[key] - 2)

            def feature(key):
                e = exp_at[key]
                dve.wait_ge(exp_ready, e + 1)
                if key[0] == "q":
                    dve.wait_ge(q_lin, TT * key[1] + key[2] + 1)
                wait_val(key)
                nc.vector.scalar_tensor_tensor(val_tile(key), lin[:, e % 2, :], 0.0, neg[:, e % 2, :],
                                               ALU.max, ALU.add).then_inc(val_dve, 1)

            def value_lo(b, t):
                key = ("v", b, t)
                dve.wait_ge(v_hi_done, TT * b + t + 1)
                nc.vector.tensor_tensor(v[:, t, :, HW:VG], pj[pj_at[key] % 2][:, :].rearrange("p (g e) -> p g e", g=KT),
                                        v[:, t, :, 0:P].bitcast(F32), ALU.subtract).then_inc(v_lo_done, 1)

            def inverse(b):
                dve.wait_ge(ze_ready, b + 1)
                if b >= 1:
                    dve.wait_ge(att_full, KT * b)
                nc.vector.reciprocal(inv32[:, :], zb[0:NH, :]).then_inc(inv_ready, 1)

            def inverse_lo(b):
                dve.wait_ge(inv_hi_done, b + 1)
                nc.vector.tensor_tensor(inv_lo[:, :], inv32[:, :], inv_hi[:, :].bitcast(F32), ALU.subtract).then_inc(inv_split, 1)

            def attention(b, g):
                key = ("a", b, g)
                dve.wait_ge(inv_out, KT * b + g + 1)
                nc.vector.tensor_tensor(val_tile(key), att_banks(g)[1][:, :], val_tile(key), ALU.mult).then_inc(val_dve, 1)

            def key_value_state(b):
                if b >= 1:
                    dve.wait_ge(st_split, b)
                    dve.wait_ge(st_ready, KT * b)
                else:
                    dve.wait_ge(ksum_zero, 1)
                for g in range(KT):
                    dve.wait_ge(kv_full, KT * b + g + 1)
                    ps = kv_bank[g]
                    state = st32[:, g * P:(g + 1) * P]
                    nc.vector.scalar_tensor_tensor(state, vb_bc[:, g * P:(g + 1) * P], ps[:, P:P + 1], ps[:, 0:P],
                                                   ALU.mult, ALU.add).then_inc(st_step, 1)
                    k0 = KT * P + g * NH + g * GHD
                    nc.vector.tensor_scalar(st32[:, k0:k0 + GHD], mask[:, 0:P:Q32], ps[:, P:P + 1], None, ALU.mult).then_inc(st_step, 1)
                for g in range(KT):
                    state = st32[:, g * P:(g + 1) * P]
                    dve.wait_ge(st_step, 3 * KT * b + 2 * g + 1)
                    nc.vector.tensor_tensor(state, state, kv_bank[g][:, HW:VG], ALU.add).then_inc(st_step, 1)
                for g in range(KT):
                    dve.wait_ge(st_step, 3 * KT * b + 2 * KT + g + 1)
                    state = st32[:, g * P:(g + 1) * P]
                    nc.vector.tensor_tensor(state, state, mask[:, :], ALU.mult).then_inc(st_ready, 1)

            def residual(b, t):
                key = ("o", b, t)
                n = ot_at[(b, t)]
                if t == 0:
                    dve.wait_ge(ld_ga[b % 2], 16 * (b // 2 + 1))
                dve.wait_ge(pj_full, pj_at[key] + 1)
                if n >= 2:
                    dve.wait_ge(x1_ready, n - 1)
                nc.vector.tensor_tensor(ot[:, n % 2, :], pj[pj_at[key] % 2][:, :], ga_bc[:, b % 2, :], ALU.mult).then_inc(ot_ready, 1)

            def gate(i, ps, done):
                if i:
                    dve.wait_ge(g_step, 5)
                nc.vector.tensor_scalar(gs[:, :], ps, 0.0, 2.0, ALU.is_ge, ALU.mult).then_inc(g_step, 1)
                nc.vector.tensor_copy(gr[:, i, :], ps).then_inc(g_step, 1)
                dve.wait_ge(g_step, done + 1)
                nc.vector.tensor_scalar(gs[:, :], gs[:, :], -1.0, None, ALU.add).then_inc(g_step, 1)
                dve.wait_ge(g_step, done + 2)
                nc.vector.scalar_tensor_tensor(gr[:, i, :], gr[:, i, :], -1.0, gr[:, i, :], ALU.mult, ALU.max).then_inc(g_step, 1)
                dve.wait_ge(g_step, done + 4)
                nc.vector.scalar_tensor_tensor(gr[:, i, :], gr[:, i, :], G_MIN, gs[:, :], ALU.max, ALU.mult).then_inc(g_step, 1)

            def modulation(s, ps, plus):
                ps = ps[:, 0:KT * NB].rearrange("p (k b) -> p k b", b=NB)
                if plus:
                    nc.vector.tensor_scalar(modc[:, s, :, :], ps, plus, None, ALU.add).then_inc(mod_ready, 1)
                else:
                    nc.vector.tensor_copy(modc[:, s, :, :], ps).then_inc(mod_ready, 1)

            def ffn_transpose(count, which):
                if not (isinstance(count, int) and count == 0):
                    dve.wait_ge(f_lo, count)
                nc.vector.transpose(ftr[:, :, :], fraw[which][:, :, :]).then_inc(f_tr, 1)

            dve.wait_ge(const_ready, 2)
            src = ident
            for s in range(7):
                dst = had_r if s == 6 else (hada, hadb)[s % 2]
                if s >= 1:
                    dve.wait_ge(had_step, 2 * s)
                a = src[:, :].rearrange("p (n u h) -> p n u h", u=2, h=1 << s)
                o = dst[:, :].rearrange("p (n u h) -> p n u h", u=2, h=1 << s)
                for u, op in ((0, ALU.add), (1, ALU.subtract)):
                    nc.vector.tensor_tensor(o[:, :, u, :], a[:, :, 0, :], a[:, :, 1, :], op).then_inc(had_step, 1)
                src = dst
            statistics(0, xa)
            mean_variance(0)
            weight_transpose(KW, 0)
            for t in range(TT):
                normalise(0, t, xa, xa)
            dve.wait_ge(wm_used, 3)
            modulation(0, bank[5][:, :], 0.0)
            modulation(1, bank[5][:, KT * NB:], 1.0)
            for kt in range(1, KT):
                weight_transpose(KW, kt)
                weight_to_lo(KW, kt - 1)
            weight_to_lo(KW, KT - 1)
            dve.wait_ge(ld_kb, 16)
            dve.wait_ge(ld_vb, 16)
            dve.wait_ge(mask_ready, 1)
            for b in range(NB):
                if b >= 1:
                    inverse(b - 1)
                for t in range(TT):
                    k_bias(b, t)
                    if t >= 1:
                        feature(("k", b, t - 1))
                    if b == 0:
                        weight_transpose(VW, t)
                        if t >= 1:
                            weight_to_lo(VW, t - 1)
                    if b == 1 and t == 0:
                        dve.wait_ge(wmx_used, 4)
                        modulation(3, ab[:, :], 1.0)
                    if b >= 1 and t == 1:
                        inverse_lo(b - 1)
                    if b >= 1 and t >= 1:
                        butterfly(dve, 2 * b - 1, t - 1, 0)
                if b == 0:
                    weight_to_lo(VW, TT - 1)
                    dve.wait_ge(wmx_used, 1)
                    gate(0, zb[0:NB, :], 0)
                else:
                    attention(b - 1, 0)
                feature(("k", b, TT - 1))
                for t in range(TT):
                    value_lo(b, t)
                    if b == 0:
                        for kt in range(2 * t, min(2 * t + 2, KT)):
                            weight_transpose(QW, kt)
                    else:
                        if t == 0:
                            butterfly(dve, 2 * b - 1, 3, 0)
                        if t < TT - 1:
                            attention(b - 1, t + 1)
                    if t == 2:
                        chunk_transpose(2 * b)
                        if b == 0:
                            dve.wait_ge(wmx_used, 2)
                            gate(1, ab[0:NB, :], 5)
                n = b + 1
                ln_src = xa if n < NB else xh2[0]
                for t in range(TT):
                    if t >= 1:
                        feature(("q", b, t - 1))
                    if t == 0:
                        chunk_to_lo(2 * b)
                        statistics(n, ln_src)
                    if t == 1:
                        mean_variance(n)
                    if t == 2:
                        key_value_state(b)
                        for u in range(TT):
                            normalise(n, u, ln_src, ln_src)
                    if t == 2:
                        for u in range(2):
                            butterfly(dve, 2 * b, 0, u)
                    if t == 3:
                        dve.wait_ge(st_hi_done, b + 1)
                        nc.vector.tensor_tensor(st_lo[:, :], st32[:, :], st_hi[:, :].bitcast(F32), ALU.subtract).then_inc(st_split, 1)
                feature(("q", b, TT - 1))
                for u in range(2):
                    butterfly(dve, 2 * b, 1, u)
                if b == 0:
                    dve.wait_ge(wmx_used, 3)
                    modulation(2, zb[:, :], 0.0)
                if b == 1:
                    dve.wait_ge(st_g, 16)
                for t in range(TT):
                    if b == 0:
                        for kt in range(2 * t, min(2 * t + 2, KT)):
                            weight_transpose(OW, kt)
                    if b >= 1:
                        residual(b - 1, t)
                    if t == 0:
                        for s in (2, 3):
                            for u in range(2):
                                butterfly(dve, 2 * b, s, u)
                    if t == 0 and b == NB - 1:
                        dve.wait_ge(ld_f[0], 16 * KT * NQ)
                        dve.wait_ge(val_dve, dve_at[("q", b, TT - 1)] + 1)
                        ffn_transpose(0, 0)
                        inverse(b)
                    if t == 1 and b == NB - 1:
                        inverse_lo(b)
                    if t == 2:
                        chunk_transpose(2 * b + 1)
                        if b == NB - 1:
                            attention(b, 0)
                    if t == 3 and b < NB - 1:
                        chunk_to_lo(2 * b + 1)
            for g in range(1, KT):
                if g < 3:
                    add_residual(dve, NB - 2, g + 1)
                else:
                    chunk_to_lo(NCH - 1)
                attention(NB - 1, g)
            second_statistics(1)
            dve.wait_ge(f_hi, 1)
            nc.vector.tensor_tensor(f1_lo[0][:, :, :], ftr[:, :, :], f1_hi[0][:, :, :].bitcast(F32), ALU.subtract).then_inc(f_lo, 1)
            dve.wait_ge(ld_f[1], 16 * KT * NQ)
            ffn_transpose(1, 1)
            for t in range(TT):
                residual(NB - 1, t)
                for u in range(2):
                    butterfly(dve, NCH - 1, t, u)
                if t >= 1:
                    add_residual(dve, NB - 1, t - 1)
            add_residual(dve, NB - 1, TT - 1)
            second_normalise(1)

            dve.sem_inc(up_used, 1)
            dve.sem_inc(contrib, TT)
            dve.sem_inc(hid_lo, 1)

            def weight2_to_lo(g):
                dve.wait_ge(f2_hi_done, g + 1)
                nc.vector.tensor_tensor(f2_lo[:, :, :], f2raw[:, :, :], f2_hi[:, :, :].bitcast(F32), ALU.subtract).then_inc(f2_ready, 1)

            def contribution(g, b):
                last = isinstance(g, int) and g == NG - 1 and b == NB - 1
                for t in range(TT):
                    m = (g * NB + b) * TT + t
                    if last and t == 2:
                        add_contribution(dve, m - 1, b, 1)
                    dve.wait_ge(out_full, m + 1)
                    dve.wait_ge(added, m + 1)
                    nc.vector.tensor_tensor(ot[:, t % 2, :], out_ps[t][:, :], gb_bc[:, b, :], ALU.mult).then_inc(contrib, 1)
                if last:
                    add_contribution(dve, m, b, TT - 1)

            def ffn(g, par, b, more):
                n = (g * NB + b) * GB
                first = isinstance(g, int) and g == 0
                wb = 1 if first else 0
                for i in range(GB):
                    if first and b == 0 and i == 1:
                        weight2_to_lo(g)
                    dve.wait_ge(hid_lo, n + i + 1)
                    dve.wait_ge(gate_used, n + i + 2)
                    dve.wait_ge(up_full, n + i + 1)
                    nc.vector.tensor_tensor(hid32[:, :], up_ps[:, :], gate32[:, :], ALU.mult).then_inc(up_used, 1)
                    dve.wait_ge(hid_hi, n + i + 1)
                    nc.vector.tensor_tensor(hd_lo[:, i, :], hid32[:, :], hd_hi[:, i, :].bitcast(F32), ALU.subtract).then_inc(hid_lo, 1)
                    if b == 0 and i == 0 and not first:
                        weight2_to_lo(g)
                    if i == 0 and more and wb <= b < wb + 2:
                        dve.wait_ge(ld_f[b - wb], 16 * KT * NQ * (g + 2))
                        ffn_transpose(2 * g + 2 + b - wb, b - wb)
                    if i == 1 and first and b + 2 < NB:
                        second_statistics(b + 2)
                        second_normalise(b + 2)
                contribution(g, b)

            dve.wait_ge(ld_gb, 16)
            for b in range(NB):
                ffn(0, 0, b, True)
            with dve.Fori(1, NG - 1, 2) as g:
                for par in (1, 0):
                    for b in range(NB):
                        ffn(g + (1 - par), par, b, True)
            for b in range(NB):
                ffn(NG - 1, 1, b, False)

        @block.gpsimd
        def _(pool):
            nc.gpsimd.memset(ident[:, :], 0.0).then_inc(pool_step, 1)
            nc.gpsimd.memset(mask[:, :], 1.0).then_inc(pool_step, 1)
            nc.gpsimd.memset(mhalf[:, :], -0.5).then_inc(const_ready, 1)
            pool.wait_ge(pool_step, 2)
            nc.gpsimd.affine_select(out=ident[:, :], in_=ident[:, :], compare_op=ALU.not_equal, fill=1.0,
                                    base=0, pattern=[[-1, P]], channel_multiplier=1).then_inc(const_ready, 1)
            heads = mask[:, :].rearrange("p (a j) -> p a j", j=Q32)
            nc.gpsimd.affine_select(out=heads, in_=heads, compare_op=ALU.is_ge, fill=0.0,
                                    base=0, pattern=[[-Q32, NQ], [0, Q32]], channel_multiplier=1).then_inc(pool_step, 1)
            pool.wait_ge(pool_step, 3)
            nc.gpsimd.affine_select(out=heads, in_=heads, compare_op=ALU.is_ge, fill=0.0,
                                    base=Q32 - 1, pattern=[[Q32, NQ], [0, Q32]], channel_multiplier=-1).then_inc(mask_ready, 1)

            nc.gpsimd.memset(spread32[:, :, :], 1.0).then_inc(spread_step, 1)
            for n, (base, sign) in enumerate(((0, 1), (Q32 - 1, -1))):
                pool.wait_ge(spread_step, n + 1)
                nc.gpsimd.affine_select(out=spread32[:, :, :], in_=spread32[:, :, :], compare_op=ALU.is_ge, fill=0.0,
                                        base=base, pattern=[[sign * P, KT], [sign, P]], channel_multiplier=-sign * Q32).then_inc(spread_step, 1)
            pool.wait_ge(spread_step, 3)
            nc.gpsimd.tensor_copy(spread_r[:, :, :], spread32[:, :, :]).then_inc(spread_ready, 1)
            nc.gpsimd.memset(st32[:, KT * P:], 0.0).then_inc(ksum_zero, 1)

            def ffn_weight_lo(count, which, par):
                pool.wait_ge(f_hi, count)
                nc.gpsimd.tensor_tensor((f1_lo, f3_lo)[which][par][:, :, :], ftr[:, :, :],
                                        (f1_hi, f3_hi)[which][par][:, :, :].bitcast(F32), ALU.subtract).then_inc(f_lo, 1)

            def rstd_of(n):
                pool.wait_ge(stat_step, 9 * (n + 1))
                if n == 0:
                    pool.wait_ge(const_ready, 2)
                else:
                    pool.wait_ge(xhat_ready, TT * n)
                nc.gpsimd.tensor_tensor(rstd[:, :], ve[:, :], mhalf[:, :], ALU.pow).then_inc(rstd_ready, 1)

            def to_lo(key):
                pool.wait_ge(split_hi, split_at[key] + 1)
                hi, lo = split_tile(key)
                nc.gpsimd.tensor_tensor(lo, val_tile(key), hi.bitcast(F32), ALU.subtract).then_inc(split_lo, 1)

            def weight_to_lo(i, kt):
                pool.wait_ge(w_hi_done, KT * i + kt + 1)
                nc.gpsimd.tensor_tensor(w_lo[i][:, kt, :], wtr[:, kt, :], w_hi[i][:, kt, :].bitcast(F32), ALU.subtract).then_inc(w_ready, 1)

            def output_bias(b):
                pool.wait_ge(ld_ga[b % 2], 16 * (b // 2 + 1))
                if b >= 1:
                    pool.wait_ge(xob_ready, TT * b)
                nc.gpsimd.tensor_tensor(gaob[:, :], ga_bc[:, b % 2, :], ob_bc[:, :], ALU.mult).then_inc(gaob_ready, 1)
                pool.wait_ge(gaob_ready, b + 1)

            def add_bias(b, t):
                pool.wait_ge(ld_xt[t], 16 * (b + 1))
                nc.gpsimd.tensor_tensor(xt[:, t, :], xt[:, t, :], gaob[:, :], ALU.add).then_inc(xob_ready, 1)

            rstd_of(0)
            for kt in range(KT):
                to_lo(("h", 0, kt))
            pool.wait_ge(wm_used, 3)
            nc.gpsimd.memset(v[:, :, :, P:HW].bitcast(F32), 1.0).then_inc(v_ones, 1)
            pool.wait_ge(ld_ob, 16)
            for b in range(NB):
                for t in range(TT):
                    if t >= 1:
                        if b >= 1:
                            butterfly(pool, 2 * b - 1, t - 1, 1)
                        to_lo(("k", b, t - 1))
                for t in range(TT):
                    if b >= 1:
                        to_lo(("a", b - 1, t))
                    if t == 0:
                        to_lo(("k", b, TT - 1))
                    if t == 0 and b >= 1:
                        butterfly(pool, 2 * b - 1, 3, 1)
                    if b == 0:
                        for kt in range(2 * t, min(2 * t + 2, KT)):
                            weight_to_lo(QW, kt)
                for t in range(TT):
                    if t == 1:
                        rstd_of(b + 1)
                    if t >= 1:
                        to_lo(("q", b, t - 1))
                to_lo(("q", b, TT - 1))
                if b >= 1:
                    output_bias(b - 1)
                for t in range(TT):
                    for kt in transposed_after(b, t):
                        to_lo(("h", b + 1, kt) if b + 1 < NB else ("h2", 0, kt))
                    if b == 0 and t >= 2:
                        for kt in range(2 * t - 4, 2 * t - 2):
                            weight_to_lo(OW, kt)
                    if b >= 1:
                        add_bias(b - 1, t)
                        if b < NB - 1 or t < 2:
                            add_residual(pool, b - 1, t)
            for g in range(KT):
                to_lo(("a", NB - 1, g))
            output_bias(NB - 1)
            for t in range(TT):
                add_bias(NB - 1, t)
                if t == 1:
                    for kt in range(2, KT):
                        to_lo(("h2", 0, kt))
                    ffn_weight_lo(2, 1, 0)
            rstd_of(NB + 1)

            def ffn(g, par, b, more):
                first = isinstance(g, int) and g == 0
                wb = 1 if first else 0
                if first:
                    pool.wait_ge(ld_x1[b], 16)
                if first and b + 1 < NB:
                    for kt in range(KT):
                        to_lo(("h2", b + 1, kt))
                if more and wb <= b < wb + 2:
                    ffn_weight_lo(2 * g + 3 + b - wb, b - wb, 1 - par)
                if first:
                    if b + 2 < NB:
                        rstd_of(NB + b + 2)
                last = isinstance(g, int) and g == NG - 1 and b == NB - 1
                for t in range(TT):
                    if not (last and t % 2):
                        add_contribution(pool, (g * NB + b) * TT + t, b, t)

            pool.sem_inc(added, 2)
            for b in range(NB):
                ffn(0, 0, b, True)
            with pool.Fori(1, NG - 1, 2) as g:
                for par in (1, 0):
                    for b in range(NB):
                        ffn(g + (1 - par), par, b, True)
            for b in range(NB):
                ffn(NG - 1, 1, b, False)


_INS = ['L0_attn_hidden_states', 'L0_attn_q_w', 'L0_attn_q_b', 'L0_attn_k_w', 'L0_attn_k_b', 'L0_attn_v_w', 'L0_attn_v_b',
        'L0_attn_o_w', 'L0_attn_o_b', 'L0_ffn_W1', 'L0_ffn_W2', 'L0_ffn_W3', 'L0_c', 'L0_wmod']


def kernel(**inputs):
    import numpy as _np
    import concourse.bacc as _bacc
    from concourse import mybir as _mybir
    from concourse.bass_utils import run_bass_kernel_spmd as _run

    nc = _bacc.Bacc("TRN2", target_bir_lowering=False, num_devices=1, dynamic_dma_scratch_size=1024)
    arrays, args = {}, []
    for name in _INS:
        a = _np.ascontiguousarray(inputs[name])
        arrays[f"in_{name}_dram"] = a
        args.append(nc.dram_tensor(f"in_{name}_dram", a.shape, _mybir.dt.from_np(a.dtype), kind="ExternalInput").ap())
    o = nc.dram_tensor("out_dram", arrays["in_L0_attn_hidden_states_dram"].shape, _mybir.dt.float32, kind="ExternalOutput").ap()
    build(nc, *args, o)
    r = _run(nc, [arrays], core_ids=[0])
    return r.results[0]["out_dram"]
```
